# Optimizing a Trainium2 kernel written in Bass

```python
import numpy as np
import jax
import jax.numpy as jnp

def _softmax(x, axis=-1):
    return jax.nn.softmax(x, axis=axis)

def _gelu(x):
    return jax.nn.gelu(x, approximate=True)

def _silu(x):
    return jax.nn.silu(x)

def _sigmoid(x):
    return jax.nn.sigmoid(x)

def _layernorm(x, axis=-1, eps=1e-05):
    m = jnp.mean(x, axis=axis, keepdims=True)
    v = jnp.var(x, axis=axis, keepdims=True)
    return (x - m) / jnp.sqrt(v + eps)

def _scatter_add(tgt, idx, src, axis=0):
    return tgt.at[idx].add(src)

def _segment_sum(src, seg, n):
    return jax.ops.segment_sum(src, seg, n)
kernel_name = 'mk_flamingo_gated_d1_seqx_r4_f274e8'

def setup_inputs(seed: int=0):
    np.random.seed(seed)
    _w = jnp.asarray

    def _rec_inputs():
        import jax
        import jax.numpy as jnp
        _rk = jax.random.key(seed)
        x = -0.0002928 + 1 * jax.random.normal(jax.random.fold_in(_rk, 1), (4, 512, 256), jnp.float32)
        _lenS = 512 - jax.random.randint(jax.random.fold_in(_rk, 7), (4,), 0, max(1, 512 // 4) + 1, jnp.int32)
        _lenS2 = 512 - jax.random.randint(jax.random.fold_in(_rk, 8), (4,), 0, max(1, 512 // 4) + 1, jnp.int32)
        _ctx_1024P = jax.random.normal(jax.random.fold_in(_rk, 11), (4, 16, 256), jnp.float32)
        _ctx_1024c = jax.random.dirichlet(jax.random.fold_in(_rk, 511), 0.3 * jnp.ones((16,), jnp.float32), (4, 512))
        _ctx_1024t = jnp.einsum('bsk,bkd->bsd', _ctx_1024c, _ctx_1024P)
        _ctx_1024t = _ctx_1024t * jax.lax.rsqrt(jnp.mean(jnp.square(_ctx_1024t)) + 1e-12) * 0.953939
        ctx_1024 = -1.39393e-06 + 0.999914 * (_ctx_1024t + 0.3 * jax.random.normal(jax.random.fold_in(_rk, 611), (4, 512, 256), jnp.float32))
        _g = jax.random.normal(jax.random.fold_in(_rk, 9001), (2, 1), jnp.float32)
        _g = jnp.sign(_g) * jnp.maximum(jnp.abs(_g), 1.0) + (_g == 0) * 1.0
        g_xattn = _g[0]
        g_ffn = _g[1]
        return (x, ctx_1024, g_xattn, g_ffn)
    x, ctx_1024, g_xattn, g_ffn = _rec_inputs()

    def _L0_xattn_setup():
        import jax, jax.numpy as jnp
        import numpy as np
        B, S, H, NH = (2, 512, 256, 4)
        DH = H // NH
        EPS_BACKEND = 1e-06
        EPS_LN = 1e-06

        def _mlstm_parallel_stabilized(q, k, v, igate_preact, fgate_preact):
            b, nh, s, dh = q.shape
            log_fg = jax.nn.log_sigmoid(fgate_preact)
            cs = jnp.concatenate([jnp.zeros((b, nh, 1), q.dtype), jnp.cumsum(log_fg[..., 0], axis=2)], axis=2)
            fg_matrix = cs[:, :, :, None] - cs[:, :, None, :]
            fg_matrix = fg_matrix[:, :, 1:, 1:]
            causal = jnp.tril(jnp.ones((s, s), dtype=bool))
            log_fg_matrix = jnp.where(causal, fg_matrix, -jnp.inf)
            log_D = log_fg_matrix + jnp.swapaxes(igate_preact, -2, -1)
            max_log_D = jnp.max(log_D, axis=-1, keepdims=True)
            D = jnp.exp(log_D - max_log_D)
            qk = jnp.einsum('bhsd,bhtd->bhst', q, k) / jnp.sqrt(jnp.asarray(dh, q.dtype))
            C = qk * D
            normalizer = jnp.maximum(jnp.abs(jnp.sum(C, axis=-1, keepdims=True)), jnp.exp(-max_log_D))
            C_norm = C / (normalizer + EPS_BACKEND)
            return jnp.einsum('bhst,bhtd->bhsd', C_norm, v)

        def _multihead_layernorm(x, scale):
            mean = jnp.mean(x, axis=-1, keepdims=True)
            var = jnp.var(x, axis=-1, keepdims=True)
            xn = (x - mean) * jax.lax.rsqrt(var + EPS_LN)
            return xn * scale.reshape(NH, 1, DH)
        key = jax.random.key(seed)
        kq, kk, kv, kib = jax.random.split(key, 4)
        q = jax.random.normal(kq, (B, S, H), dtype=jnp.float32)
        k = jax.random.normal(kk, (B, S, H), dtype=jnp.float32)
        v = jax.random.normal(kv, (B, S, H), dtype=jnp.float32)
        igate_kernel = jnp.zeros((3 * H, NH), dtype=jnp.float32)
        igate_bias = 0.1 * jax.random.normal(kib, (NH,), dtype=jnp.float32)
        fgate_kernel = jnp.zeros((3 * H, NH), dtype=jnp.float32)
        fgate_bias = jnp.linspace(3.0, 6.0, NH, dtype=jnp.float32)
        outnorm_scale = jnp.ones((H,), dtype=jnp.float32)
        return {'q': q, 'k': k, 'v': v, 'igate_kernel': igate_kernel, 'igate_bias': igate_bias, 'fgate_kernel': fgate_kernel, 'fgate_bias': fgate_bias, 'outnorm_scale': outnorm_scale}
    _L0_xattn_all = _L0_xattn_setup()
    _L0_xattn_in = {k: v for k, v in _L0_xattn_all.items() if k in ('igate_kernel', 'igate_bias', 'fgate_kernel', 'fgate_bias', 'outnorm_scale')}
    del _L0_xattn_all

    def _L0_ffn_setup():
        import jax, jax.numpy as jnp
        import numpy as np
        B, S, H = (2, 512, 256)
        E_DYN, E_FIX = (8, 1)
        I_DYN, I_FIX = (128, 512)
        TOP_K = 4
        TOP_P = 0.75
        JITTER_EPS = 0.1
        CAPACITY_FACTOR = 1.25
        MIN_CAPACITY = 4

        def _sparse_mixer(scores):
            T = scores.shape[0]
            rows = jnp.arange(T)
            masked_scores = scores
            mults, sels = ([], [])
            for _ in range(TOP_K):
                thr = jnp.max(masked_scores, axis=-1, keepdims=True)
                sel = jnp.argmax(masked_scores, axis=-1)
                factor = jnp.maximum(jnp.abs(scores), jnp.abs(thr))
                jmask = (thr - scores) / factor > 2.0 * JITTER_EPS
                gates = jax.nn.softmax(jnp.where(jmask, -jnp.inf, masked_scores), axis=-1)
                mult = jnp.take_along_axis(gates, sel[:, None], axis=-1)[:, 0]
                masked_scores = masked_scores.at[rows, sel].set(-jnp.inf)
                mults.append(mult)
                sels.append(sel)
            return (jnp.stack(mults, axis=-1), jnp.stack(sels, axis=-1))
        key = jax.random.key(seed)
        k = jax.random.split(key, 8)
        sc = 0.02
        return {'hidden_states': jax.random.normal(k[0], (B, S, H), jnp.float32), 'gate_w': jax.random.normal(k[1], (E_DYN + E_FIX, H), jnp.float32) * sc, 'dyn_gate_w': jax.random.normal(k[2], (E_DYN, I_DYN, H), jnp.float32) * sc, 'dyn_up_w': jax.random.normal(k[3], (E_DYN, I_DYN, H), jnp.float32) * sc, 'dyn_down_w': jax.random.normal(k[4], (E_DYN, H, I_DYN), jnp.float32) * sc, 'sh_gate_w': jax.random.normal(k[5], (E_FIX, I_FIX, H), jnp.float32) * sc, 'sh_up_w': jax.random.normal(k[6], (E_FIX, I_FIX, H), jnp.float32) * sc, 'sh_down_w': jax.random.normal(k[7], (E_FIX, H, I_FIX), jnp.float32) * sc}
    _L0_ffn_all = _L0_ffn_setup()
    _L0_ffn_in = {k: v for k, v in _L0_ffn_all.items() if k in ('gate_w', 'dyn_gate_w', 'dyn_up_w', 'dyn_down_w', 'sh_gate_w', 'sh_up_w', 'sh_down_w')}
    del _L0_ffn_all
    return {'x': x, 'ctx_1024': ctx_1024, 'g_xattn': g_xattn, 'g_ffn': g_ffn, 'L0_xattn_igate_kernel': _L0_xattn_in['igate_kernel'], 'L0_xattn_igate_bias': _L0_xattn_in['igate_bias'], 'L0_xattn_fgate_kernel': _L0_xattn_in['fgate_kernel'], 'L0_xattn_fgate_bias': _L0_xattn_in['fgate_bias'], 'L0_xattn_outnorm_scale': _L0_xattn_in['outnorm_scale'], 'L0_ffn_gate_w': _L0_ffn_in['gate_w'], 'L0_ffn_dyn_gate_w': _L0_ffn_in['dyn_gate_w'], 'L0_ffn_dyn_up_w': _L0_ffn_in['dyn_up_w'], 'L0_ffn_dyn_down_w': _L0_ffn_in['dyn_down_w'], 'L0_ffn_sh_gate_w': _L0_ffn_in['sh_gate_w'], 'L0_ffn_sh_up_w': _L0_ffn_in['sh_up_w'], 'L0_ffn_sh_down_w': _L0_ffn_in['sh_down_w']}

def reference(x, ctx_1024, g_xattn, g_ffn, L0_xattn_igate_kernel, L0_xattn_igate_bias, L0_xattn_fgate_kernel, L0_xattn_fgate_bias, L0_xattn_outnorm_scale, L0_ffn_gate_w, L0_ffn_dyn_gate_w, L0_ffn_dyn_up_w, L0_ffn_dyn_down_w, L0_ffn_sh_gate_w, L0_ffn_sh_up_w, L0_ffn_sh_down_w):
    import jax
    import jax.numpy as jnp

    def _L0_xattn_ref(q, k, v, igate_kernel, igate_bias, fgate_kernel, fgate_bias, outnorm_scale):
        import jax, jax.numpy as jnp
        import numpy as np
        B, S, H, NH = (2, 512, 256, 4)
        DH = H // NH
        EPS_BACKEND = 1e-06
        EPS_LN = 1e-06

        def _mlstm_parallel_stabilized(q, k, v, igate_preact, fgate_preact):
            b, nh, s, dh = q.shape
            log_fg = jax.nn.log_sigmoid(fgate_preact)
            cs = jnp.concatenate([jnp.zeros((b, nh, 1), q.dtype), jnp.cumsum(log_fg[..., 0], axis=2)], axis=2)
            fg_matrix = cs[:, :, :, None] - cs[:, :, None, :]
            fg_matrix = fg_matrix[:, :, 1:, 1:]
            causal = jnp.tril(jnp.ones((s, s), dtype=bool))
            log_fg_matrix = jnp.where(causal, fg_matrix, -jnp.inf)
            log_D = log_fg_matrix + jnp.swapaxes(igate_preact, -2, -1)
            max_log_D = jnp.max(log_D, axis=-1, keepdims=True)
            D = jnp.exp(log_D - max_log_D)
            qk = jnp.einsum('bhsd,bhtd->bhst', q, k) / jnp.sqrt(jnp.asarray(dh, q.dtype))
            C = qk * D
            normalizer = jnp.maximum(jnp.abs(jnp.sum(C, axis=-1, keepdims=True)), jnp.exp(-max_log_D))
            C_norm = C / (normalizer + EPS_BACKEND)
            return jnp.einsum('bhst,bhtd->bhsd', C_norm, v)

        def _multihead_layernorm(x, scale):
            mean = jnp.mean(x, axis=-1, keepdims=True)
            var = jnp.var(x, axis=-1, keepdims=True)
            xn = (x - mean) * jax.lax.rsqrt(var + EPS_LN)
            return xn * scale.reshape(NH, 1, DH)
        b, s, h = q.shape
        gate_in = jnp.concatenate([q, k, v], axis=-1)
        ig = gate_in @ igate_kernel + igate_bias
        fg = gate_in @ fgate_kernel + fgate_bias
        ig = jnp.transpose(ig, (0, 2, 1))[..., None]
        fg = jnp.transpose(fg, (0, 2, 1))[..., None]
        qh = jnp.transpose(q.reshape(b, s, NH, DH), (0, 2, 1, 3))
        kh = jnp.transpose(k.reshape(b, s, NH, DH), (0, 2, 1, 3))
        vh = jnp.transpose(v.reshape(b, s, NH, DH), (0, 2, 1, 3))
        hs = _mlstm_parallel_stabilized(qh, kh, vh, ig, fg)
        hn = _multihead_layernorm(hs, outnorm_scale)
        return jnp.transpose(hn, (0, 2, 1, 3)).reshape(b, s, h)

    def _L0_ffn_ref(hidden_states, gate_w, dyn_gate_w, dyn_up_w, dyn_down_w, sh_gate_w, sh_up_w, sh_down_w):
        import jax, jax.numpy as jnp
        import numpy as np
        B, S, H = (2, 512, 256)
        E_DYN, E_FIX = (8, 1)
        I_DYN, I_FIX = (128, 512)
        TOP_K = 4
        TOP_P = 0.75
        JITTER_EPS = 0.1
        CAPACITY_FACTOR = 1.25
        MIN_CAPACITY = 4

        def _sparse_mixer(scores):
            T = scores.shape[0]
            rows = jnp.arange(T)
            masked_scores = scores
            mults, sels = ([], [])
            for _ in range(TOP_K):
                thr = jnp.max(masked_scores, axis=-1, keepdims=True)
                sel = jnp.argmax(masked_scores, axis=-1)
                factor = jnp.maximum(jnp.abs(scores), jnp.abs(thr))
                jmask = (thr - scores) / factor > 2.0 * JITTER_EPS
                gates = jax.nn.softmax(jnp.where(jmask, -jnp.inf, masked_scores), axis=-1)
                mult = jnp.take_along_axis(gates, sel[:, None], axis=-1)[:, 0]
                masked_scores = masked_scores.at[rows, sel].set(-jnp.inf)
                mults.append(mult)
                sels.append(sel)
            return (jnp.stack(mults, axis=-1), jnp.stack(sels, axis=-1))
        Bv, Sv, Hv = hidden_states.shape
        T = Bv * Sv
        x = hidden_states.reshape(T, Hv)
        full_logits = x @ gate_w.T
        dyn_logits = full_logits[:, :E_DYN]
        probs = jax.nn.softmax(dyn_logits, axis=-1)
        sorted_p = jnp.sort(probs, axis=-1)[:, ::-1]
        csum = jnp.cumsum(sorted_p, axis=-1)
        dyn_k = jnp.minimum(jnp.sum(csum < TOP_P, axis=-1) + 1, TOP_K)
        mult, sel = _sparse_mixer(dyn_logits)
        slot_valid = jnp.arange(TOP_K)[None, :] < dyn_k[:, None]
        mult = jnp.where(slot_valid, mult, 0.0)
        rows = jnp.arange(T)
        rw = jnp.zeros((T, E_DYN), x.dtype).at[rows[:, None], sel].add(mult)
        rw = rw / jnp.sum(rw, axis=-1, keepdims=True)
        mask_dyn = (rw > 0).astype(jnp.int32)
        cap = max(int(np.ceil(T / E_DYN * CAPACITY_FACTOR)), MIN_CAPACITY)
        mask_dyn = mask_dyn * (jnp.cumsum(mask_dyn, axis=0) <= cap)
        expert_mask = jnp.concatenate([mask_dyn, jnp.ones((T, E_FIX), jnp.int32)], axis=-1)
        maskf = expert_mask.astype(x.dtype)
        gw = jax.nn.softmax(jnp.where(expert_mask == 0, -jnp.inf, full_logits), axis=-1)
        gd = rw * jnp.sum(gw[:, :E_DYN], axis=-1, keepdims=True)
        global_w = jnp.concatenate([gd, gw[:, E_DYN:]], axis=-1) * maskf
        g = jnp.einsum('th,eih->tei', x, dyn_gate_w)
        u = jnp.einsum('th,eih->tei', x, dyn_up_w)
        y_dyn = jnp.einsum('tei,ehi->teh', jax.nn.silu(g) * u, dyn_down_w)
        out = jnp.einsum('te,teh->th', global_w[:, :E_DYN], y_dyn)
        gs = jnp.einsum('th,fih->tfi', x, sh_gate_w)
        us = jnp.einsum('th,fih->tfi', x, sh_up_w)
        y_sh = jnp.einsum('tfi,fhi->tfh', jax.nn.silu(gs) * us, sh_down_w)
        out = out + jnp.einsum('tf,tfh->th', global_w[:, E_DYN:], y_sh)
        return out.reshape(Bv, Sv, Hv)
    x = x + jnp.tanh(g_xattn[0]) * _L0_xattn_ref(_layernorm(x, axis=-1), ctx_1024, ctx_1024, L0_xattn_igate_kernel, L0_xattn_igate_bias, L0_xattn_fgate_kernel, L0_xattn_fgate_bias, L0_xattn_outnorm_scale)
    x = x + jnp.tanh(g_ffn[0]) * _L0_ffn_ref(_layernorm(x, axis=-1), L0_ffn_gate_w, L0_ffn_dyn_gate_w, L0_ffn_dyn_up_w, L0_ffn_dyn_down_w, L0_ffn_sh_gate_w, L0_ffn_sh_up_w, L0_ffn_sh_down_w)
    return x

_drawn_inputs = setup_inputs


def setup_inputs(seed=0):
    import zlib

    import numpy as np

    out = dict(_drawn_inputs(seed))
    spreads = {'L0_xattn_igate_kernel': (0.0, 0.1),
     'L0_xattn_fgate_kernel': (0.0, 0.1),
     'L0_xattn_outnorm_scale': (1.0, 0.2)}
    factors = {'L0_xattn_igate_bias': 64.0,
     'L0_ffn_gate_w': 8.0,
     'L0_ffn_dyn_gate_w': 8.0,
     'L0_ffn_dyn_up_w': 8.0,
     'L0_ffn_dyn_down_w': 8.0,
     'L0_ffn_sh_gate_w': 4.271,
     'L0_ffn_sh_up_w': 4.218,
     'L0_ffn_sh_down_w': 4.232}
    for name, (base, spread) in spreads.items():
        noise = np.random.default_rng([zlib.crc32(name.encode()), seed]).standard_normal(out[name].shape)
        drawn = base * np.exp(spread * noise) if base else spread * noise
        out[name] = jnp.asarray(drawn.astype(out[name].dtype))
    for name, factor in factors.items():
        out[name] = (out[name] * factor).astype(out[name].dtype)
    return out
```

```python
import concourse.bass as bass
from concourse import mybir
from contextlib import ExitStack


def gated_mlstm_moe_block(nc, A, out):
    fp32, f32r, bf16, i32 = (mybir.dt.float32, mybir.dt.float32r, mybir.dt.bfloat16, mybir.dt.int32)
    ALU = mybir.AluOpType
    ACT = mybir.ActivationFunctionType
    AX = mybir.AxisListType

    P = 128
    B, SEQ, HD = 4, 512, 256
    NH, DH = 4, 64
    DA = DH + 1
    NC = SEQ // P
    NT = B * NC
    T = B * SEQ
    KH = HD // P
    E, EI = 8, 128
    SI = 512
    IC = SI // P
    CAP = 320
    EJ = 3
    EROWS = [128, 128, 64]
    NV = 5
    XR, YR = 3, 2
    EMPTY = 4096.0
    QSCALE = float(DH) ** -0.5
    NEG = -1.0e30

    ctx = ExitStack()
    with ctx:
        def sb(name, shape, dt=fp32):
            return ctx.enter_context(nc.sbuf_tensor(name, shape, dt))

        def sem(name):
            return ctx.enter_context(nc.semaphore(name))

        def bank(name):
            return ctx.enter_context(nc.psum_tensor(name, [P, 512], fp32))

        def order(h):
            return (h % 2) * 2 + h // 2

        def bc(ap, axis, n):
            ap = ap.unsqueeze(axis)
            shape = list(ap.shape)
            shape[axis] = n
            return ap.to_broadcast(shape)

        xs = sb("xs", [P, NT, HD])
        v_aug = sb("v_aug", [P, NT, NH, DA])
        kT = sb("kT", [P, KH, T])
        qT = sb("qT", [P, KH, T])
        x2T = sb("x2T", [P, KH, T])
        normed = sb("normed", [P, 2, NC, HD])
        wgu_sh = sb("wgu_sh", [P, 2, KH, SI])
        wd_sh = sb("wd_sh", [P, IC, HD])
        wgu_dyn = sb("wgu_dyn", [P, 2, E, KH, EI])
        wd_dyn = sb("wd_dyn", [P, E, HD])
        w_route = sb("w_route", [P, KH, E + 1])
        w_gates = sb("w_gates", [P, 3 * KH, 2 * NH])
        b_gates = sb("b_gates", [P, 2 * NH])
        g_pair = sb("g_pair", [P, 2])
        tanh_g = sb("tanh_g", [P, 2])
        half_gf = sb("half_gf", [P, 1])
        out_scale = sb("out_scale", [P, HD])
        ident = sb("ident", [P, P])
        ident_b = sb("ident_b", [P, P], bf16)
        tri_b = sb("tri_b", [P, P], bf16)
        ones_b = sb("ones_b", [P, P], bf16)
        causal_b = sb("causal_b", [P, NH, P], bf16)
        iota1 = sb("iota1", [P, P], bf16)
        tri_e = sb("tri_e", [P, E, E])
        row_of = sb("row_of", [P, NH, 32])
        head_of = sb("head_of", [P, NH])
        rep_of = sb("rep_of", [P, 8])
        is_a = sb("is_a", [P, 1])
        is_m = sb("is_m", [P, 1])
        is_hi = sb("is_hi", [P, 1])
        is_lo = sb("is_lo", [P, 1])
        parity = sb("parity", [P, 2])
        par_sel = sb("par_sel", [P, P])
        pair_row = sb("pair_row", [P, B, 2])
        m_half = sb("m_half", [P, 16])
        act_sh = sb("act_sh", [P, 2, IC, SEQ])
        fmin, fabs, fexp, u_row, w_row, n_row, av, av_lo = (act_sh[:, i // IC, i % IC, :] for i in range(2 * IC))
        ones_row, av_hi = fexp, fabs.bitcast(f32r)
        a_row = sb("a_row", [P, SEQ])
        m_row = sb("m_row", [P, SEQ])
        negm = sb("negm", [P, SEQ])
        dec_row = sb("dec_row", [P, NC])
        dec_sel = sb("dec_sel", [P, B, 2, NC])
        dl = sb("dl", [P, SEQ], f32r)
        dr = sb("dr", [P, NC, NH, P], f32r)
        u_t = sb("u_t", [P, NC, B, NH])
        w_t = sb("w_t", [P, NC, B, NH])
        n_t = sb("n_t", [P, NC, B, NH])
        dec_t = sb("dec_t", [P, B, 2, NC])
        dexp = sb("dexp", [P, 2, NH * P])
        cmat = sb("cmat", [P, 2, NH * P])
        gate_tok = dexp[:, :, :].rearrange("p q (c r) -> p q c r", c=NC)
        cs, mld = cmat[:, 0, :], cmat[:, 1, :]
        uv = sb("uv", [P, 2, NH, DA])
        state = sb("state", [P, 2, 2, DA])
        far = sb("far", [P, 2, NH, DA])
        heads = sb("heads", [P, 2, NC, NH, DA])
        st = sb("st", [P, 16, 6])
        st_s = sb("st_s", [P, 16])
        st_d = sb("st_d", [P, 16])
        st_v = sb("st_v", [P, 16])
        st_d2 = sb("st_d2", [P, 16])
        mean = sb("mean", [P, 16])
        var_eps = sb("var_eps", [P, 16])
        rstd = sb("rstd", [P, 16])
        den = sb("den", [P, 16])
        rden = sb("rden", [P, 16])
        rden2 = sb("rden2", [P, 16])
        hscale = sb("hscale", [P, 16])
        logit = sb("logit", [P, 2, NC, E + 1])
        lmax = sb("lmax", [P, NC])
        labs = sb("labs", [P, NC, E])
        lsh = sb("lsh", [P, NC, E])
        ex = sb("ex", [P, NC, E])
        tot75 = sb("tot75", [P, NC])
        pd = sb("pd", [P, NC * E, E])
        pe_ = sb("pe_", [P, NC * E, E])
        pb = sb("pb", [P, NC * E, E])
        pc = sb("pc", [P, NC * E, E])
        pm = sb("pm", [P, NC * E, E])
        rank = sb("rank", [P, NC, E])
        before = sb("before", [P, NC, E])
        valid = sb("valid", [P, NC, E])
        valid_b = sb("valid_b", [P, NC, E], bf16)
        mden = sb("mden", [P, NC, E])
        rw = sb("rw", [P, NC, E])
        rsum = sb("rsum", [P, NC])
        carry = sb("carry", [P, E])
        carry_b = sb("carry_b", [P, E], bf16)
        msum = sb("msum", [P, E])
        pos = sb("pos", [P, NC, E])
        keep9 = sb("keep9", [P, NC, E + 1])
        l9 = sb("l9", [P, NC, E + 1])
        t9 = sb("t9", [P, NC, E + 1])
        e9 = sb("e9", [P, NC, E + 1])
        sdyn = sb("sdyn", [P, NC])
        w_shared = sb("w_shared", [P, NT])
        tile_j = sb("tile_j", [P, NC * E])
        pk = sb("pk", [P, NC * E])
        onehot = sb("onehot", [P, NC * E, P], bf16)
        val = sb("val", [P, NT * E, NV], bf16)
        res = sb("res", [P, NC * E])
        val_j = sb("val_j", [P, NC * E, EJ, NV], bf16)
        slots = sb("slots", [P, E, EJ, NV])
        slot_w = sb("slot_w", [P, E * EJ])
        slot_id = sb("slot_id", [P, E * EJ])
        slot_s = sb("slot_s", [P, E * EJ], i32)
        slot_g = sb("slot_g", [P, E * EJ], i32)
        sig = sb("sig", [P, 2, SEQ])
        k_flat = kT[:, :, :].rearrange("p k t -> p (k t)")
        q_flat = qT[:, :, :].rearrange("p k t -> p (k t)")
        n_xg, n_ys = XR * EJ * HD, YR * EJ * HD
        xg = k_flat[:, 0:n_xg].rearrange("p (r j h) -> p r j h", r=XR, j=EJ)
        xgT = k_flat[:, n_xg:n_xg + 2 * KH * CAP].rearrange("p (r k s) -> p r k s", r=2, k=KH)
        ys = q_flat[:, 0:n_ys].rearrange("p (r j h) -> p r j h", r=YR, j=EJ)
        act_d = q_flat[:, n_ys:n_ys + 2 * CAP].rearrange("p (r s) -> p r s", r=2)

        s0_ps, s1_ps, d_ps, h_ps, t_ps, g_ps, u_ps, y_ps = (
            bank(s) for s in ("s0_ps", "s1_ps", "d_ps", "h_ps", "t_ps", "g_ps", "u_ps", "y_ps"))
        qk_ps = [s_[:, 0:2 * P] for s_ in (s0_ps, s1_ps)]
        far_ps = [s_[:, 2 * P:2 * P + 2 * DA].rearrange("p (i d) -> p i d", i=2) for s_ in (s0_ps, s1_ps)]
        kv_ps = h_ps[:, NH * DA:NH * DA + 2 * DA].rearrange("p (a d) -> p a d", a=2)
        near_ps = h_ps[:, 0:NH * DA].rearrange("p (h d) -> p h d", h=NH)
        route_ps = t_ps[:, 0:NC * (E + 1)].rearrange("p (c e) -> p c e", c=NC)
        csum_ps = t_ps[:, 64:64 + NC * E].rearrange("p (c e) -> p c e", c=NC)
        slots_ps = t_ps[:, 128:128 + E * EJ * NV]

        x2_dram = nc.dram_tensor("x2_rows", (T, HD), fp32, kind="Internal").ap()
        x_v = A["x"].rearrange("(b c p) h -> b p c h", c=NC, p=P)
        v_v = A["ctx"].rearrange("(n p) (h d) -> n p h d", p=P, h=NH)
        kT_v = A["ctxT"].rearrange("(k p) (b s) -> b p k s", p=P, s=SEQ)
        x2_v = x2_dram.rearrange("(b c p) h -> b p c h", c=NC, p=P)
        out_v = out.rearrange("b (c p) h -> b p c h", p=P)
        out_rows = out.rearrange("b s h -> (b s) h")

        x_in = [sem(f"x_in{b}") for b in range(B)]
        k_in = sem("k_in")
        v_in = sem("v_in")
        small_in = sem("small_in")
        w_sh_in = sem("w_sh_in")
        w_dyn_in = sem("w_dyn_in")
        pool_step, dve_step, act_step = sem("pool_step"), sem("dve_step"), sem("act_step")
        consts_ready = sem("consts_ready")
        masks_ready = sem("masks_ready")
        ones_ready = sem("ones_ready")
        tanh_ready = sem("tanh_ready")
        gate_w_ready = sem("gate_w_ready")
        var1_ready, rstd1_ready = sem("var1_ready"), sem("rstd1_ready")
        q_ready = sem("q_ready")
        qT_psum, qT_act, qT_dve = sem("qT_psum"), sem("qT_act"), sem("qT_dve")
        gates_psum, gates_tok, gates_rows = sem("gates_psum"), sem("gates_tok"), sem("gates_rows")
        fabs_ready, softplus_ready = sem("fabs_ready"), sem("softplus_ready")
        mrow_ready, exps_ready = sem("mrow_ready"), sem("exps_ready")
        drows_ready = sem("drows_ready")
        decsel_ready = sem("decsel_ready")
        cols_psum, cols_ready = sem("cols_psum"), sem("cols_ready")
        d_psum, dexp_ready = sem("d_psum"), sem("dexp_ready")
        scores_psum = sem("scores_psum")
        c_ready, far_ready, near_psum = sem("c_ready"), sem("far_ready"), sem("near_psum")
        uv_ready, state_ready, heads_ready = sem("uv_ready"), sem("state_ready"), sem("heads_ready")
        hvar_ready, hrstd_ready, z_ready, x1_ready = (
            sem("hvar_ready"), sem("hrstd_ready"), sem("z_ready"), sem("x1_ready"))
        var2_ready, rstd2_ready, x2_ready = sem("var2_ready"), sem("rstd2_ready"), sem("x2_ready")
        x2T_psum, x2T_ready = sem("x2T_psum"), sem("x2T_ready")
        route_psum, route_read = sem("route_psum"), sem("route_read")
        lsh_ready, ex_ready = sem("lsh_ready"), sem("ex_ready")
        valid_ready, csum_psum, csum_read = sem("valid_ready"), sem("csum_psum"), sem("csum_read")
        t9_ready, e9_ready = sem("t9_ready"), sem("e9_ready")
        onehot_ready, slots_psum, slots_read = sem("onehot_ready"), sem("slots_psum"), sem("slots_read")
        g_psum, u_psum, sig_ready, act_ready = sem("g_psum"), sem("u_psum"), sem("sig_ready"), sem("act_ready")
        y_psum, o_ready = sem("y_psum"), sem("o_ready")
        x2_stored = [sem(f"x2_stored{b}") for b in range(B)]
        o_stored = [sem(f"o_stored{b}") for b in range(B)]
        slots_ready = sem("slots_ready")
        gathered = [sem(f"gathered{r}") for r in range(XR)]
        xgT_psum, xgT_ready = sem("xgT_psum"), sem("xgT_ready")
        dg_psum, du_psum, dsig_ready, dact_ready = (
            sem("dg_psum"), sem("du_psum"), sem("dsig_ready"), sem("dact_ready"))
        dy_psum, ys_ready = sem("dy_psum"), sem("ys_ready")
        added = sem("added")

        block = ctx.enter_context(nc.Block())

        @block.sync
        def _(sp):
            for b in range(B):
                sp.dma_start(xs[:, b * NC:(b + 1) * NC, :], x_v[b]).then_inc(x_in[b], 16)
            for b in range(B):
                sp.dma_start(kT[:, :, b * SEQ:(b + 1) * SEQ], kT_v[b]).then_inc(k_in, 16)
            sp.dma_start(wgu_sh[:, :, :, :], A["wgu_sh"]).then_inc(w_sh_in, 16)
            sp.dma_start(wd_sh[:, :, :], A["wd_sh"]).then_inc(w_sh_in, 16)
            sp.dma_start(wgu_dyn[:, :, :, :, :], A["wgu_dyn"]).then_inc(w_dyn_in, 16)
            sp.dma_start(wd_dyn[:, :, :], A["wd_dyn"]).then_inc(w_dyn_in, 16)
            for b in range(B):
                sp.wait_ge(x2_ready, NC * (b + 1))
                sp.dma_start(x2_v[b], normed[:, b % 2, :, :]).then_inc(x2_stored[b], 16)
                if b >= 1:
                    sp.wait_ge(o_ready, NC * b)
                    sp.dma_start(out_v[b - 1], xs[:, (b - 1) * NC:b * NC, :]).then_inc(o_stored[b - 1], 16)
            sp.wait_ge(o_ready, NC * B)
            sp.dma_start(out_v[B - 1], xs[:, (B - 1) * NC:B * NC, :]).then_inc(o_stored[B - 1], 16)
            for b in range(B):
                sp.wait_ge(x2_stored[b], 16)
                sp.wait_ge(o_stored[b], 16)
            sp.wait_ge(added, 16 * E * EJ)

        @block.gpsimd
        def _(pool):
            done = [0]

            def step(ins):
                done[0] += 1
                ins.then_inc(pool_step, 1)
                pool.wait_ge(pool_step, done[0])

            pool.memset(m_half[:, :], -0.5)
            pool.memset(ones_b[:, :], 1.0)
            pool.memset(tri_b[:, :], 1.0)
            pool.memset(causal_b[:, :, :], 0.0)
            pool.memset(tri_e[:, :, :], 1.0)
            pool.memset(row_of[:, :, :], 0.0)
            pool.memset(slots[:, :, :, :], 0.0)
            pool.memset(carry[:, :], 0.0)
            pool.memset(carry_b[:, :], 0.0)
            pool.memset(keep9[:, :, :], 1.0)
            step(pool.memset(ident[:, :], 0.0))
            pool.affine_select(out=ident[:, :], in_=ident[:, :], compare_op=ALU.not_equal, fill=1.0, base=0,
                               pattern=[[-1, P]], channel_multiplier=1)
            step(pool.affine_select(out=row_of[:, :, :], in_=row_of[:, :, :], compare_op=ALU.not_equal, fill=1.0,
                                    base=0, pattern=[[-1, NH], [-4, 32]], channel_multiplier=1))
            pool.tensor_copy(ident_b[:, :], ident[:, :])
            pool.affine_select(out=tri_b[:, :], in_=tri_b[:, :], compare_op=ALU.is_ge, fill=0.0, base=0,
                               pattern=[[1, P]], channel_multiplier=-1)
            pool.affine_select(out=causal_b[:, :, :], in_=causal_b[:, :, :], compare_op=ALU.is_ge, fill=NEG, base=0,
                               pattern=[[0, NH], [1, P]], channel_multiplier=-1)
            pool.affine_select(out=tri_e[:, :, :], in_=tri_e[:, :, :], compare_op=ALU.is_gt, fill=0.0, base=0,
                               pattern=[[1, E], [-1, E]], channel_multiplier=0)
            pool.iota(iota1[:, :], pattern=[[1, P]], base=1, channel_multiplier=0,
                      allow_small_or_imprecise_dtypes=True)
            pool.iota(val[:, :, 0:1], pattern=[[0, NT * E], [0, 1]], base=0, channel_multiplier=1,
                      allow_small_or_imprecise_dtypes=True)
            pool.iota(val[:, :, 1:2].rearrange("p (n e) v -> p n (e v)", e=E), pattern=[[P, NT], [0, E]],
                      base=-int(EMPTY), channel_multiplier=0,
                      allow_small_or_imprecise_dtypes=True).then_inc(consts_ready, 1)

            def rsqrt(m, ready, count, signal):
                pool.wait_ge(ready, count)
                pool.tensor_tensor(rstd[:, 0:m], var_eps[:, 0:m], m_half[:, 0:m], ALU.pow).then_inc(signal, 1)

            def scaled_v(n):
                b, c = divmod(n, NC)
                if n >= 2:
                    pool.wait_ge(near_psum, n - 1)
                pool.tensor_tensor(uv[:, n % 2, :, :], v_aug[:, n, :, :], bc(u_t[:, c, b, :], 2, DA),
                                   ALU.mult).then_inc(uv_ready, 1)

            def add_x(b):
                pool.wait_ge(z_ready, b + 1)
                if b == 0:
                    pool.wait_ge(tanh_ready, 1)
                z = heads[:, b % 2, :, :, 0:DH]
                xb = xs[:, b * NC:(b + 1) * NC, :].rearrange("p c (h d) -> p c h d", h=NH)
                step(pool.tensor_tensor(z, z, bc(out_scale[:, :].rearrange("p (h d) -> p h d", h=NH), 1, NC), ALU.mult))
                pool.tensor_tensor(xb, z, xb, ALU.add).then_inc(x1_ready, 1)

            for b in range(B):
                rsqrt(NC, var1_ready, b + 1, rstd1_ready)
            pool.wait_ge(cols_ready, 1)
            pool.wait_ge(v_in, 16 * NT)
            pool.wait_ge(ones_ready, 1)
            for n in range(NT + NC):
                if n < NT:
                    scaled_v(n)
                if n >= NC and n % NC == 0:
                    b = n // NC - 1
                    rsqrt(NC * NH, hvar_ready, b + 1, hrstd_ready)
                if n >= NC and n % NC == 1:
                    b = n // NC - 1
                    add_x(b)
                    rsqrt(NC, var2_ready, b + 1, rstd2_ready)

            def gather(e):
                if e >= XR:
                    pool.wait_ge(xgT_psum, e - XR + 1)
                for j in range(EJ):
                    pool.indirect_dma_start(
                        out=xg[0:EROWS[j], e % XR, j, :], out_offset=None, in_=x2_dram[:, :],
                        in_offset=bass.IndirectOffsetOnAxis(ap=slot_g[0:EROWS[j], e * EJ + j:e * EJ + j + 1], axis=0),
                        bounds_check=T - 1, oob_is_err=False).then_inc(gathered[e % XR], 16)

            def scatter_add(e):
                pool.wait_ge(ys_ready, e + 1)
                if e >= 1:
                    pool.wait_ge(added, 16 * EJ * e)
                for j in range(EJ):
                    pool.indirect_dma_start(
                        out=out_rows, out_offset=bass.IndirectOffsetOnAxis(
                            ap=slot_s[0:EROWS[j], e * EJ + j:e * EJ + j + 1], axis=0),
                        in_=ys[0:EROWS[j], e % YR, j, :], in_offset=None,
                        bounds_check=T - 1, oob_is_err=False, compute_op=ALU.add).then_inc(added, 16)

            pool.wait_ge(slots_ready, 1)
            for b in range(B):
                pool.wait_ge(x2_stored[b], 16)
            for e in range(XR):
                gather(e)
            for b in range(B):
                pool.wait_ge(o_stored[b], 16)
            for e in range(E):
                if e + XR < E:
                    gather(e + XR)
                scatter_add(e)

        @block.scalar
        def _(act):
            done = [0]

            def step(ins):
                done[0] += 1
                ins.then_inc(act_step, 1)
                act.wait_ge(act_step, done[0])

            act.dma_start(w_gates[:, :, :], A["w_gates"]).then_inc(small_in, 16)
            act.dma_start(b_gates[:, :], A["b_gates"].partition_broadcast(P)).then_inc(small_in, 16)
            act.dma_start(g_pair[:, :], A["g_pair"].partition_broadcast(P)).then_inc(small_in, 16)
            act.dma_start(out_scale[:, :], A["out_scale"].partition_broadcast(P)).then_inc(small_in, 16)
            act.dma_start(w_route[:, :, :], A["w_route"]).then_inc(small_in, 16)
            for n in range(NT):
                act.dma_start(v_aug[:, n, :, 0:DH], v_v[n]).then_inc(v_in, 16)
            for b in range(B):
                act.wait_ge(qT_psum, 2 * b + 1)
                act.copy(qT[:, 0, b * SEQ:(b + 1) * SEQ], s0_ps[:, :]).then_inc(qT_act, 1)
            act.wait_ge(fabs_ready, 1)
            step(act.activation(fexp[:, :], fabs[:, :], ACT.Exp, scale=-1.0))
            act.activation(fabs[:, :], fexp[:, :], ACT.Ln, bias=1.0).then_inc(softplus_ready, 1)
            act.wait_ge(mrow_ready, 1)
            act.activation(n_row[:, :], mld[:, :], ACT.Exp, scale=-1.0)
            act.activation(dec_row[:, 1:NC], dec_row[:, 1:NC], ACT.Exp)
            for c in range(NC):
                s = slice(c * P, (c + 1) * P)
                if c >= 1:
                    act.activation(w_row[:, s], negm[:, s], ACT.Exp, bias=m_row[:, c * P - 1:c * P])
                last = act.activation(u_row[:, s], a_row[:, s], ACT.Exp, bias=negm[:, (c + 1) * P - 1:(c + 1) * P])
            last.then_inc(exps_ready, 1)
            act.wait_ge(small_in, 16 * 5)
            act.activation(tanh_g[:, :], g_pair[:, :], ACT.Tanh).then_inc(tanh_ready, 1)

            def decay(n):
                act.wait_ge(d_psum, n + 1)
                if n >= 2:
                    act.wait_ge(c_ready, n - 1)
                act.activation(dexp[:, n % 2, :], d_ps[:, :], ACT.Exp).then_inc(dexp_ready, 1)

            def copy_x2T(b):
                for k in range(KH):
                    act.wait_ge(x2T_psum, KH * b + k + 1)
                    act.copy(x2T[:, k, b * SEQ:(b + 1) * SEQ], t_ps[:, :]).then_inc(x2T_ready, 1)

            def copy_route(b):
                act.wait_ge(route_psum, b + 1)
                if b >= 2:
                    act.wait_ge(t9_ready, b - 1)
                act.copy(logit[:, b % 2, :, :], route_ps).then_inc(route_read, 1)

            def gate_sigmoid(b, i):
                m = IC * b + i
                act.wait_ge(g_psum, m + 1)
                if m >= 2:
                    act.wait_ge(act_ready, m - 1)
                act.activation(sig[:, m % 2, :], g_ps[:, :], ACT.Tanh, scale=0.5).then_inc(sig_ready, 1)

            for it in range(B + 3):
                for j in range(NC):
                    n = NC * it + j
                    if it < B:
                        decay(n)
                    if 1 <= it <= B and j == 2:
                        copy_x2T(it - 1)
                    if 1 <= it <= B and j == 3:
                        copy_route(it - 1)
                    if 2 <= it <= B + 1:
                        b = it - 2
                        if j == 0:
                            act.wait_ge(lsh_ready, b + 1)
                            act.activation(ex[:, :, :], lsh[:, :, :], ACT.Exp).then_inc(ex_ready, 1)
                        if j == 2:
                            act.wait_ge(t9_ready, b + 1)
                            act.activation(e9[:, :, :], t9[:, :, :], ACT.Exp).then_inc(e9_ready, 1)
                        gate_sigmoid(b, j)

            def copy_xgT(e):
                act.wait_ge(xgT_psum, e + 1)
                if e >= 2:
                    act.wait_ge(du_psum, e - 1)
                act.copy(xgT[:, e % 2, 0, :], s0_ps[:, 0:CAP])
                act.copy(xgT[:, e % 2, 1, :], d_ps[:, 0:CAP]).then_inc(xgT_ready, 1)

            def weigh(e):
                act.wait_ge(dy_psum, e + 1)
                if e >= YR:
                    act.wait_ge(added, 16 * EJ * (e - YR + 1))
                for j in range(EJ):
                    src = y_ps[:, j * HD:(j + 1) * HD] if j < 2 else t_ps[0:EROWS[2], 0:HD]
                    last = act.activation(ys[0:EROWS[j], e % YR, j, :], src, ACT.Copy,
                                          scale=slot_w[0:EROWS[j], e * EJ + j:e * EJ + j + 1])
                last.then_inc(ys_ready, 1)

            for e in range(E + 1):
                if e < E:
                    copy_xgT(e)
                    act.wait_ge(dg_psum, e + 1)
                    if e >= 2:
                        act.wait_ge(dact_ready, e - 1)
                    act.activation(sig[:, e % 2, 0:CAP], g_ps[:, 0:CAP], ACT.Tanh, scale=0.5).then_inc(dsig_ready, 1)
                if e >= 1:
                    weigh(e - 1)

        @block.tensor
        def _(pe):
            pe.wait_ge(consts_ready, 1)
            for b in range(B):
                pe.wait_ge(q_ready, b + 1)
                for k, dst in ((0, s0_ps), (1, d_ps)):
                    if b >= 1:
                        pe.wait_ge(qT_act if k == 0 else qT_dve, b)
                    for c in range(NC):
                        last = pe.transpose(dst[:, c * P:(c + 1) * P], normed[:, b % 2, c, k * P:(k + 1) * P],
                                            ident[:, :])
                    last.then_inc(qT_psum, 1)
            pe.wait_ge(gate_w_ready, 1)
            pe.wait_ge(k_in, 16 * B)
            for b in range(B):
                pe.wait_ge(qT_act, b + 1)
                pe.wait_ge(qT_dve, b + 1)
                for n in range(b * NC, (b + 1) * NC):
                    s = slice(n * P, (n + 1) * P)
                    for m in range(2 * KH):
                        src = qT if m < KH else kT
                        last = pe.matmul(t_ps[:, n * 2 * NH:(n + 1) * 2 * NH], src[:, m % KH, s], w_gates[:, m, :],
                                         start=(m == 0), stop=(m == 2 * KH - 1))
            last.then_inc(gates_psum, 1)
            pe.wait_ge(gates_tok, 1)
            for q, dst in ((1, u_ps), (0, g_ps)):
                for c in range(NC):
                    last = pe.transpose(dst[:, c * P:(c + 1) * P], gate_tok[:, q, c, :], ident[:, :])
                last.then_inc(gates_rows, 1)
            pe.wait_ge(exps_ready, 1)
            for row, dst, c0 in ((u_row, s0_ps, 0), (w_row, d_ps, 1), (n_row, h_ps, 0)):
                for c in range(c0, NC):
                    pe.transpose(dst[:, c * P:(c + 1) * P], row[:, c * P:(c + 1) * P], ident[:, :])
            pe.wait_ge(decsel_ready, 1)
            pe.matmul(y_ps[:, 0:B * 2 * NC], par_sel[:, :], dec_sel[:, :, :, :].rearrange("p b a c -> p (b a c)"),
                      start=True, stop=True).then_inc(cols_psum, 1)
            pe.wait_ge(drows_ready, 1)
            pe.wait_ge(cols_ready, 1)
            pe.wait_ge(v_in, 16 * NT)
            pe.wait_ge(ones_ready, 1)

            def scores(n):
                b, c = divmod(n, NC)
                tok = slice(n * P, (n + 1) * P)
                r = slice(32 * b, 32 * b + 32)
                if n >= 1:
                    pe.wait_ge(dexp_ready, n)
                pe.matmul(d_ps[:, :], dl[r, c * P:(c + 1) * P], dr[r, c, :, :].rearrange("p h s -> p (h s)"),
                          start=True, stop=False)
                pe.matmul(d_ps[:, :], ident_b[:, :], causal_b[:, :, :].rearrange("p h s -> p (h s)"),
                          start=False, stop=True).then_inc(d_psum, 1)
                if n >= 1:
                    pe.wait_ge(far_ready, n)
                for h in range(NH):
                    g = slice(DH * (h % 2), DH * (h % 2) + DH)
                    i = h // 2
                    last = pe.matmul(qk_ps[h % 2][:, i * P:(i + 1) * P], kT[g, i, tok], qT[g, i, tok],
                                     start=True, stop=True)
                if c > 0:
                    pe.wait_ge(state_ready, n)
                    for h in range(NH):
                        g = slice(DH * (h % 2), DH * (h % 2) + DH)
                        last = pe.matmul(far_ps[h % 2][:, h // 2, :], qT[g, h // 2, tok],
                                         state[g, (n - 1) % 2, h // 2, :], start=True, stop=True)
                last.then_inc(scores_psum, 1)

            def near(n):
                if n >= 0:
                    pe.wait_ge(c_ready, n + 1)
                    pe.wait_ge(state_ready, n + 1)
                if n >= 1:
                    pe.wait_ge(heads_ready, n)
                for h in range(NH if n >= 0 else 0):
                    last = pe.matmul(near_ps[:, h, :], cmat[:, n % 2, order(h) * P:(order(h) + 1) * P],
                                     v_aug[:, n, h, :], start=True, stop=True)
                if n + 1 < NT:
                    pe.wait_ge(uv_ready, n + 2)
                    for h in range(NH):
                        g = slice(DH * (h % 2), DH * (h % 2) + DH)
                        last = pe.matmul(kv_ps[g, h // 2, :], v_aug[:, n + 1, h, 0:DH], uv[:, (n + 1) % 2, h, :],
                                         start=True, stop=True)
                last.then_inc(near_psum, 1)

            def transpose_x2(b):
                pe.wait_ge(x2_ready, NC * (b + 1))
                if b >= 1:
                    pe.wait_ge(csum_read, b)
                for k in range(KH):
                    if k >= 1:
                        pe.wait_ge(x2T_ready, KH * b + k)
                    for c in range(NC):
                        last = pe.transpose(t_ps[:, c * P:(c + 1) * P], normed[:, b % 2, c, k * P:(k + 1) * P],
                                            ident[:, :])
                    last.then_inc(x2T_psum, 1)

            def route(b):
                pe.wait_ge(x2T_ready, KH * (b + 1))
                for c in range(NC):
                    s = slice((b * NC + c) * P, (b * NC + c + 1) * P)
                    for k in range(KH):
                        last = pe.matmul(route_ps[:, c, :], x2T[:, k, s], w_route[:, k, :],
                                         start=(k == 0), stop=(k == KH - 1))
                last.then_inc(route_psum, 1)

            def count(b):
                pe.wait_ge(valid_ready, b + 1)
                pe.wait_ge(route_read, min(b + 1, B))
                if b >= 1:
                    pe.wait_ge(slots_read, b)
                pe.matmul(csum_ps, ones_b[:, :], bc(carry_b[:, :], 1, NC), start=True, stop=False)
                for k in range(1, NC):
                    pe.matmul(csum_ps[:, k:NC, :], ones_b[:, :], valid_b[:, 0:NC - k, :], start=False, stop=False)
                pe.matmul(csum_ps, tri_b[:, :], valid_b[:, :, :], start=False, stop=True).then_inc(csum_psum, 1)

            def list_slots(b):
                pe.wait_ge(onehot_ready, b + 1)
                pe.wait_ge(route_read, min(b + 2, B))
                for e in range(E):
                    for c in range(NC):
                        m = c * E + e
                        last = pe.matmul(slots_ps[:, e * EJ * NV:(e + 1) * EJ * NV], onehot[:, m, :],
                                         val_j[:, m, :, :].rearrange("p j v -> p (j v)"),
                                         start=(c == 0), stop=(c == NC - 1))
                last.then_inc(slots_psum, 1)

            def gate_up(b, i):
                m = IC * b + i
                s = slice(b * SEQ, (b + 1) * SEQ)
                if m == 0:
                    pe.wait_ge(w_sh_in, 32)
                for w, dst, signal in ((0, g_ps, g_psum), (1, u_ps, u_psum)):
                    if m >= 1:
                        pe.wait_ge(act_ready, m)
                    for k in range(KH):
                        last = pe.matmul(dst[:, :], wgu_sh[:, w, k, i * P:(i + 1) * P], x2T[:, k, s],
                                         start=(k == 0), stop=(k == KH - 1))
                    last.then_inc(signal, 1)

            def down(b, c):
                pe.wait_ge(act_ready, IC * (b + 1))
                if b * NC + c >= 1:
                    pe.wait_ge(o_ready, b * NC + c)
                for i in range(IC):
                    last = pe.matmul(y_ps[:, 0:HD], act_sh[:, b % 2, i, c * P:(c + 1) * P], wd_sh[:, i, :],
                                     start=(i == 0), stop=(i == IC - 1))
                last.then_inc(y_psum, 1)

            for it in range(B + 3):
                for j in range(NC):
                    n = NC * it + j
                    if it < B:
                        scores(n)
                    if n <= NT:
                        near(n - 1)
                    if 2 <= it <= B + 1:
                        if j == 1:
                            count(it - 2)
                        gate_up(it - 2, j)
                    if 1 <= it <= B and j == 2:
                        transpose_x2(it - 1)
                    if 1 <= it <= B and j == 3:
                        route(it - 1)
                    if 2 <= it <= B + 1 and j == 3:
                        list_slots(it - 2)
                    if 3 <= it <= B + 2:
                        down(it - 3, j)

            def spread(e):
                pe.wait_ge(gathered[e % XR], 16 * EJ * (e // XR + 1))
                if e >= 1:
                    pe.wait_ge(xgT_ready, e)
                for k, dst in ((0, s0_ps), (1, d_ps)):
                    for t in range(EJ):
                        m = EROWS[t]
                        last = pe.transpose(dst[:, t * P:t * P + m], xg[0:m, e % XR, t, k * P:(k + 1) * P],
                                            ident[0:m, 0:m])
                last.then_inc(xgT_psum, 1)

            def expert_gate_up(e):
                pe.wait_ge(xgT_ready, e + 1)
                if e >= 1:
                    pe.wait_ge(dact_ready, e)
                for w, dst, signal in ((0, g_ps, dg_psum), (1, u_ps, du_psum)):
                    for k in range(KH):
                        last = pe.matmul(dst[:, 0:CAP], wgu_dyn[:, w, e, k, :], xgT[:, e % 2, k, :],
                                         start=(k == 0), stop=(k == KH - 1))
                    last.then_inc(signal, 1)

            def expert_down(e):
                pe.wait_ge(dact_ready, e + 1)
                if e >= 1:
                    pe.wait_ge(ys_ready, e)
                for t in range(EJ):
                    m = EROWS[t]
                    dst = y_ps[:, t * HD:(t + 1) * HD] if t < 2 else t_ps[0:m, 0:HD]
                    last = pe.matmul(dst, act_d[:, e % 2, t * P:t * P + m], wd_dyn[:, e, :], start=True, stop=True)
                last.then_inc(dy_psum, 1)

            pe.wait_ge(w_dyn_in, 32)
            pe.wait_ge(o_ready, NT)
            pe.wait_ge(slots_read, B)
            spread(0)
            for e in range(E):
                expert_gate_up(e)
                if e + 1 < E:
                    spread(e + 1)
                expert_down(e)

        @block.vector
        def _(dve):
            done = [0]

            def step(ins):
                done[0] += 1
                ins.then_inc(dve_step, 1)
                dve.wait_ge(dve_step, done[0])

            def variance(m, width, eps, ready):
                dve.tensor_tensor(st_s[:, 0:m], st[:, 0:m, 1], st[:, 0:m, 4], ALU.add)
                dve.tensor_tensor(st_v[:, 0:m], st[:, 0:m, 2], st[:, 0:m, 5], ALU.add)
                step(dve.tensor_tensor(st_d[:, 0:m], st[:, 0:m, 1], st[:, 0:m, 4], ALU.subtract))
                dve.tensor_scalar(mean[:, 0:m], st_s[:, 0:m], 0.5, None, ALU.mult)
                dve.tensor_scalar(st_v[:, 0:m], st_v[:, 0:m], 1.0 / width, eps, ALU.mult, ALU.add)
                step(dve.scalar_tensor_tensor(out=st_d2[:, 0:m], in0=st_d[:, 0:m], scalar=0.25, in1=st_d[:, 0:m],
                                              op0=ALU.mult, op1=ALU.mult))

            dve.memset(v_aug[:, :, :, DH:DA].rearrange("p n h d -> p (n h d)"), 1.0).then_inc(ones_ready, 1)
            for b in range(B):
                dve.wait_ge(x_in[b], 16)
                for c in range(NC):
                    last = dve.bn_stats(st[:, c, :], xs[:, b * NC + c, :])
                step(last)
                variance(NC, HD, 1e-5, None)
                dve.tensor_tensor(var_eps[:, 0:NC], st_v[:, 0:NC], st_d2[:, 0:NC], ALU.add).then_inc(var1_ready, 1)
                dve.wait_ge(rstd1_ready, b + 1)
                if b >= 2:
                    dve.wait_ge(qT_psum, KH * (b - 1))
                for c in range(NC):
                    last = dve.tensor_scalar(normed[:, b % 2, c, :], xs[:, b * NC + c, :], mean[:, c:c + 1],
                                             rstd[:, c:c + 1], ALU.subtract, ALU.mult)
                last.then_inc(q_ready, 1)
                if b == 0:
                    dve.wait_ge(small_in, 16 * 5)
                    dve.tensor_tensor(w_gates[:, KH:2 * KH, :], w_gates[:, KH:2 * KH, :], w_gates[:, 2 * KH:3 * KH, :],
                                      ALU.add).then_inc(gate_w_ready, 1)
                dve.wait_ge(qT_psum, KH * b + 2)
                dve.tensor_copy(qT[:, 1, b * SEQ:(b + 1) * SEQ], d_ps[:, :]).then_inc(qT_dve, 1)
            dve.wait_ge(consts_ready, 1)
            dve.tensor_reduce(head_of[:, :], row_of[:, :, :], AX.X, ALU.add)
            dve.tensor_reduce(pair_row[:, :, :].rearrange("p b a -> p (b a)"),
                              row_of[:, :, :].rearrange("p (a r) (b j) -> p b j a r", a=2, j=8)[:, :, 0, :, :],
                              AX.X, ALU.add)
            step(dve.tensor_reduce(rep_of[:, :], row_of[:, :, :].rearrange("p h (b j) -> p j b h", j=8), AX.XY, ALU.add))
            dve.tensor_tensor(is_a[:, :], rep_of[:, 0:1], rep_of[:, 1:2], ALU.add)
            dve.tensor_tensor(is_m[:, :], rep_of[:, 2:3], rep_of[:, 3:4], ALU.add)
            dve.tensor_tensor(is_hi[:, :], rep_of[:, 0:1], rep_of[:, 2:3], ALU.add)
            dve.tensor_tensor(is_lo[:, :], rep_of[:, 1:2], rep_of[:, 3:4], ALU.add)
            step(dve.tensor_tensor(parity[:, :], head_of[:, 0:2], head_of[:, 2:4], ALU.add))
            for a in range(2):
                dve.tensor_copy(par_sel[:, a * DH:(a + 1) * DH], parity[:, a:a + 1].to_broadcast([P, DH]))
            dve.wait_ge(gates_psum, 1)
            gp = t_ps[:, 0:NT * 2 * NH].rearrange("p (b c q h) -> p c q b h", c=NC, q=2, h=NH)
            for c in range(NC):
                for q in range(2):
                    last = dve.tensor_tensor(
                        gate_tok[:, q, c, :].rearrange("p (b j h) -> p b j h", j=8, h=NH),
                        bc(gp[:, c, q, :, :], 2, 8),
                        bc(bc(b_gates[:, q * NH:(q + 1) * NH], 1, 8), 1, B), ALU.add)
            last.then_inc(gates_tok, 1)
            dve.wait_ge(gates_rows, 1)
            dve.tensor_scalar(fmin[:, :], u_ps[:, :], 0.0, None, ALU.min)
            step(dve.tensor_copy(w_row[:, :], u_ps[:, :]))
            dve.scalar_tensor_tensor(out=fabs[:, :], in0=w_row[:, :], scalar=-1.0, in1=w_row[:, :],
                                     op0=ALU.mult, op1=ALU.max).then_inc(fabs_ready, 1)
            dve.wait_ge(softplus_ready, 1)
            dve.memset(ones_row[:, :], 1.0)
            step(dve.tensor_tensor(fmin[:, :], fmin[:, :], fabs[:, :], ALU.subtract))
            step(dve.tensor_tensor_scan(cs[:, :], ones_row[:, :], fmin[:, :], 0.0, ALU.mult, ALU.add))
            dve.wait_ge(gates_rows, 2)
            step(dve.tensor_tensor(a_row[:, :], g_ps[:, :], cs[:, :], ALU.subtract))
            step(dve.tensor_tensor_scan(m_row[:, :], ones_row[:, :], a_row[:, :], -3.0e38, ALU.mult, ALU.max))
            dve.tensor_tensor(dec_row[:, 1:NC], m_row[:, P - 1:(NC - 1) * P:P], m_row[:, 2 * P - 1:NC * P:P],
                              ALU.subtract)
            dve.tensor_tensor(mld[:, :], cs[:, :], m_row[:, :], ALU.add)
            dve.tensor_scalar(negm[:, :], m_row[:, :], -1.0, None, ALU.mult).then_inc(mrow_ready, 1)
            dve.wait_ge(mrow_ready, 1)
            step(dve.tensor_scalar(av[:, :], a_row[:, :], is_a[:, :], None, ALU.mult))
            step(dve.scalar_tensor_tensor(out=av[:, :], in0=negm[:, :], scalar=is_m[:, :], in1=av[:, :],
                                          op0=ALU.mult, op1=ALU.add))
            step(dve.tensor_copy(av_hi[:, :], av[:, :]))
            step(dve.tensor_tensor(av_lo[:, :], av[:, :], av_hi[:, :].bitcast(fp32), ALU.subtract))
            step(dve.tensor_scalar(av[:, :], av_hi[:, :].bitcast(fp32), is_hi[:, :], None, ALU.mult))
            step(dve.scalar_tensor_tensor(out=av[:, :], in0=av_lo[:, :], scalar=is_lo[:, :], in1=av[:, :],
                                          op0=ALU.mult, op1=ALU.add))
            dve.tensor_scalar(dl[:, :], av[:, :], is_a[:, :], is_m[:, :], ALU.mult, ALU.add)
            step(dve.tensor_scalar(av_lo[:, :], av[:, :], is_m[:, :], is_a[:, :], ALU.mult, ALU.add))
            for h in range(NH):
                last = dve.tensor_scalar(dr[:, :, order(h), :], av_lo[:, :].rearrange("p (c s) -> p c s", c=NC),
                                         head_of[:, h:h + 1], None, ALU.mult)
            last.then_inc(drows_ready, 1)
            dve.wait_ge(exps_ready, 1)
            step(dve.memset(dec_row[:, 0:1], 0.0))
            dve.tensor_tensor(dec_sel[:, :, :, :].rearrange("p b a c -> p (b a) c"),
                              bc(pair_row[:, :, :].rearrange("p b a -> p (b a)"), 2, NC),
                              bc(dec_row[:, :], 1, 2 * B), ALU.mult).then_inc(decsel_ready, 1)
            dve.wait_ge(cols_psum, 1)
            for dst, src, c0 in ((u_t, s0_ps, 0), (w_t, d_ps, 1), (n_t, h_ps, 0)):
                dve.tensor_copy(dst[:, c0:NC, :, :],
                                src[:, :].rearrange("p (c b r) -> p c b r", c=NC, b=B)[:, c0:NC, :, 0:NH])
            dve.tensor_copy(dec_t[:, :, :, :].rearrange("p b a c -> p (b a c)"),
                            y_ps[:, 0:B * 2 * NC]).then_inc(cols_ready, 1)
            dve.wait_ge(cols_ready, 1)
            dve.wait_ge(tanh_ready, 1)
            dve.tensor_scalar(half_gf[:, :], tanh_g[:, 1:2], 0.5, None, ALU.mult)
            step(dve.tensor_scalar(out_scale[:, :], out_scale[:, :], tanh_g[:, 0:1], None, ALU.mult))

            def decay_scores(n):
                b, c = divmod(n, NC)
                dve.wait_ge(scores_psum, n + 1)
                dve.wait_ge(dexp_ready, n + 1)
                if n >= 2:
                    dve.wait_ge(near_psum, n)
                for a in range(2):
                    m = slice(a * 2 * P, (a + 1) * 2 * P)
                    last = dve.scalar_tensor_tensor(out=cmat[:, n % 2, m], in0=qk_ps[a], scalar=QSCALE,
                                                    in1=dexp[:, n % 2, m], op0=ALU.mult, op1=ALU.mult)
                last.then_inc(c_ready, 1)
                if c > 0:
                    for a in range(2):
                        last = dve.tensor_tensor(far[:, n % 2, a:NH:2, :], far_ps[a], bc(w_t[:, c, b, a:NH:2], 2, DA),
                                                 ALU.mult)
                    last.then_inc(far_ready, 1)
                else:
                    dve.memset(far[:, n % 2, :, :], 0.0).then_inc(far_ready, 1)

            def new_state(n):
                b, c = divmod(n, NC)
                dve.wait_ge(near_psum, n + 1)
                if n >= 2:
                    dve.wait_ge(scores_psum, n)
                if c == 0 or c == NC - 1:
                    dve.tensor_copy(state[:, n % 2, :, :], kv_ps).then_inc(state_ready, 1)
                else:
                    dve.wait_ge(state_ready, n)
                    for a in range(2):
                        last = dve.scalar_tensor_tensor(
                            out=state[:, n % 2, a, :], in0=state[:, (n - 1) % 2, a, :], scalar=dec_t[:, b, a, c:c + 1],
                            in1=kv_ps[:, a, :], op0=ALU.mult, op1=ALU.add)
                    last.then_inc(state_ready, 1)

            def join(n):
                b, c = divmod(n, NC)
                dve.wait_ge(near_psum, n + 2)
                dve.wait_ge(far_ready, n + 1)
                if b >= 2 and c == 0:
                    dve.wait_ge(x1_ready, b - 1)
                dve.scalar_tensor_tensor(
                    out=heads[:, b % 2, c, :, :].rearrange("p h d -> p (h d)"),
                    in0=far[:, n % 2, :, :].rearrange("p h d -> p (h d)"), scalar=QSCALE,
                    in1=h_ps[:, 0:NH * DA], op0=ALU.mult, op1=ALU.add).then_inc(heads_ready, 1)
                dve.wait_ge(heads_ready, n + 1)

            def head_stats(b):
                hb = heads[:, b % 2, :, :, :].rearrange("p c h d -> p (c h) d")
                for g in range(NC * NH):
                    last = dve.bn_stats(st[:, g, :], hb[:, g, 0:DH])
                step(last)
                m = NC * NH
                variance(m, DH, 0.0, None)
                step(dve.tensor_tensor(st_v[:, :], st_v[:, :], st_d2[:, :], ALU.add))
                step(dve.scalar_tensor_tensor(out=den[:, :], in0=hb[:, :, DH], scalar=-1.0, in1=hb[:, :, DH],
                                              op0=ALU.mult, op1=ALU.max))
                step(dve.tensor_tensor(den[:, :].rearrange("p (c h) -> p c h", c=NC),
                                       den[:, :].rearrange("p (c h) -> p c h", c=NC), n_t[:, :, b, :], ALU.max))
                step(dve.tensor_scalar(den[:, :], den[:, :], 1e-6, None, ALU.add))
                step(dve.reciprocal(rden[:, :], den[:, :]))
                step(dve.tensor_tensor(rden2[:, :], rden[:, :], rden[:, :], ALU.mult))
                step(dve.tensor_tensor(st_v[:, :], st_v[:, :], rden2[:, :], ALU.mult))
                dve.tensor_scalar(var_eps[:, :], st_v[:, :], 1e-6, None, ALU.add).then_inc(hvar_ready, 1)

            def head_norm(b):
                hb = heads[:, b % 2, :, :, :].rearrange("p c h d -> p (c h) d")
                dve.wait_ge(hrstd_ready, b + 1)
                step(dve.tensor_tensor(hscale[:, :], rstd[:, :], rden[:, :], ALU.mult))
                for g in range(NC * NH):
                    last = dve.tensor_scalar(hb[:, g, 0:DH], hb[:, g, 0:DH],
                                             mean[:, g:g + 1], hscale[:, g:g + 1], ALU.subtract, ALU.mult)
                last.then_inc(z_ready, 1)

            def norm2_stats(b):
                dve.wait_ge(x1_ready, b + 1)
                for c in range(NC):
                    last = dve.bn_stats(st[:, c, :], xs[:, b * NC + c, :])
                step(last)
                variance(NC, HD, 1e-5, None)
                dve.tensor_tensor(var_eps[:, 0:NC], st_v[:, 0:NC], st_d2[:, 0:NC], ALU.add).then_inc(var2_ready, 1)

            def norm2(b):
                dve.wait_ge(rstd2_ready, b + 1)
                if b >= 2:
                    dve.wait_ge(x2_stored[b - 2], 16)
                    dve.wait_ge(x2T_psum, KH * (b - 1))
                for c in range(NC):
                    dve.tensor_scalar(normed[:, b % 2, c, :], xs[:, b * NC + c, :], mean[:, c:c + 1],
                                      rstd[:, c:c + 1], ALU.subtract, ALU.mult).then_inc(x2_ready, 1)

            def choose(b):
                lg = logit[:, b % 2, :, 0:E]
                pq = "p (c i) j -> p c i j"
                dve.wait_ge(route_read, b + 1)
                dve.scalar_tensor_tensor(out=labs[:, :, :], in0=lg, scalar=-1.0, in1=lg, op0=ALU.mult, op1=ALU.max)
                step(dve.tensor_reduce(lmax[:, :], lg, AX.X, ALU.max))
                dve.tensor_tensor(lsh[:, :, :], lg, bc(lmax[:, :], 2, E), ALU.subtract).then_inc(lsh_ready, 1)
                li, lj = bc(lg, 3, E), bc(lg, 2, E)
                pd4, pb4, pc4, pm4 = (t[:, :, :].rearrange(pq, c=NC) for t in (pd, pb, pc, pm))
                dve.tensor_tensor(pd4, lj, li, ALU.subtract)
                step(dve.tensor_tensor(pm4, bc(labs[:, :, :], 2, E), bc(labs[:, :, :], 3, E), ALU.max))
                flat = "p m j -> p (m j)"
                tri = bc(tri_e[:, :, :].rearrange("p i j -> p (i j)"), 1, NC)
                f4 = "p (c i) j -> p c (i j)"
                step(dve.scalar_tensor_tensor(out=pe_[:, :, :].rearrange(f4, c=NC), in0=pd[:, :, :].rearrange(f4, c=NC),
                                              scalar=0.0, in1=tri, op0=ALU.is_equal, op1=ALU.mult))
                step(dve.scalar_tensor_tensor(out=pb[:, :, :].rearrange(flat), in0=pd[:, :, :].rearrange(flat), scalar=0.0,
                                              in1=pe_[:, :, :].rearrange(flat), op0=ALU.is_gt, op1=ALU.add))
                step(dve.scalar_tensor_tensor(out=pm[:, :, :].rearrange(flat), in0=pm[:, :, :].rearrange(flat), scalar=0.2,
                                              in1=pd[:, :, :].rearrange(flat), op0=ALU.mult, op1=ALU.add))
                step(dve.scalar_tensor_tensor(out=pm[:, :, :].rearrange(flat), in0=pm[:, :, :].rearrange(flat), scalar=0.0,
                                              in1=pb[:, :, :].rearrange(flat), op0=ALU.is_ge, op1=ALU.is_gt))
                dve.tensor_reduce(rank[:, :, :].rearrange("p c e -> p (c e)"), pb[:, :, :], AX.X, ALU.add)
                dve.wait_ge(ex_ready, b + 1)
                ej = bc(ex[:, :, :], 2, E)
                dve.tensor_tensor(pc4, pb4, ej, ALU.mult)
                step(dve.tensor_tensor(pm4, pm4, ej, ALU.mult))
                dve.tensor_reduce(before[:, :, :].rearrange("p c e -> p (c e)"), pc[:, :, :], AX.X, ALU.add)
                dve.tensor_reduce(mden[:, :, :].rearrange("p c e -> p (c e)"), pm[:, :, :], AX.X, ALU.add)
                step(dve.tensor_reduce(tot75[:, :], ex[:, :, :], AX.X, ALU.add))
                step(dve.tensor_scalar(tot75[:, :], tot75[:, :], 0.75, None, ALU.mult))
                step(dve.tensor_tensor(before[:, :, :], before[:, :, :], bc(tot75[:, :], 2, E), ALU.is_lt))
                step(dve.scalar_tensor_tensor(out=valid[:, :, :].rearrange("p c e -> p (c e)"),
                                              in0=rank[:, :, :].rearrange("p c e -> p (c e)"), scalar=4.0,
                                              in1=before[:, :, :].rearrange("p c e -> p (c e)"),
                                              op0=ALU.is_lt, op1=ALU.mult))
                if b >= 1:
                    step(dve.tensor_tensor(carry[:, :], carry[:, :], msum[:, :], ALU.add))
                    dve.wait_ge(csum_psum, b)
                    dve.tensor_copy(carry_b[:, :], carry[:, :])
                dve.tensor_copy(valid_b[:, :, :], valid[:, :, :]).then_inc(valid_ready, 1)
                step(dve.tensor_reduce(msum[:, :], valid[:, :, :].rearrange("p c e -> p e c"), AX.X, ALU.add))
                step(dve.tensor_scalar(mden[:, :, :], mden[:, :, :], 1e-30, None, ALU.max))
                step(dve.reciprocal(mden[:, :, :], mden[:, :, :]))
                step(dve.tensor_tensor(rw[:, :, :], ex[:, :, :], mden[:, :, :], ALU.mult))
                step(dve.tensor_tensor(rw[:, :, :], rw[:, :, :], valid[:, :, :], ALU.mult))
                step(dve.tensor_reduce(rsum[:, :], rw[:, :, :], AX.X, ALU.add))
                step(dve.reciprocal(rsum[:, :], rsum[:, :]))
                step(dve.tensor_tensor(rw[:, :, :], rw[:, :, :], bc(rsum[:, :], 2, E), ALU.mult))

            def capacity(b):
                dve.wait_ge(csum_psum, b + 1)
                dve.tensor_copy(pos[:, :, :], csum_ps).then_inc(csum_read, 1)
                dve.wait_ge(csum_read, b + 1)
                step(dve.tensor_scalar(l9[:, :, 0:E], pos[:, :, :], float(CAP), None, ALU.is_le))
                step(dve.tensor_tensor(keep9[:, :, 0:E], l9[:, :, 0:E], valid[:, :, :], ALU.mult))
                step(dve.tensor_scalar(l9[:, :, :], keep9[:, :, :], -NEG, NEG, ALU.mult, ALU.add))
                step(dve.tensor_tensor(l9[:, :, :], l9[:, :, :], logit[:, b % 2, :, :], ALU.add))
                step(dve.tensor_reduce(lmax[:, :], l9[:, :, :], AX.X, ALU.max))
                dve.tensor_tensor(t9[:, :, :], l9[:, :, :], bc(lmax[:, :], 2, E + 1), ALU.subtract).then_inc(t9_ready, 1)
                kf = keep9[:, :, 0:E]
                pf = pos[:, :, :].rearrange("p c e -> p (c e)")
                step(dve.tensor_scalar(tile_j[:, :], pf, float(P), None, ALU.is_gt))
                step(dve.scalar_tensor_tensor(out=tile_j[:, :], in0=pf, scalar=float(2 * P), in1=tile_j[:, :],
                                              op0=ALU.is_gt, op1=ALU.add))
                step(dve.scalar_tensor_tensor(out=pk[:, :], in0=tile_j[:, :], scalar=-float(P), in1=pf,
                                              op0=ALU.mult, op1=ALU.add))
                step(dve.tensor_tensor(pk[:, :].rearrange("p (c e) -> p c e", c=NC),
                                       pk[:, :].rearrange("p (c e) -> p c e", c=NC), kf, ALU.mult))

            def weights(b):
                kf = keep9[:, :, 0:E]
                dve.wait_ge(e9_ready, b + 1)
                dve.tensor_reduce(rsum[:, :], e9[:, :, :], AX.X, ALU.add)
                step(dve.tensor_reduce(sdyn[:, :], e9[:, :, 0:E], AX.X, ALU.add))
                step(dve.reciprocal(rsum[:, :], rsum[:, :]))
                step(dve.tensor_scalar(rsum[:, :], rsum[:, :], half_gf[:, :], None, ALU.mult))
                dve.tensor_tensor(w_shared[:, b * NC:(b + 1) * NC], e9[:, :, E], rsum[:, :], ALU.mult)
                step(dve.tensor_tensor(sdyn[:, :], sdyn[:, :], rsum[:, :], ALU.mult))
                step(dve.tensor_tensor(rw[:, :, :], rw[:, :, :], bc(sdyn[:, :], 2, E), ALU.mult))
                step(dve.tensor_tensor(rw[:, :, :], rw[:, :, :], kf, ALU.mult))
                rf = rw[:, :, :].rearrange("p c e -> p (c e)")
                vb = val[:, b * NC * E:(b + 1) * NC * E, :]
                if b >= 1:
                    dve.wait_ge(slots_psum, b)
                step(dve.tensor_copy(vb[:, :, 2], rf))
                step(dve.tensor_tensor(res[:, :], rf, vb[:, :, 2], ALU.subtract))
                step(dve.tensor_copy(vb[:, :, 3], res[:, :]))
                step(dve.tensor_tensor(res[:, :], res[:, :], vb[:, :, 3], ALU.subtract))
                step(dve.tensor_copy(vb[:, :, 4], res[:, :]))
                for j in range(EJ):
                    dve.scalar_tensor_tensor(out=val_j[:, :, j, :], in0=bc(tile_j[:, :], 2, NV), scalar=float(j),
                                             in1=vb, op0=ALU.is_equal, op1=ALU.mult)
                for m in range(NC * E):
                    last = dve.tensor_scalar(onehot[:, m, :], iota1[:, :], pk[:, m:m + 1], None, ALU.is_equal)
                last.then_inc(onehot_ready, 1)

            def add_slots(b):
                dve.wait_ge(slots_psum, b + 1)
                sf = slots[:, :, :, :].rearrange("p e j v -> p (e j v)")
                dve.tensor_tensor(sf, sf, slots_ps, ALU.add).then_inc(slots_read, 1)
                dve.wait_ge(slots_read, b + 1)

            def silu_mul(b, i):
                m = IC * b + i
                dve.wait_ge(sig_ready, m + 1)
                if b >= 2 and i == 0:
                    dve.wait_ge(y_psum, NC * (b - 1))
                step(dve.scalar_tensor_tensor(out=sig[:, m % 2, :], in0=sig[:, m % 2, :], scalar=1.0, in1=g_ps[:, :],
                                              op0=ALU.add, op1=ALU.mult))
                dve.wait_ge(u_psum, m + 1)
                dve.tensor_tensor(act_sh[:, b % 2, i, :], sig[:, m % 2, :], u_ps[:, :], ALU.mult).then_inc(act_ready, 1)

            def shared_out(b, c):
                n = b * NC + c
                dve.wait_ge(y_psum, n + 1)
                dve.scalar_tensor_tensor(out=xs[:, n, :], in0=y_ps[:, 0:HD], scalar=w_shared[:, n:n + 1],
                                         in1=xs[:, n, :], op0=ALU.mult, op1=ALU.add).then_inc(o_ready, 1)

            for it in range(B + 3):
                for j in range(NC):
                    n = NC * it + j
                    if it < B:
                        decay_scores(n)
                    if 1 <= n <= NT:
                        join(n - 1)
                    if it < B:
                        new_state(n)
                    if 1 <= it <= B:
                        if j == 0:
                            head_stats(it - 1)
                            head_norm(it - 1)
                        if j == 1:
                            norm2_stats(it - 1)
                            norm2(it - 1)
                    if 2 <= it <= B + 1:
                        if j == 0:
                            choose(it - 2)
                        if j == 1:
                            capacity(it - 2)
                        if j == 2:
                            weights(it - 2)
                        silu_mul(it - 2, j)
                        if j == 3:
                            add_slots(it - 2)
                    if 3 <= it <= B + 2:
                        shared_out(it - 3, j)
                    if it == B + 1 and j == 3:
                        sl = slots[:, :, :, :].rearrange("p e j v -> p (e j) v")
                        dve.tensor_tensor(slot_id[:, :], sl[:, :, 0], sl[:, :, 1], ALU.add)
                        step(dve.tensor_tensor(slot_w[:, :], sl[:, :, 3], sl[:, :, 4], ALU.add))
                        dve.tensor_tensor(slot_w[:, :], slot_w[:, :], sl[:, :, 2], ALU.add)
                        step(dve.tensor_scalar(slot_id[:, :], slot_id[:, :], EMPTY, None, ALU.add))
                        dve.tensor_copy(slot_s[:, :], slot_id[:, :])
                        dve.tensor_scalar(slot_g[:, :], slot_id[:, :], float(T - 1), None,
                                          ALU.min).then_inc(slots_ready, 1)

            for e in range(E):
                dve.wait_ge(dsig_ready, e + 1)
                step(dve.scalar_tensor_tensor(out=sig[:, e % 2, 0:CAP], in0=sig[:, e % 2, 0:CAP], scalar=1.0,
                                              in1=g_ps[:, 0:CAP], op0=ALU.add, op1=ALU.mult))
                dve.wait_ge(du_psum, e + 1)
                if e >= 2:
                    dve.wait_ge(dy_psum, e - 1)
                dve.tensor_tensor(act_d[:, e % 2, :], sig[:, e % 2, 0:CAP], u_ps[:, 0:CAP],
                                  ALU.mult).then_inc(dact_ready, 1)


def kernel(**inputs):
    import numpy as np
    import concourse.bacc as bacc
    from concourse.bass_utils import run_bass_kernel_spmd as run

    a = {k: np.asarray(v) for k, v in inputs.items()}
    P, KH = 128, 2

    def lay(t):
        return np.ascontiguousarray(t)

    x = a["x"].reshape(2048, 256)
    ctx = a["ctx_1024"].reshape(2048, 256)
    sh = np.stack([a["L0_ffn_sh_gate_w"][0], a["L0_ffn_sh_up_w"][0]])
    dyn = np.stack([a["L0_ffn_dyn_gate_w"], a["L0_ffn_dyn_up_w"]])
    gates = np.concatenate([a["L0_xattn_igate_kernel"], a["L0_xattn_fgate_kernel"]], axis=1)
    laid = {
        "x": lay(x),
        "ctx": lay(ctx),
        "ctxT": lay(ctx.T),
        "wgu_sh": lay(sh.reshape(2, 512, KH, P).transpose(3, 0, 2, 1)),
        "wd_sh": lay(a["L0_ffn_sh_down_w"][0].reshape(256, 4, P).transpose(2, 1, 0)),
        "wgu_dyn": lay(dyn.reshape(2, 8, P, KH, P).transpose(4, 0, 1, 3, 2)),
        "wd_dyn": lay(a["L0_ffn_dyn_down_w"].transpose(2, 0, 1)),
        "w_route": lay(a["L0_ffn_gate_w"].reshape(9, KH, P).transpose(2, 1, 0)),
        "w_gates": lay(gates.reshape(3 * KH, P, 8).transpose(1, 0, 2)),
        "b_gates": lay(np.concatenate([a["L0_xattn_igate_bias"], a["L0_xattn_fgate_bias"]])),
        "g_pair": lay(np.concatenate([a["g_xattn"], a["g_ffn"]])),
        "out_scale": lay(a["L0_xattn_outnorm_scale"]),
    }
    nc = bacc.Bacc("TRN2", target_bir_lowering=False, num_devices=1)
    fp32 = mybir.dt.float32
    aps = {k: nc.dram_tensor(f"in_{k}", v.shape, fp32, kind="ExternalInput").ap() for k, v in laid.items()}
    out = nc.dram_tensor("out_rows", (4, 512, 256), fp32, kind="ExternalOutput").ap()
    gated_mlstm_moe_block(nc, aps, out)
    r = run(nc, [{f"in_{k}": v for k, v in laid.items()}], core_ids=[0])
    return r.results[0]["out_rows"]
```

```python
import concourse.bass as bass
from concourse import mybir
from contextlib import ExitStack


def gated_mlstm_moe_block(nc, A, out):
    fp32, f32r, bf16, i32 = (mybir.dt.float32, mybir.dt.float32r, mybir.dt.bfloat16, mybir.dt.int32)
    ALU = mybir.AluOpType
    ACT = mybir.ActivationFunctionType
    AX = mybir.AxisListType

    P = 128
    B, SEQ, HD = 4, 512, 256
    NH, DH = 4, 64
    DA = DH + 1
    NC = SEQ // P
    NT = B * NC
    T = B * SEQ
    KH = HD // P
    E, EI = 8, 128
    SI = 512
    IC = SI // P
    CAP = 320
    EJ = 3
    EROWS = [128, 128, 64]
    NV = 5
    AHEAD = 3
    EMPTY = 4096.0
    HS = SEQ // 2
    NG = IC * 2
    PB = 2 * NC
    HSTATS, HNORM, ADDX, STATS2, NORM2, X2T = 9, 10, 11, 13, 14, 15
    ROUTE, CHOOSE, PICK, COUNT, CAPAC, LISTS = 17, 18, 19, 20, 21, 23
    GATEUP, DOWN = 18, 24
    LAST = PB * (B - 1) + DOWN + 2 * NC
    QSCALE = float(DH) ** -0.5
    NEG = -1.0e30

    ctx = ExitStack()
    with ctx:
        def sb(name, shape, dt=fp32):
            return ctx.enter_context(nc.sbuf_tensor(name, shape, dt))

        def sem(name):
            return ctx.enter_context(nc.semaphore(name))

        def bank(name):
            return ctx.enter_context(nc.psum_tensor(name, [P, 512], fp32))

        def order(h):
            return (h % 2) * 2 + h // 2

        def due(t, offset):
            b, r = divmod(t - offset, PB)
            return b if r == 0 and 0 <= b < B else None

        def unit(t, offset, count, every):
            for i in range(count):
                b = due(t, offset + i * every)
                if b is not None:
                    return b, i
            return None

        def bc(ap, axis, n):
            ap = ap.unsqueeze(axis)
            shape = list(ap.shape)
            shape[axis] = n
            return ap.to_broadcast(shape)

        xs = sb("xs", [P, NT, HD])
        v_aug = sb("v_aug", [P, NT, NH, DA])
        kT = sb("kT", [P, KH, T])
        qT = sb("qT", [P, KH, T])
        x2T = sb("x2T", [P, KH, T])
        normed = sb("normed", [P, 2, NC, HD])
        wgu_sh = sb("wgu_sh", [P, 2, KH, SI])
        wd_sh = sb("wd_sh", [P, IC, HD])
        wgu_dyn = sb("wgu_dyn", [P, 2, E, KH, EI])
        wd_dyn = sb("wd_dyn", [P, E, HD])
        w_route = sb("w_route", [P, KH, E + 1])
        w_gates = sb("w_gates", [P, 3 * KH, 2 * NH])
        b_rows = sb("b_rows", [P, 2])
        w_rows = sb("w_rows", [P, 2 * KH, 2, 8, NH])
        g_pair = sb("g_pair", [P, 2])
        tanh_g = sb("tanh_g", [P, 2])
        half_gf = sb("half_gf", [P, 1])
        out_scale = sb("out_scale", [P, HD])
        ident = sb("ident", [P, P])
        ident_b = sb("ident_b", [P, P], bf16)
        tri_b = sb("tri_b", [P, P], bf16)
        ones_b = sb("ones_b", [P, P], bf16)
        causal_b = sb("causal_b", [P, NH, P], bf16)
        iota1 = sb("iota1", [P, P], bf16)
        tri_e = sb("tri_e", [P, E, E])
        row_of = sb("row_of", [P, NH, 32])
        head_of = sb("head_of", [P, NH])
        rep_of = sb("rep_of", [P, 8])
        is_a = sb("is_a", [P, 1])
        is_m = sb("is_m", [P, 1])
        is_hi = sb("is_hi", [P, 1])
        is_lo = sb("is_lo", [P, 1])
        parity = sb("parity", [P, 2])
        par_sel = sb("par_sel", [P, P])
        pair_row = sb("pair_row", [P, B, 2])
        m_half = sb("m_half", [P, 16])
        act_sh = sb("act_sh", [P, 2, IC, SEQ])
        fmin, fabs, fexp, u_row, w_row, n_row, av, av_lo = (act_sh[:, i // IC, i % IC, :] for i in range(2 * IC))
        ones_row, av_hi = fexp, fabs.bitcast(f32r)
        sig = sb("sig", [P, 2, SEQ])
        a_row, negm = sig[:, 0, :], sig[:, 1, :]
        m_row = sb("m_row", [P, SEQ])
        dec_row = sb("dec_row", [P, NC])
        dec_sel = sb("dec_sel", [P, B, 2, NC])
        dl = sb("dl", [P, SEQ], f32r)
        dr = sb("dr", [P, NC, NH, P], f32r)
        u_t = sb("u_t", [P, NC, B, NH])
        w_t = sb("w_t", [P, NC, B, NH])
        n_t = sb("n_t", [P, NC, B, NH])
        dec_t = sb("dec_t", [P, B, 2, NC])
        dexp = sb("dexp", [P, 2, NH * P])
        cmat = sb("cmat", [P, 2, NH * P])
        gi_row, gf_row = dexp[:, 0, :], dexp[:, 1, :]
        cs, mld = cmat[:, 0, :], cmat[:, 1, :]
        uv = sb("uv", [P, 2, NH, DA])
        state = sb("state", [P, 2, 2, 2 * DA])
        far = sb("far", [P, 2, NH, DA])
        heads = sb("heads", [P, 2, NC, NH, DA])
        st = sb("st", [P, 16, 6])
        st_s = sb("st_s", [P, 16])
        st_d = sb("st_d", [P, 16])
        st_v = sb("st_v", [P, 16])
        st_d2 = sb("st_d2", [P, 16])
        mean = sb("mean", [P, 16])
        var_eps = sb("var_eps", [P, 16])
        rstd = sb("rstd", [P, 16])
        den = sb("den", [P, 16])
        rden = sb("rden", [P, 16])
        rden2 = sb("rden2", [P, 16])
        hscale = sb("hscale", [P, 16])
        hshift = sb("hshift", [P, 16])
        mean2 = sb("mean2", [P, NC])
        var2 = sb("var2", [P, NC])
        rstd2 = sb("rstd2", [P, NC])
        scale2 = sb("scale2", [P, NC])
        shift2 = sb("shift2", [P, NC])
        logit = sb("logit", [P, 2, NC, E + 1])
        lmax = sb("lmax", [P, NC])
        labs = sb("labs", [P, NC, E])
        lsh = sb("lsh", [P, NC, E])
        ex = sb("ex", [P, NC, E])
        tot75 = sb("tot75", [P, NC])
        pd = sb("pd", [P, NC * E, E])
        pe_ = sb("pe_", [P, NC * E, E])
        pb = sb("pb", [P, NC * E, E])
        pc = sb("pc", [P, NC * E, E])
        pm = sb("pm", [P, NC * E, E])
        rank = sb("rank", [P, NC, E])
        before = sb("before", [P, NC, E])
        valid = sb("valid", [P, NC, E])
        valid_b = sb("valid_b", [P, NC, E], bf16)
        mden = sb("mden", [P, NC, E])
        rw = sb("rw", [P, NC, E])
        rsum = sb("rsum", [P, NC])
        carry = sb("carry", [P, E])
        carry_b = sb("carry_b", [P, E], bf16)
        msum = sb("msum", [P, E])
        pos = sb("pos", [P, NC, E])
        keep9 = sb("keep9", [P, NC, E + 1])
        l9 = sb("l9", [P, NC, E + 1])
        t9 = sb("t9", [P, NC, E + 1])
        e9 = sb("e9", [P, NC, E + 1])
        sdyn = sb("sdyn", [P, NC])
        w_shared = sb("w_shared", [P, NT])
        tile_j = sb("tile_j", [P, NC * E])
        pk = sb("pk", [P, NC * E])
        onehot = sb("onehot", [P, NC * E, P], bf16)
        val = sb("val", [P, NT * E, NV], bf16)
        res = sb("res", [P, NC * E])
        val_j = sb("val_j", [P, NC * E, EJ, NV], bf16)
        slots = sb("slots", [P, E, EJ, NV])
        slot_w = sb("slot_w", [P, E * EJ])
        slot_id = sb("slot_id", [P, E * EJ])
        slot_s = sb("slot_s", [P, E * EJ], i32)
        slot_g = sb("slot_g", [P, E * EJ], i32)
        k_flat = kT[:, :, :].rearrange("p k t -> p (k t)")
        q_flat = qT[:, :, :].rearrange("p k t -> p (k t)")
        n_e = EJ * HD
        ek = KH * T // n_e
        rows = [(k_flat if e < ek else q_flat)[:, (e % ek) * n_e:(e % ek + 1) * n_e].rearrange("p (j h) -> p j h", j=EJ)
                for e in range(E)]
        n_flat = normed[:, :, :, :].rearrange("p r c h -> p (r c h)")
        xgT = n_flat[:, 0:2 * KH * CAP].rearrange("p (r k s) -> p r k s", r=2, k=KH)
        act_d = n_flat[:, 2 * KH * CAP:2 * (KH + 1) * CAP].rearrange("p (r s) -> p r s", r=2)

        s0_ps, s1_ps, d_ps, h_ps, t_ps, g_ps, u_ps, y_ps = (
            bank(s) for s in ("s0_ps", "s1_ps", "d_ps", "h_ps", "t_ps", "g_ps", "u_ps", "y_ps"))
        qk_ps = [s_[:, 0:2 * P] for s_ in (s0_ps, s1_ps)]
        far_ps = [s_[:, 2 * P:2 * P + 2 * DA] for s_ in (s0_ps, s1_ps)]
        kv_ps = h_ps[:, NH * DA:NH * DA + 2 * DA].rearrange("p (a d) -> p a d", a=2)
        gate_ps = [g_ps, u_ps, y_ps, h_ps]
        gu_ps = [g_ps, u_ps]
        near_ps = h_ps[:, 0:NH * DA].rearrange("p (h d) -> p h d", h=NH)
        route_ps = t_ps[:, 0:NC * (E + 1)].rearrange("p (c e) -> p c e", c=NC)
        csum_ps = t_ps[:, 64:64 + NC * E].rearrange("p (c e) -> p c e", c=NC)
        slots_ps = t_ps[:, 128:128 + E * EJ * NV]

        x2_dram = nc.dram_tensor("x2_rows", (T, HD), fp32, kind="Internal").ap()
        x_v = A["x"].rearrange("p (b c) h -> b p c h", c=NC)
        v_v = A["ctx"].rearrange("p (b c) (h d) -> b p (c h) d", c=NC, h=NH)
        kT_v = A["ctxT"].rearrange("(k p) (b s) -> b p k s", p=P, s=SEQ)
        x2_v = x2_dram.rearrange("(p b c) h -> b p c h", c=NC, b=B)
        out_v = out.rearrange("p (b c) h -> b p c h", c=NC)
        out_rows = out.rearrange("p n h -> (p n) h")

        x_in = [sem(f"x_in{b}") for b in range(B)]
        k_in = sem("k_in")
        v_in = sem("v_in")
        small_in = sem("small_in")
        w_sh_in = sem("w_sh_in")
        w_dyn_in = sem("w_dyn_in")
        pool_step, dve_step, act_step = sem("pool_step"), sem("dve_step"), sem("act_step")
        consts_ready = sem("consts_ready")
        masks_ready = sem("masks_ready")
        ones_ready = sem("ones_ready")
        tanh_ready = sem("tanh_ready")
        gate_w_ready = sem("gate_w_ready")
        var1_ready, rstd1_ready = sem("var1_ready"), sem("rstd1_ready")
        q_ready = sem("q_ready")
        qT_psum, qT_act, qT_dve = sem("qT_psum"), sem("qT_act"), sem("qT_dve")
        gates_psum, gf_ready, gi_ready = sem("gates_psum"), sem("gf_ready"), sem("gi_ready")
        softplus_ready = sem("softplus_ready")
        mrow_ready, exps_ready = sem("mrow_ready"), sem("exps_ready")
        drows_ready = sem("drows_ready")
        decsel_ready = sem("decsel_ready")
        cols_psum, cols_ready = sem("cols_psum"), sem("cols_ready")
        d_psum, dexp_ready = sem("d_psum"), sem("dexp_ready")
        scores_psum = sem("scores_psum")
        c_ready, far_ready, near_psum = sem("c_ready"), sem("far_ready"), sem("near_psum")
        uv_ready, state_ready, heads_ready = sem("uv_ready"), sem("state_ready"), sem("heads_ready")
        hvar_ready, hrstd_ready, z_ready, x1_ready = (
            sem("hvar_ready"), sem("hrstd_ready"), sem("z_ready"), sem("x1_ready"))
        hscale_ready, scale2_ready = sem("hscale_ready"), sem("scale2_ready")
        var2_ready, rstd2_ready, x2_ready = sem("var2_ready"), sem("rstd2_ready"), sem("x2_ready")
        x2T_psum, x2T_ready = sem("x2T_psum"), sem("x2T_ready")
        route_psum, route_read = sem("route_psum"), sem("route_read")
        lsh_ready, ex_ready = sem("lsh_ready"), sem("ex_ready")
        valid_ready, csum_psum, csum_read = sem("valid_ready"), sem("csum_psum"), sem("csum_read")
        t9_ready, e9_ready = sem("t9_ready"), sem("e9_ready")
        pk_ready, val_ready = sem("pk_ready"), sem("val_ready")
        onehot_ready, onehot_pool, slots_psum, slots_read = sem("onehot_ready"), sem("onehot_pool"), sem("slots_psum"), sem("slots_read")
        gu_psum, sig_ready, act_ready = sem("gu_psum"), sem("sig_ready"), sem("act_ready")
        y_psum, o_ready = sem("y_psum"), sem("o_ready")
        x2_stored = [sem(f"x2_stored{b}") for b in range(B)]
        o_stored = [sem(f"o_stored{b}") for b in range(B)]
        slots_ready = sem("slots_ready")
        gathered = [sem(f"gathered{e}") for e in range(E)]
        xgT_psum, xgT_ready = sem("xgT_psum"), sem("xgT_ready")
        dg_psum, du_psum, dsig_ready, dact_ready = (
            sem("dg_psum"), sem("du_psum"), sem("dsig_ready"), sem("dact_ready"))
        dy_psum, ys_ready = sem("dy_psum"), sem("ys_ready")
        added = sem("added")

        block = ctx.enter_context(nc.Block())

        @block.sync
        def _(sp):
            for b in range(B):
                sp.dma_start(xs[:, b * NC:(b + 1) * NC, :], x_v[b]).then_inc(x_in[b], 16)
                sp.dma_start(kT[:, :, b * SEQ:(b + 1) * SEQ], kT_v[b]).then_inc(k_in, 16)
            for b in range(B):
                sp.dma_start(v_aug[:, b * NC:(b + 1) * NC, :, 0:DH].rearrange("p c h d -> p (c h) d"),
                             v_v[b]).then_inc(v_in, 16)
            sp.dma_start(wgu_sh[:, :, :, :], A["wgu_sh"]).then_inc(w_sh_in, 16)
            sp.dma_start(wd_sh[:, :, :], A["wd_sh"]).then_inc(w_sh_in, 16)
            sp.dma_start(wgu_dyn[:, :, :, :, :], A["wgu_dyn"]).then_inc(w_dyn_in, 16)
            sp.dma_start(wd_dyn[:, :, :], A["wd_dyn"]).then_inc(w_dyn_in, 16)
            for t in range(LAST + PB):
                if (b := due(t, NORM2)) is not None:
                    sp.wait_ge(x2_ready, b + 1)
                    sp.dma_start(x2_v[b], normed[:, b % 2, :, :]).then_inc(x2_stored[b], 16)
                if (b := due(t, DOWN + 2 * NC)) is not None:
                    sp.wait_ge(o_ready, NC * (b + 1))
                    sp.dma_start(out_v[b], xs[:, b * NC:(b + 1) * NC, :]).then_inc(o_stored[b], 16)
            for b in range(B):
                sp.wait_ge(x2_stored[b], 16)
                sp.wait_ge(o_stored[b], 16)
            sp.wait_ge(added, 16 * E * EJ)

        @block.gpsimd
        def _(pool):
            done = [0]

            def step(ins):
                done[0] += 1
                ins.then_inc(pool_step, 1)
                pool.wait_ge(pool_step, done[0])

            pool.memset(m_half[:, :], -0.5)
            pool.memset(ones_b[:, :], 1.0)
            pool.memset(tri_b[:, :], 1.0)
            pool.memset(causal_b[:, :, :], 0.0)
            pool.memset(tri_e[:, :, :], 1.0)
            pool.memset(row_of[:, :, :], 0.0)
            pool.memset(slots[:, :, :, :], 0.0)
            pool.memset(carry[:, :], 0.0)
            pool.memset(carry_b[:, :], 0.0)
            pool.memset(keep9[:, :, :], 1.0)
            step(pool.memset(ident[:, :], 0.0))
            pool.affine_select(out=ident[:, :], in_=ident[:, :], compare_op=ALU.not_equal, fill=1.0, base=0,
                               pattern=[[-1, P]], channel_multiplier=1)
            step(pool.affine_select(out=row_of[:, :, :], in_=row_of[:, :, :], compare_op=ALU.not_equal, fill=1.0,
                                    base=0, pattern=[[-1, NH], [-4, 32]], channel_multiplier=1))
            pool.tensor_copy(ident_b[:, :], ident[:, :])
            pool.affine_select(out=tri_b[:, :], in_=tri_b[:, :], compare_op=ALU.is_ge, fill=0.0, base=0,
                               pattern=[[1, P]], channel_multiplier=-1)
            pool.affine_select(out=causal_b[:, :, :], in_=causal_b[:, :, :], compare_op=ALU.is_ge, fill=NEG, base=0,
                               pattern=[[0, NH], [1, P]], channel_multiplier=-1)
            pool.affine_select(out=tri_e[:, :, :], in_=tri_e[:, :, :], compare_op=ALU.is_gt, fill=0.0, base=0,
                               pattern=[[1, E], [-1, E]], channel_multiplier=0)
            pool.iota(iota1[:, :], pattern=[[1, P]], base=1, channel_multiplier=0,
                      allow_small_or_imprecise_dtypes=True)
            pool.iota(val[:, :, 0:1], pattern=[[0, NT * E], [0, 1]], base=-int(EMPTY), channel_multiplier=NT,
                      allow_small_or_imprecise_dtypes=True)
            pool.iota(val[:, :, 1:2].rearrange("p (n e) v -> p n (e v)", e=E), pattern=[[1, NT], [0, E]],
                      base=0, channel_multiplier=0,
                      allow_small_or_imprecise_dtypes=True).then_inc(consts_ready, 1)

            def rsqrt(m, src, dst, ready, count, signal):
                pool.wait_ge(ready, count)
                pool.tensor_tensor(dst[:, 0:m], src[:, 0:m], m_half[:, 0:m], ALU.pow).then_inc(signal, 1)

            def scaled_v(n):
                b, c = divmod(n, NC)
                if n >= 2:
                    pool.wait_ge(near_psum, n - 1)
                pool.tensor_tensor(uv[:, n % 2, :, :], v_aug[:, n, :, :], bc(u_t[:, c, b, :], 2, DA),
                                   ALU.mult).then_inc(uv_ready, 1)

            def add_x(b, i):
                c = slice(i * NC // 2, (i + 1) * NC // 2)
                pool.wait_ge(z_ready, 2 * b + i + 1)
                if b == 0 and i == 0:
                    pool.wait_ge(tanh_ready, 1)
                z = heads[:, b % 2, c, :, 0:DH]
                xb = xs[:, b * NC:(b + 1) * NC, :].rearrange("p c (h d) -> p c h d", h=NH)[:, c, :, :]
                step(pool.tensor_tensor(z, z, bc(out_scale[:, :].rearrange("p (h d) -> p h d", h=NH), 1, NC // 2),
                                        ALU.mult))
                pool.tensor_tensor(xb, z, xb, ALU.add).then_inc(x1_ready, 1)

            def one_hots(b, c):
                pool.wait_ge(pk_ready, b + 1)
                if b >= 1:
                    pool.wait_ge(slots_psum, b)
                for m in range(c * E, (c + 1) * E):
                    last = pool.tensor_scalar(onehot[:, m, :], iota1[:, :], pk[:, m:m + 1], None, ALU.is_equal)
                last.then_inc(onehot_pool, 1)

            for b in range(B):
                rsqrt(NC, var2, rstd2, var1_ready, b + 1, rstd1_ready)
            pool.wait_ge(cols_ready, 1)
            pool.wait_ge(v_in, 16 * B)
            pool.wait_ge(ones_ready, 1)
            scaled_v(0)
            for t in range(LAST):
                if t % 2 == 1 and (t + 1) // 2 < NT:
                    scaled_v((t + 1) // 2)
                if (b := due(t, HSTATS)) is not None:
                    rsqrt(NC * NH, var_eps, rstd, hvar_ready, b + 1, hrstd_ready)
                if (u := unit(t, ADDX, 2, 1)) is not None:
                    add_x(*u)
                if (b := due(t, STATS2)) is not None:
                    rsqrt(NC, var2, rstd2, var2_ready, b + 1, rstd2_ready)
                if (b := due(t, CAPAC)) is not None:
                    one_hots(b, 2)
                if (b := due(t, CAPAC + 1)) is not None:
                    one_hots(b, 3)

            def gather(e):
                for j in range(EJ):
                    pool.indirect_dma_start(
                        out=rows[e][0:EROWS[j], j, :], out_offset=None, in_=x2_dram[:, :],
                        in_offset=bass.IndirectOffsetOnAxis(ap=slot_g[0:EROWS[j], e * EJ + j:e * EJ + j + 1], axis=0),
                        bounds_check=T - 1, oob_is_err=False).then_inc(gathered[e], 16)

            def scatter_add(e):
                pool.wait_ge(ys_ready, e + 1)
                if e >= 1:
                    pool.wait_ge(added, 16 * EJ * e)
                for j in range(EJ):
                    pool.indirect_dma_start(
                        out=out_rows, out_offset=bass.IndirectOffsetOnAxis(
                            ap=slot_s[0:EROWS[j], e * EJ + j:e * EJ + j + 1], axis=0),
                        in_=rows[e][0:EROWS[j], j, :], in_offset=None,
                        bounds_check=T - 1, oob_is_err=False, compute_op=ALU.add).then_inc(added, 16)

            pool.wait_ge(slots_ready, 1)
            for b in range(B):
                pool.wait_ge(x2_stored[b], 16)
            for e in range(AHEAD):
                gather(e)
            for b in range(B):
                pool.wait_ge(o_stored[b], 16)
            for e in range(E):
                if e + AHEAD < E:
                    gather(e + AHEAD)
                scatter_add(e)

        @block.scalar
        def _(act):
            done = [0]

            def step(ins):
                done[0] += 1
                ins.then_inc(act_step, 1)
                act.wait_ge(act_step, done[0])

            act.dma_start(w_gates[:, :, :], A["w_gates"]).then_inc(small_in, 16)
            act.dma_start(b_rows[:, :], A["b_rows"]).then_inc(small_in, 16)
            act.dma_start(g_pair[:, :], A["g_pair"].partition_broadcast(P)).then_inc(small_in, 16)
            act.dma_start(out_scale[:, :], A["out_scale"].partition_broadcast(P)).then_inc(small_in, 16)
            act.dma_start(w_route[:, :, :], A["w_route"]).then_inc(small_in, 16)
            for b in range(B):
                act.wait_ge(qT_psum, 2 * b + 1)
                act.copy(qT[:, 0, b * SEQ:(b + 1) * SEQ], s0_ps[:, :]).then_inc(qT_act, 1)
            for b in range(B):
                act.wait_ge(gates_psum, b + 1)
                act.copy(gf_row[32 * b:32 * b + 32, :], gate_ps[b][32:64, :]).then_inc(gf_ready, 1)
            act.wait_ge(gf_ready, B)
            step(act.activation(fabs[:, :], gf_row[:, :], ACT.Abs, bias=b_rows[:, 1:2]))
            step(act.activation(fexp[:, :], fabs[:, :], ACT.Exp, scale=-1.0))
            act.activation(fabs[:, :], fexp[:, :], ACT.Ln, bias=1.0).then_inc(softplus_ready, 1)
            act.wait_ge(mrow_ready, 1)
            act.activation(n_row[:, :], mld[:, :], ACT.Exp, scale=-1.0)
            act.activation(dec_row[:, 1:NC], dec_row[:, 1:NC], ACT.Exp)
            for c in range(NC):
                s = slice(c * P, (c + 1) * P)
                if c >= 1:
                    act.activation(w_row[:, s], negm[:, s], ACT.Exp, bias=m_row[:, c * P - 1:c * P])
                last = act.activation(u_row[:, s], a_row[:, s], ACT.Exp, bias=negm[:, (c + 1) * P - 1:(c + 1) * P])
            last.then_inc(exps_ready, 1)
            act.wait_ge(small_in, 16 * 5)
            act.activation(tanh_g[:, :], g_pair[:, :], ACT.Tanh).then_inc(tanh_ready, 1)

            def decay(n):
                act.wait_ge(d_psum, n + 1)
                if n >= 2:
                    act.wait_ge(c_ready, n - 1)
                act.activation(dexp[:, n % 2, :], d_ps[:, :], ACT.Exp).then_inc(dexp_ready, 1)

            def norm_heads(b, i):
                hb = heads[:, b % 2, :, :, :].rearrange("p c h d -> p (c h) d")
                act.wait_ge(hscale_ready, b + 1)
                for g in range(i * NC * NH // 2, (i + 1) * NC * NH // 2):
                    last = act.activation(hb[:, g, 0:DH], hb[:, g, 0:DH], ACT.Identity, scale=hscale[:, g:g + 1],
                                          bias=hshift[:, g:g + 1])
                last.then_inc(z_ready, 1)

            def norm_rows(b):
                act.wait_ge(scale2_ready, b + 1)
                if b >= 2:
                    act.wait_ge(x2_stored[b - 2], 16)
                    act.wait_ge(x2T_psum, KH * (b - 1))
                for c in range(NC):
                    last = act.activation(normed[:, b % 2, c, :], xs[:, b * NC + c, :], ACT.Identity,
                                          scale=scale2[:, c:c + 1], bias=shift2[:, c:c + 1])
                last.then_inc(x2_ready, 1)

            def copy_x2T(b, k):
                act.wait_ge(x2T_psum, KH * b + k + 1)
                act.copy(x2T[:, k, b * SEQ:(b + 1) * SEQ], t_ps[:, :]).then_inc(x2T_ready, 1)

            def copy_route(b):
                act.wait_ge(route_psum, b + 1)
                if b >= 2:
                    act.wait_ge(t9_ready, b - 1)
                act.copy(logit[:, b % 2, :, :], route_ps).then_inc(route_read, 1)

            def gate_sigmoid(b, i):
                m = NG * b + i
                act.wait_ge(gu_psum, m + 1)
                if m >= 2:
                    act.wait_ge(act_ready, m - 1)
                act.activation(sig[:, m % 2, 0:HS], gu_ps[m % 2][:, 0:HS], ACT.Tanh, scale=0.5).then_inc(sig_ready, 1)

            for t in range(LAST):
                if t % 2 == 0 and t // 2 < NT:
                    decay(t // 2)
                if (u := unit(t - 1, GATEUP, NG, 1)) is not None:
                    gate_sigmoid(*u)
                if (u := unit(t, HNORM, 2, 1)) is not None:
                    norm_heads(*u)
                if (b := due(t, NORM2)) is not None:
                    norm_rows(b)
                if (u := unit(t, X2T, KH, 1)) is not None:
                    copy_x2T(*u)
                if (b := due(t, ROUTE)) is not None:
                    copy_route(b)
                if (b := due(t, CHOOSE)) is not None:
                    act.wait_ge(lsh_ready, b + 1)
                    act.activation(ex[:, :, :], lsh[:, :, :], ACT.Exp).then_inc(ex_ready, 1)
                if (b := due(t, CAPAC)) is not None:
                    act.wait_ge(t9_ready, b + 1)
                    act.activation(e9[:, :, :], t9[:, :, :], ACT.Exp).then_inc(e9_ready, 1)

            def copy_xgT(e):
                act.wait_ge(xgT_psum, e + 1)
                if e >= 2:
                    act.wait_ge(du_psum, e - 1)
                act.copy(xgT[:, e % 2, 0, :], s0_ps[:, 0:CAP])
                act.copy(xgT[:, e % 2, 1, :], d_ps[:, 0:CAP]).then_inc(xgT_ready, 1)

            def weigh(e):
                act.wait_ge(dy_psum, e + 1)
                for j in range(EJ):
                    src = y_ps[:, j * HD:(j + 1) * HD] if j < 2 else t_ps[0:EROWS[2], 0:HD]
                    last = act.activation(rows[e][0:EROWS[j], j, :], src, ACT.Copy,
                                          scale=slot_w[0:EROWS[j], e * EJ + j:e * EJ + j + 1])
                last.then_inc(ys_ready, 1)

            for e in range(E + 1):
                if e < E:
                    copy_xgT(e)
                    act.wait_ge(dg_psum, e + 1)
                    if e >= 2:
                        act.wait_ge(dact_ready, e - 1)
                    act.activation(sig[:, e % 2, 0:CAP], g_ps[:, 0:CAP], ACT.Tanh, scale=0.5).then_inc(dsig_ready, 1)
                if e >= 1:
                    weigh(e - 1)

        @block.tensor
        def _(pe):
            pe.wait_ge(consts_ready, 1)
            pe.wait_ge(gate_w_ready, 1)
            pe.wait_ge(k_in, 16 * B)

            def gates_k(b):
                for m in range(KH):
                    pe.matmul(gate_ps[b][0:64, :], w_rows[:, KH + m, :, :, :].rearrange("p q j h -> p (q j h)"),
                              kT[:, m, b * SEQ:(b + 1) * SEQ], start=(m == 0), stop=False)

            for b in range(B):
                gates_k(b)
                pe.wait_ge(q_ready, b + 1)
                for k, dst in ((0, s0_ps), (1, d_ps)):
                    if b >= 1:
                        pe.wait_ge(qT_act if k == 0 else qT_dve, b)
                    for c in range(NC):
                        last = pe.transpose(dst[:, c * P:(c + 1) * P], normed[:, b % 2, c, k * P:(k + 1) * P],
                                            ident[:, :])
                    last.then_inc(qT_psum, 1)
            for b in range(B):
                pe.wait_ge(qT_act, b + 1)
                pe.wait_ge(qT_dve, b + 1)
                for m in range(KH):
                    last = pe.matmul(gate_ps[b][0:64, :], w_rows[:, m, :, :, :].rearrange("p q j h -> p (q j h)"),
                                     qT[:, m, b * SEQ:(b + 1) * SEQ], start=False, stop=(m == KH - 1))
                last.then_inc(gates_psum, 1)
            pe.wait_ge(exps_ready, 1)
            for row, dst, c0 in ((u_row, s0_ps, 0), (w_row, d_ps, 1), (n_row, h_ps, 0)):
                for c in range(c0, NC):
                    pe.transpose(dst[:, c * P:(c + 1) * P], row[:, c * P:(c + 1) * P], ident[:, :])
            pe.wait_ge(decsel_ready, 1)
            pe.matmul(y_ps[:, 0:B * 2 * NC], par_sel[:, :], dec_sel[:, :, :, :].rearrange("p b a c -> p (b a c)"),
                      start=True, stop=True).then_inc(cols_psum, 1)
            pe.wait_ge(drows_ready, 1)
            pe.wait_ge(cols_ready, 1)
            pe.wait_ge(v_in, 16 * B)
            pe.wait_ge(ones_ready, 1)

            def scores(n):
                b, c = divmod(n, NC)
                tok = slice(n * P, (n + 1) * P)
                r = slice(32 * b, 32 * b + 32)
                if n >= 1:
                    pe.wait_ge(dexp_ready, n)
                pe.matmul(d_ps[:, :], dl[r, c * P:(c + 1) * P], dr[r, c, :, :].rearrange("p h s -> p (h s)"),
                          start=True, stop=False)
                pe.matmul(d_ps[:, :], ident_b[:, :], causal_b[:, :, :].rearrange("p h s -> p (h s)"),
                          start=False, stop=True).then_inc(d_psum, 1)
                if n >= 1:
                    pe.wait_ge(far_ready, n)
                for h in range(NH):
                    g = slice(DH * (h % 2), DH * (h % 2) + DH)
                    i = h // 2
                    last = pe.matmul(qk_ps[h % 2][:, i * P:(i + 1) * P], kT[g, i, tok], qT[g, i, tok],
                                     start=True, stop=True)
                if c > 0:
                    pe.wait_ge(state_ready, n)
                    for i in range(2):
                        last = pe.matmul(far_ps[i], qT[:, i, tok], state[:, (n - 1) % 2, i, :], start=True, stop=True)
                last.then_inc(scores_psum, 1)

            def near(n):
                if n >= 0:
                    pe.wait_ge(c_ready, n + 1)
                    pe.wait_ge(state_ready, n + 1)
                if n >= 1:
                    pe.wait_ge(heads_ready, n)
                for h in range(NH if n >= 0 else 0):
                    last = pe.matmul(near_ps[:, h, :], cmat[:, n % 2, order(h) * P:(order(h) + 1) * P],
                                     v_aug[:, n, h, :], start=True, stop=True)
                if n + 1 < NT:
                    pe.wait_ge(uv_ready, n + 2)
                    for h in range(NH):
                        g = slice(DH * (h % 2), DH * (h % 2) + DH)
                        last = pe.matmul(kv_ps[g, h // 2, :], v_aug[:, n + 1, h, 0:DH], uv[:, (n + 1) % 2, h, :],
                                         start=True, stop=True)
                last.then_inc(near_psum, 1)

            def transpose_x2(b, k):
                pe.wait_ge(x2_ready, b + 1)
                if b >= 1:
                    pe.wait_ge(slots_read, b)
                if k >= 1:
                    pe.wait_ge(x2T_ready, KH * b + k)
                for c in range(NC):
                    last = pe.transpose(t_ps[:, c * P:(c + 1) * P], normed[:, b % 2, c, k * P:(k + 1) * P],
                                        ident[:, :])
                last.then_inc(x2T_psum, 1)

            def route(b):
                pe.wait_ge(x2T_ready, KH * (b + 1))
                for c in range(NC):
                    s = slice((b * NC + c) * P, (b * NC + c + 1) * P)
                    for k in range(KH):
                        last = pe.matmul(route_ps[:, c, :], x2T[:, k, s], w_route[:, k, :],
                                         start=(k == 0), stop=(k == KH - 1))
                last.then_inc(route_psum, 1)

            def count(b):
                pe.wait_ge(valid_ready, b + 1)
                pe.wait_ge(route_read, b + 1)
                pe.matmul(csum_ps, ones_b[:, :], bc(carry_b[:, :], 1, NC), start=True, stop=False)
                for k in range(1, NC):
                    pe.matmul(csum_ps[:, k:NC, :], ones_b[:, :], valid_b[:, 0:NC - k, :], start=False, stop=False)
                pe.matmul(csum_ps, tri_b[:, :], valid_b[:, :, :], start=False, stop=True).then_inc(csum_psum, 1)

            def list_slots(b):
                pe.wait_ge(onehot_ready, 2 * (b + 1))
                pe.wait_ge(onehot_pool, 2 * (b + 1))
                pe.wait_ge(val_ready, EJ * (b + 1))
                pe.wait_ge(csum_read, b + 1)
                for e in range(E):
                    for c in range(NC):
                        m = c * E + e
                        last = pe.matmul(slots_ps[:, e * EJ * NV:(e + 1) * EJ * NV], onehot[:, m, :],
                                         val_j[:, m, :, :].rearrange("p j v -> p (j v)"),
                                         start=(c == 0), stop=(c == NC - 1))
                last.then_inc(slots_psum, 1)

            def gate_up(b, i):
                m = NG * b + i
                s = slice(b * SEQ + (i // IC) * HS, b * SEQ + (i // IC + 1) * HS)
                w_i = slice((i % IC) * P, (i % IC + 1) * P)
                pe.wait_ge(x2T_ready, KH * (b + 1))
                if m == 0:
                    pe.wait_ge(w_sh_in, 32)
                if m >= 2:
                    pe.wait_ge(act_ready, m - 1)
                for w in range(2):
                    for k in range(KH):
                        last = pe.matmul(gu_ps[m % 2][:, w * HS:(w + 1) * HS], wgu_sh[:, w, k, w_i],
                                         x2T[:, k, s], start=(k == 0), stop=(k == KH - 1))
                last.then_inc(gu_psum, 1)

            def down(b, c):
                pe.wait_ge(act_ready, NG * b + IC * (c // (NC // 2) + 1))
                if b * NC + c >= 1:
                    pe.wait_ge(o_ready, b * NC + c)
                for i in range(IC):
                    last = pe.matmul(y_ps[:, 0:HD], act_sh[:, b % 2, i, c * P:(c + 1) * P], wd_sh[:, i, :],
                                     start=(i == 0), stop=(i == IC - 1))
                last.then_inc(y_psum, 1)

            for t in range(LAST):
                n = t // 2
                if t % 2 == 0 and n < NT:
                    scores(n)
                if t % 2 == 1 and n <= NT:
                    near(n - 1)
                if (u := unit(t, GATEUP, NG, 1)) is not None:
                    gate_up(*u)
                if (u := unit(t, DOWN, NC, 2)) is not None:
                    down(*u)
                if (b := due(t, COUNT)) is not None:
                    count(b)
                if (b := due(t, LISTS)) is not None:
                    list_slots(b)
                if (u := unit(t, X2T, KH, 1)) is not None:
                    transpose_x2(*u)
                if (b := due(t, ROUTE)) is not None:
                    route(b)

            def spread(e):
                pe.wait_ge(gathered[e], 16 * EJ)
                if e >= 1:
                    pe.wait_ge(xgT_ready, e)
                for k, dst in ((0, s0_ps), (1, d_ps)):
                    for t in range(EJ):
                        m = EROWS[t]
                        last = pe.transpose(dst[:, t * P:t * P + m], rows[e][0:m, t, k * P:(k + 1) * P],
                                            ident[0:m, 0:m])
                last.then_inc(xgT_psum, 1)

            def expert_gate_up(e):
                pe.wait_ge(xgT_ready, e + 1)
                if e >= 1:
                    pe.wait_ge(dact_ready, e)
                for w, dst, signal in ((0, g_ps, dg_psum), (1, u_ps, du_psum)):
                    for k in range(KH):
                        last = pe.matmul(dst[:, 0:CAP], wgu_dyn[:, w, e, k, :], xgT[:, e % 2, k, :],
                                         start=(k == 0), stop=(k == KH - 1))
                    last.then_inc(signal, 1)

            def expert_down(e):
                pe.wait_ge(dact_ready, e + 1)
                if e >= 1:
                    pe.wait_ge(ys_ready, e)
                for t in range(EJ):
                    m = EROWS[t]
                    dst = y_ps[:, t * HD:(t + 1) * HD] if t < 2 else t_ps[0:m, 0:HD]
                    last = pe.matmul(dst, act_d[:, e % 2, t * P:t * P + m], wd_dyn[:, e, :], start=True, stop=True)
                last.then_inc(dy_psum, 1)

            pe.wait_ge(w_dyn_in, 32)
            pe.wait_ge(o_ready, NT)
            pe.wait_ge(slots_read, B)
            spread(0)
            for e in range(E):
                expert_gate_up(e)
                if e + 1 < E:
                    spread(e + 1)
                expert_down(e)

        @block.vector
        def _(dve):
            done = [0]

            def step(ins):
                done[0] += 1
                ins.then_inc(dve_step, 1)
                dve.wait_ge(dve_step, done[0])

            def variance(m, width, eps, mean=mean):
                dve.tensor_tensor(st_s[:, 0:m], st[:, 0:m, 1], st[:, 0:m, 4], ALU.add)
                dve.tensor_tensor(st_v[:, 0:m], st[:, 0:m, 2], st[:, 0:m, 5], ALU.add)
                step(dve.tensor_tensor(st_d[:, 0:m], st[:, 0:m, 1], st[:, 0:m, 4], ALU.subtract))
                dve.tensor_scalar(mean[:, 0:m], st_s[:, 0:m], 0.5, None, ALU.mult)
                dve.tensor_scalar(st_v[:, 0:m], st_v[:, 0:m], 1.0 / width, eps, ALU.mult, ALU.add)
                step(dve.scalar_tensor_tensor(out=st_d2[:, 0:m], in0=st_d[:, 0:m], scalar=0.25, in1=st_d[:, 0:m],
                                              op0=ALU.mult, op1=ALU.mult))

            dve.memset(v_aug[:, :, :, DH:DA].rearrange("p n h d -> p (n h d)"), 1.0).then_inc(ones_ready, 1)
            dve.memset(state[:, :, :, :].rearrange("p r i d -> p (r i d)"), 0.0)
            dve.wait_ge(small_in, 16 * 5)
            for m in range(KH):
                for q in range(2):
                    wq, wk, wv = (bc(w_gates[:, m + KH * i, q * NH:(q + 1) * NH], 1, 8) for i in range(3))
                    dve.tensor_copy(w_rows[:, m, q, :, :], wq)
                    last = dve.tensor_tensor(w_rows[:, KH + m, q, :, :], wk, wv, ALU.add)
            last.then_inc(gate_w_ready, 1)
            for b in range(B):
                dve.wait_ge(x_in[b], 16)
                for c in range(NC):
                    last = dve.bn_stats(st[:, c, :], xs[:, b * NC + c, :])
                step(last)
                variance(NC, HD, 1e-5, mean2)
                dve.tensor_tensor(var2[:, :], st_v[:, 0:NC], st_d2[:, 0:NC], ALU.add).then_inc(var1_ready, 1)
                dve.wait_ge(rstd1_ready, b + 1)
                if b >= 2:
                    dve.wait_ge(qT_psum, KH * (b - 1))
                for c in range(NC):
                    last = dve.tensor_scalar(normed[:, b % 2, c, :], xs[:, b * NC + c, :], mean2[:, c:c + 1],
                                             rstd2[:, c:c + 1], ALU.subtract, ALU.mult)
                last.then_inc(q_ready, 1)
                dve.wait_ge(qT_psum, KH * b + 2)
                dve.tensor_copy(qT[:, 1, b * SEQ:(b + 1) * SEQ], d_ps[:, :]).then_inc(qT_dve, 1)
            dve.wait_ge(consts_ready, 1)
            dve.tensor_reduce(head_of[:, :], row_of[:, :, :], AX.X, ALU.add)
            dve.tensor_reduce(pair_row[:, :, :].rearrange("p b a -> p (b a)"),
                              row_of[:, :, :].rearrange("p (a r) (b j) -> p b j a r", a=2, j=8)[:, :, 0, :, :],
                              AX.X, ALU.add)
            step(dve.tensor_reduce(rep_of[:, :], row_of[:, :, :].rearrange("p h (b j) -> p j b h", j=8), AX.XY, ALU.add))
            dve.tensor_tensor(is_a[:, :], rep_of[:, 0:1], rep_of[:, 1:2], ALU.add)
            dve.tensor_tensor(is_m[:, :], rep_of[:, 2:3], rep_of[:, 3:4], ALU.add)
            dve.tensor_tensor(is_hi[:, :], rep_of[:, 0:1], rep_of[:, 2:3], ALU.add)
            dve.tensor_tensor(is_lo[:, :], rep_of[:, 1:2], rep_of[:, 3:4], ALU.add)
            step(dve.tensor_tensor(parity[:, :], head_of[:, 0:2], head_of[:, 2:4], ALU.add))
            for a in range(2):
                dve.tensor_copy(par_sel[:, a * DH:(a + 1) * DH], parity[:, a:a + 1].to_broadcast([P, DH]))
            for b in range(B):
                dve.wait_ge(gf_ready, b + 1)
                dve.tensor_copy(gi_row[32 * b:32 * b + 32, :], gate_ps[b][0:32, :]).then_inc(gi_ready, 1)
            dve.wait_ge(gi_ready, B)
            step(dve.tensor_scalar(fmin[:, :], gf_row[:, :], b_rows[:, 1:2], 0.0, ALU.add, ALU.min))
            dve.wait_ge(softplus_ready, 1)
            dve.memset(ones_row[:, :], 1.0)
            step(dve.tensor_tensor(fmin[:, :], fmin[:, :], fabs[:, :], ALU.subtract))
            step(dve.tensor_tensor_scan(cs[:, :], ones_row[:, :], fmin[:, :], 0.0, ALU.mult, ALU.add))
            step(dve.scalar_tensor_tensor(out=a_row[:, :], in0=gi_row[:, :], scalar=b_rows[:, 0:1], in1=cs[:, :],
                                          op0=ALU.add, op1=ALU.subtract))
            step(dve.tensor_tensor_scan(m_row[:, :], ones_row[:, :], a_row[:, :], -3.0e38, ALU.mult, ALU.max))
            dve.tensor_tensor(dec_row[:, 1:NC], m_row[:, P - 1:(NC - 1) * P:P], m_row[:, 2 * P - 1:NC * P:P],
                              ALU.subtract)
            dve.tensor_tensor(mld[:, :], cs[:, :], m_row[:, :], ALU.add)
            dve.tensor_scalar(negm[:, :], m_row[:, :], -1.0, None, ALU.mult).then_inc(mrow_ready, 1)
            dve.wait_ge(mrow_ready, 1)
            step(dve.tensor_scalar(av[:, :], a_row[:, :], is_a[:, :], None, ALU.mult))
            step(dve.scalar_tensor_tensor(out=av[:, :], in0=negm[:, :], scalar=is_m[:, :], in1=av[:, :],
                                          op0=ALU.mult, op1=ALU.add))
            step(dve.tensor_copy(av_hi[:, :], av[:, :]))
            step(dve.tensor_tensor(av_lo[:, :], av[:, :], av_hi[:, :].bitcast(fp32), ALU.subtract))
            step(dve.tensor_scalar(av[:, :], av_hi[:, :].bitcast(fp32), is_hi[:, :], None, ALU.mult))
            step(dve.scalar_tensor_tensor(out=av[:, :], in0=av_lo[:, :], scalar=is_lo[:, :], in1=av[:, :],
                                          op0=ALU.mult, op1=ALU.add))
            dve.tensor_scalar(dl[:, :], av[:, :], is_a[:, :], is_m[:, :], ALU.mult, ALU.add)
            step(dve.tensor_scalar(av_lo[:, :], av[:, :], is_m[:, :], is_a[:, :], ALU.mult, ALU.add))
            for h in range(NH):
                last = dve.tensor_scalar(dr[:, :, order(h), :], av_lo[:, :].rearrange("p (c s) -> p c s", c=NC),
                                         head_of[:, h:h + 1], None, ALU.mult)
            last.then_inc(drows_ready, 1)
            dve.wait_ge(exps_ready, 1)
            step(dve.memset(dec_row[:, 0:1], 0.0))
            dve.tensor_tensor(dec_sel[:, :, :, :].rearrange("p b a c -> p (b a) c"),
                              bc(pair_row[:, :, :].rearrange("p b a -> p (b a)"), 2, NC),
                              bc(dec_row[:, :], 1, 2 * B), ALU.mult).then_inc(decsel_ready, 1)
            dve.wait_ge(cols_psum, 1)
            for dst, src, c0 in ((u_t, s0_ps, 0), (w_t, d_ps, 1), (n_t, h_ps, 0)):
                dve.tensor_copy(dst[:, c0:NC, :, :],
                                src[:, :].rearrange("p (c b r) -> p c b r", c=NC, b=B)[:, c0:NC, :, 0:NH])
            dve.tensor_copy(dec_t[:, :, :, :].rearrange("p b a c -> p (b a c)"),
                            y_ps[:, 0:B * 2 * NC]).then_inc(cols_ready, 1)
            dve.wait_ge(cols_ready, 1)
            dve.wait_ge(tanh_ready, 1)
            dve.tensor_scalar(half_gf[:, :], tanh_g[:, 1:2], 0.5, None, ALU.mult)
            step(dve.tensor_scalar(out_scale[:, :], out_scale[:, :], tanh_g[:, 0:1], None, ALU.mult))

            def decay_scores(n):
                b, c = divmod(n, NC)
                dve.wait_ge(scores_psum, n + 1)
                dve.wait_ge(dexp_ready, n + 1)
                if n >= 2:
                    dve.wait_ge(near_psum, n)
                for a in range(2):
                    m = slice(a * 2 * P, (a + 1) * 2 * P)
                    last = dve.scalar_tensor_tensor(out=cmat[:, n % 2, m], in0=qk_ps[a], scalar=QSCALE,
                                                    in1=dexp[:, n % 2, m], op0=ALU.mult, op1=ALU.mult)
                last.then_inc(c_ready, 1)
                if c > 0:
                    for i in range(2):
                        last = dve.tensor_tensor(far[:, n % 2, 2 * i:2 * i + 2, :],
                                                 far_ps[i].rearrange("p (h d) -> p h d", h=2),
                                                 bc(w_t[:, c, b, 2 * i:2 * i + 2], 2, DA), ALU.mult)
                    last.then_inc(far_ready, 1)
                else:
                    dve.memset(far[:, n % 2, :, :], 0.0).then_inc(far_ready, 1)

            def new_state(n):
                b, c = divmod(n, NC)
                dve.wait_ge(near_psum, n + 1)
                if n >= 2:
                    dve.wait_ge(scores_psum, n)
                if c == 0 or c == NC - 1:
                    for a in range(2):
                        g, d = slice(DH * a, DH * a + DH), slice(DA * a, DA * a + DA)
                        last = dve.tensor_copy(state[g, n % 2, :, d], kv_ps[g, :, :])
                    last.then_inc(state_ready, 1)
                else:
                    dve.wait_ge(state_ready, n)
                    for i in range(2):
                        for a in range(2):
                            g, d = slice(DH * a, DH * a + DH), slice(DA * a, DA * a + DA)
                            last = dve.scalar_tensor_tensor(
                                out=state[g, n % 2, i, d], in0=state[g, (n - 1) % 2, i, d],
                                scalar=dec_t[g, b, i, c:c + 1], in1=kv_ps[g, i, :], op0=ALU.mult, op1=ALU.add)
                    last.then_inc(state_ready, 1)

            def join(n):
                b, c = divmod(n, NC)
                dve.wait_ge(near_psum, n + 2)
                dve.wait_ge(far_ready, n + 1)
                if b >= 2 and c == 0:
                    dve.wait_ge(x1_ready, 2 * (b - 1))
                dve.scalar_tensor_tensor(
                    out=heads[:, b % 2, c, :, :].rearrange("p h d -> p (h d)"),
                    in0=far[:, n % 2, :, :].rearrange("p h d -> p (h d)"), scalar=QSCALE,
                    in1=h_ps[:, 0:NH * DA], op0=ALU.mult, op1=ALU.add).then_inc(heads_ready, 1)
                dve.wait_ge(heads_ready, n + 1)

            def head_stats(b):
                hb = heads[:, b % 2, :, :, :].rearrange("p c h d -> p (c h) d")
                for g in range(NC * NH):
                    last = dve.bn_stats(st[:, g, :], hb[:, g, 0:DH])
                step(last)
                m = NC * NH
                variance(m, DH, 0.0)
                step(dve.tensor_tensor(st_v[:, :], st_v[:, :], st_d2[:, :], ALU.add))
                step(dve.scalar_tensor_tensor(out=den[:, :], in0=hb[:, :, DH], scalar=-1.0, in1=hb[:, :, DH],
                                              op0=ALU.mult, op1=ALU.max))
                step(dve.tensor_tensor(den[:, :].rearrange("p (c h) -> p c h", c=NC),
                                       den[:, :].rearrange("p (c h) -> p c h", c=NC), n_t[:, :, b, :], ALU.max))
                step(dve.tensor_scalar(den[:, :], den[:, :], 1e-6, None, ALU.add))
                step(dve.reciprocal(rden[:, :], den[:, :]))
                step(dve.tensor_tensor(rden2[:, :], rden[:, :], rden[:, :], ALU.mult))
                step(dve.tensor_tensor(st_v[:, :], st_v[:, :], rden2[:, :], ALU.mult))
                dve.tensor_scalar(var_eps[:, :], st_v[:, :], 1e-6, None, ALU.add).then_inc(hvar_ready, 1)

            def head_norm(b):
                dve.wait_ge(hrstd_ready, b + 1)
                if b >= 1:
                    dve.wait_ge(z_ready, 2 * b)
                step(dve.tensor_tensor(hscale[:, :], rstd[:, :], rden[:, :], ALU.mult))
                dve.scalar_tensor_tensor(out=hshift[:, :], in0=mean[:, :], scalar=-1.0, in1=hscale[:, :],
                                         op0=ALU.mult, op1=ALU.mult).then_inc(hscale_ready, 1)

            def norm2_stats(b):
                dve.wait_ge(x1_ready, 2 * (b + 1))
                for c in range(NC):
                    last = dve.bn_stats(st[:, c, :], xs[:, b * NC + c, :])
                step(last)
                variance(NC, HD, 1e-5, mean2)
                dve.tensor_tensor(var2[:, :], st_v[:, 0:NC], st_d2[:, 0:NC], ALU.add).then_inc(var2_ready, 1)

            def norm2(b):
                dve.wait_ge(rstd2_ready, b + 1)
                if b >= 1:
                    dve.wait_ge(x2_ready, b)
                dve.tensor_copy(scale2[:, :], rstd2[:, :])
                dve.scalar_tensor_tensor(out=shift2[:, :], in0=mean2[:, :], scalar=-1.0, in1=rstd2[:, :],
                                         op0=ALU.mult, op1=ALU.mult).then_inc(scale2_ready, 1)

            def choose(b):
                lg = logit[:, b % 2, :, 0:E]
                pq = "p (c i) j -> p c i j"
                dve.wait_ge(route_read, b + 1)
                dve.scalar_tensor_tensor(out=labs[:, :, :], in0=lg, scalar=-1.0, in1=lg, op0=ALU.mult, op1=ALU.max)
                step(dve.tensor_reduce(lmax[:, :], lg, AX.X, ALU.max))
                dve.tensor_tensor(lsh[:, :, :], lg, bc(lmax[:, :], 2, E), ALU.subtract).then_inc(lsh_ready, 1)
                li, lj = bc(lg, 3, E), bc(lg, 2, E)
                pd4, pm4 = (t[:, :, :].rearrange(pq, c=NC) for t in (pd, pm))
                dve.tensor_tensor(pd4, lj, li, ALU.subtract)
                step(dve.tensor_tensor(pm4, bc(labs[:, :, :], 2, E), bc(labs[:, :, :], 3, E), ALU.max))
                flat = "p m j -> p (m j)"
                tri = bc(tri_e[:, :, :].rearrange("p i j -> p (i j)"), 1, NC)
                f4 = "p (c i) j -> p c (i j)"
                step(dve.scalar_tensor_tensor(out=pe_[:, :, :].rearrange(f4, c=NC), in0=pd[:, :, :].rearrange(f4, c=NC),
                                              scalar=0.0, in1=tri, op0=ALU.is_equal, op1=ALU.mult))
                step(dve.scalar_tensor_tensor(out=pb[:, :, :].rearrange(flat), in0=pd[:, :, :].rearrange(flat), scalar=0.0,
                                              in1=pe_[:, :, :].rearrange(flat), op0=ALU.is_gt, op1=ALU.add))
                step(dve.scalar_tensor_tensor(out=pm[:, :, :].rearrange(flat), in0=pm[:, :, :].rearrange(flat), scalar=0.2,
                                              in1=pd[:, :, :].rearrange(flat), op0=ALU.mult, op1=ALU.add))
                step(dve.scalar_tensor_tensor(out=pm[:, :, :].rearrange(flat), in0=pm[:, :, :].rearrange(flat), scalar=0.0,
                                              in1=pb[:, :, :].rearrange(flat), op0=ALU.is_ge, op1=ALU.is_gt))
                dve.tensor_reduce(rank[:, :, :].rearrange("p c e -> p (c e)"), pb[:, :, :], AX.X, ALU.add)

            def pick(b):
                pc4, pb4, pm4 = (t[:, :, :].rearrange("p (c i) j -> p c i j", c=NC) for t in (pc, pb, pm))
                dve.wait_ge(ex_ready, b + 1)
                ej = bc(ex[:, :, :], 2, E)
                dve.tensor_tensor(pc4, pb4, ej, ALU.mult)
                step(dve.tensor_tensor(pm4, pm4, ej, ALU.mult))
                dve.tensor_reduce(before[:, :, :].rearrange("p c e -> p (c e)"), pc[:, :, :], AX.X, ALU.add)
                dve.tensor_reduce(mden[:, :, :].rearrange("p c e -> p (c e)"), pm[:, :, :], AX.X, ALU.add)
                step(dve.tensor_reduce(tot75[:, :], ex[:, :, :], AX.X, ALU.add))
                step(dve.tensor_scalar(tot75[:, :], tot75[:, :], 0.75, None, ALU.mult))
                step(dve.tensor_tensor(before[:, :, :], before[:, :, :], bc(tot75[:, :], 2, E), ALU.is_lt))
                step(dve.scalar_tensor_tensor(out=valid[:, :, :].rearrange("p c e -> p (c e)"),
                                              in0=rank[:, :, :].rearrange("p c e -> p (c e)"), scalar=4.0,
                                              in1=before[:, :, :].rearrange("p c e -> p (c e)"),
                                              op0=ALU.is_lt, op1=ALU.mult))
                if b >= 1:
                    step(dve.tensor_tensor(carry[:, :], carry[:, :], msum[:, :], ALU.add))
                    dve.wait_ge(csum_psum, b)
                    dve.tensor_copy(carry_b[:, :], carry[:, :])
                dve.tensor_copy(valid_b[:, :, :], valid[:, :, :]).then_inc(valid_ready, 1)
                step(dve.tensor_reduce(msum[:, :], valid[:, :, :].rearrange("p c e -> p e c"), AX.X, ALU.add))
                step(dve.tensor_scalar(mden[:, :, :], mden[:, :, :], 1e-30, None, ALU.max))
                step(dve.reciprocal(mden[:, :, :], mden[:, :, :]))
                step(dve.tensor_tensor(rw[:, :, :], ex[:, :, :], mden[:, :, :], ALU.mult))
                step(dve.tensor_tensor(rw[:, :, :], rw[:, :, :], valid[:, :, :], ALU.mult))
                step(dve.tensor_reduce(rsum[:, :], rw[:, :, :], AX.X, ALU.add))
                step(dve.reciprocal(rsum[:, :], rsum[:, :]))
                step(dve.tensor_tensor(rw[:, :, :], rw[:, :, :], bc(rsum[:, :], 2, E), ALU.mult))

            def capacity(b):
                dve.wait_ge(csum_psum, b + 1)
                dve.tensor_copy(pos[:, :, :], csum_ps).then_inc(csum_read, 1)
                dve.wait_ge(csum_read, b + 1)
                step(dve.tensor_scalar(l9[:, :, 0:E], pos[:, :, :], float(CAP), None, ALU.is_le))
                step(dve.tensor_tensor(keep9[:, :, 0:E], l9[:, :, 0:E], valid[:, :, :], ALU.mult))
                step(dve.tensor_scalar(l9[:, :, :], keep9[:, :, :], -NEG, NEG, ALU.mult, ALU.add))
                step(dve.tensor_tensor(l9[:, :, :], l9[:, :, :], logit[:, b % 2, :, :], ALU.add))
                step(dve.tensor_reduce(lmax[:, :], l9[:, :, :], AX.X, ALU.max))
                dve.tensor_tensor(t9[:, :, :], l9[:, :, :], bc(lmax[:, :], 2, E + 1), ALU.subtract).then_inc(t9_ready, 1)
                if b >= 1:
                    dve.wait_ge(onehot_pool, 2 * b)
                kf = keep9[:, :, 0:E]
                pf = pos[:, :, :].rearrange("p c e -> p (c e)")
                step(dve.tensor_scalar(tile_j[:, :], pf, float(P), None, ALU.is_gt))
                step(dve.scalar_tensor_tensor(out=tile_j[:, :], in0=pf, scalar=float(2 * P), in1=tile_j[:, :],
                                              op0=ALU.is_gt, op1=ALU.add))
                step(dve.scalar_tensor_tensor(out=pk[:, :], in0=tile_j[:, :], scalar=-float(P), in1=pf,
                                              op0=ALU.mult, op1=ALU.add))
                dve.tensor_tensor(pk[:, :].rearrange("p (c e) -> p c e", c=NC),
                                  pk[:, :].rearrange("p (c e) -> p c e", c=NC), kf, ALU.mult).then_inc(pk_ready, 1)

            def weights(b):
                kf = keep9[:, :, 0:E]
                dve.wait_ge(e9_ready, b + 1)
                dve.tensor_reduce(rsum[:, :], e9[:, :, :], AX.X, ALU.add)
                step(dve.tensor_reduce(sdyn[:, :], e9[:, :, 0:E], AX.X, ALU.add))
                step(dve.reciprocal(rsum[:, :], rsum[:, :]))
                step(dve.tensor_scalar(rsum[:, :], rsum[:, :], half_gf[:, :], None, ALU.mult))
                dve.tensor_tensor(w_shared[:, b * NC:(b + 1) * NC], e9[:, :, E], rsum[:, :], ALU.mult)
                step(dve.tensor_tensor(sdyn[:, :], sdyn[:, :], rsum[:, :], ALU.mult))
                step(dve.tensor_tensor(rw[:, :, :], rw[:, :, :], bc(sdyn[:, :], 2, E), ALU.mult))
                step(dve.tensor_tensor(rw[:, :, :], rw[:, :, :], kf, ALU.mult))
                rf = rw[:, :, :].rearrange("p c e -> p (c e)")
                vb = val[:, b * NC * E:(b + 1) * NC * E, :]
                if b >= 1:
                    dve.wait_ge(slots_psum, b)
                step(dve.tensor_copy(vb[:, :, 2], rf))
                step(dve.tensor_tensor(res[:, :], rf, vb[:, :, 2], ALU.subtract))
                step(dve.tensor_copy(vb[:, :, 3], res[:, :]))
                step(dve.tensor_tensor(res[:, :], res[:, :], vb[:, :, 3], ALU.subtract))
                step(dve.tensor_copy(vb[:, :, 4], res[:, :]))
                for j in range(EJ):
                    dve.scalar_tensor_tensor(out=val_j[:, :, j, :], in0=bc(tile_j[:, :], 2, NV), scalar=float(j),
                                             in1=vb, op0=ALU.is_equal,
                                             op1=ALU.mult).then_inc(val_ready, 1)

            def one_hots(b, c):
                m = slice(c * E, (c + 1) * E)
                dve.tensor_tensor(onehot[:, m, :], bc(iota1[:, :], 1, E), bc(pk[:, m], 2, P),
                                  ALU.is_equal).then_inc(onehot_ready, 1)

            def add_slots(b):
                dve.wait_ge(slots_psum, b + 1)
                sf = slots[:, :, :, :].rearrange("p e j v -> p (e j v)")
                dve.tensor_tensor(sf, sf, slots_ps, ALU.add).then_inc(slots_read, 1)
                dve.wait_ge(slots_read, b + 1)

            def silu_mul(b, i):
                m = NG * b + i
                dve.wait_ge(sig_ready, m + 1)
                if b >= 2 and i == 0:
                    dve.wait_ge(y_psum, NC * (b - 1))
                step(dve.scalar_tensor_tensor(out=sig[:, m % 2, 0:HS], in0=sig[:, m % 2, 0:HS], scalar=1.0,
                                              in1=gu_ps[m % 2][:, 0:HS], op0=ALU.add, op1=ALU.mult))
                dve.tensor_tensor(act_sh[:, b % 2, i % IC, (i // IC) * HS:(i // IC + 1) * HS], sig[:, m % 2, 0:HS],
                                  gu_ps[m % 2][:, HS:2 * HS], ALU.mult).then_inc(act_ready, 1)

            def shared_out(b, c):
                n = b * NC + c
                dve.wait_ge(y_psum, n + 1)
                dve.scalar_tensor_tensor(out=xs[:, n, :], in0=y_ps[:, 0:HD], scalar=w_shared[:, n:n + 1],
                                         in1=xs[:, n, :], op0=ALU.mult, op1=ALU.add).then_inc(o_ready, 1)

            for t in range(LAST):
                n = t // 2
                if t % 2 == 0 and n < NT:
                    decay_scores(n)
                if t % 2 == 1 and 1 <= n <= NT:
                    join(n - 1)
                if t % 2 == 1 and n < NT:
                    new_state(n)
                if (u := unit(t - 1, GATEUP, NG, 1)) is not None:
                    silu_mul(*u)
                if (u := unit(t - 1, DOWN, NC, 2)) is not None:
                    shared_out(*u)
                if (b := due(t, HSTATS)) is not None:
                    head_stats(b)
                if (b := due(t, HNORM)) is not None:
                    head_norm(b)
                if (b := due(t, STATS2)) is not None:
                    norm2_stats(b)
                if (b := due(t, NORM2)) is not None:
                    norm2(b)
                if (b := due(t, CHOOSE)) is not None:
                    choose(b)
                if (b := due(t, PICK)) is not None:
                    pick(b)
                if (b := due(t, CAPAC)) is not None:
                    capacity(b)
                    weights(b)
                if (b := due(t, CAPAC + 1)) is not None:
                    one_hots(b, 0)
                    one_hots(b, 1)
                if (b := due(t, LISTS)) is not None:
                    add_slots(b)
                if due(t, LISTS) == B - 1:
                    sl = slots[:, :, :, :].rearrange("p e j v -> p (e j) v")
                    dve.tensor_tensor(slot_id[:, :], sl[:, :, 0], sl[:, :, 1], ALU.add)
                    step(dve.tensor_tensor(slot_w[:, :], sl[:, :, 3], sl[:, :, 4], ALU.add))
                    dve.tensor_tensor(slot_w[:, :], slot_w[:, :], sl[:, :, 2], ALU.add)
                    step(dve.tensor_scalar(slot_id[:, :], slot_id[:, :], EMPTY, None, ALU.add))
                    dve.tensor_copy(slot_s[:, :], slot_id[:, :])
                    dve.tensor_scalar(slot_g[:, :], slot_id[:, :], float(T - 1), None,
                                      ALU.min).then_inc(slots_ready, 1)

            for e in range(E):
                dve.wait_ge(dsig_ready, e + 1)
                step(dve.scalar_tensor_tensor(out=sig[:, e % 2, 0:CAP], in0=sig[:, e % 2, 0:CAP], scalar=1.0,
                                              in1=g_ps[:, 0:CAP], op0=ALU.add, op1=ALU.mult))
                dve.wait_ge(du_psum, e + 1)
                if e >= 2:
                    dve.wait_ge(dy_psum, e - 1)
                dve.tensor_tensor(act_d[:, e % 2, :], sig[:, e % 2, 0:CAP], u_ps[:, 0:CAP],
                                  ALU.mult).then_inc(dact_ready, 1)


def kernel(**inputs):
    import numpy as np
    import concourse.bacc as bacc
    from concourse.bass_utils import run_bass_kernel_spmd as run

    a = {k: np.asarray(v) for k, v in inputs.items()}
    P, KH = 128, 2

    def lay(t):
        return np.ascontiguousarray(t)

    x = a["x"].reshape(16, P, 256).transpose(1, 0, 2)
    ctx = a["ctx_1024"].reshape(16, P, 256).transpose(1, 0, 2)
    sh = np.stack([a["L0_ffn_sh_gate_w"][0], a["L0_ffn_sh_up_w"][0]])
    dyn = np.stack([a["L0_ffn_dyn_gate_w"], a["L0_ffn_dyn_up_w"]])
    gates = np.concatenate([a["L0_xattn_igate_kernel"], a["L0_xattn_fgate_kernel"]], axis=1)
    laid = {
        "x": lay(x),
        "ctx": lay(ctx),
        "ctxT": lay(a["ctx_1024"].reshape(2048, 256).T),
        "wgu_sh": lay(sh.reshape(2, 512, KH, P).transpose(3, 0, 2, 1)),
        "wd_sh": lay(a["L0_ffn_sh_down_w"][0].reshape(256, 4, P).transpose(2, 1, 0)),
        "wgu_dyn": lay(dyn.reshape(2, 8, P, KH, P).transpose(4, 0, 1, 3, 2)),
        "wd_dyn": lay(a["L0_ffn_dyn_down_w"].transpose(2, 0, 1)),
        "w_route": lay(a["L0_ffn_gate_w"].reshape(9, KH, P).transpose(2, 1, 0)),
        "w_gates": lay(gates.reshape(3 * KH, P, 8).transpose(1, 0, 2)),
        "b_rows": lay(np.tile(np.stack([a["L0_xattn_igate_bias"], a["L0_xattn_fgate_bias"]], axis=1), (32, 1))),
        "g_pair": lay(np.concatenate([a["g_xattn"], a["g_ffn"]])),
        "out_scale": lay(a["L0_xattn_outnorm_scale"]),
    }
    nc = bacc.Bacc("TRN2", target_bir_lowering=False, num_devices=1)
    fp32 = mybir.dt.float32
    aps = {k: nc.dram_tensor(f"in_{k}", v.shape, fp32, kind="ExternalInput").ap() for k, v in laid.items()}
    out = nc.dram_tensor("out_rows", (P, 16, 256), fp32, kind="ExternalOutput").ap()
    gated_mlstm_moe_block(nc, aps, out)
    r = run(nc, [{f"in_{k}": v for k, v in laid.items()}], core_ids=[0])
    return r.results[0]["out_rows"].transpose(1, 0, 2).reshape(4, 512, 256)
```

```python
import concourse.bass as bass
from concourse import mybir
from contextlib import ExitStack


def gated_mlstm_moe_block(nc, A, out):
    fp32, f32r, bf16, i32 = (mybir.dt.float32, mybir.dt.float32r, mybir.dt.bfloat16, mybir.dt.int32)
    ALU = mybir.AluOpType
    ACT = mybir.ActivationFunctionType
    AX = mybir.AxisListType

    P = 128
    B, SEQ, HD = 4, 512, 256
    NH, DH = 4, 64
    DA = DH + 1
    NC = SEQ // P
    NT = B * NC
    T = B * SEQ
    KH = HD // P
    E, EI = 8, 128
    SI = 512
    IC = SI // P
    CAP = 320
    EJ = 3
    EROWS = [128, 128, 64]
    NV = 5
    AHEAD = 13
    GAP = 2
    SHIFT = 4096.0
    DVE_HOT = (3, 2, 2, 3)
    HS = SEQ // 2
    GR = 3
    NG = IC * 2
    HSTATS = (9, 17, 25, 30, 33)
    HNORM = (10, 19, 26, 31, 34)
    ADDX = (12, 19, 27, 35)
    STATS2 = (13, 21, 30, 36)
    NORM2 = (14, 22, 31, 37)
    X2T = (15, 23, 32, 38)
    ROUTE = (17, 25, 34, 39)
    CHOOSE = (18, 26, 35, 41)
    PICK = (19, 27, 36, 42)
    SHARE = (19, 27, 36, 42)
    COUNT = (20, 28, 37, 43)
    CAPAC = (20, 29, 38, 44)
    WEIGHTS = (20, 29, 38, 44)
    ONEHOT = (21, 30, 39, 45)
    LISTS = (22, 31, 40, 45)
    GATEUP = (18, 26, 34, 42)
    GRATE = (2, 1, 1, 2)
    DOWN = (23, 31, 38, 49)
    DSTEP = (2, 2, 2, 1)
    gate_up_at = [GATEUP[b] + i // GRATE[b] for b in range(B) for i in range(NG)]
    act_at = gate_up_at[1:] + [gate_up_at[-1] + 1]
    down_at = [DOWN[b] + c * DSTEP[b] for b in range(B) for c in range(NC)]
    store_at = [down_at[NC * b + NC - 1] + 2 for b in range(B)]
    LAST = max(down_at[-1], act_at[-1]) + 3
    QSCALE = float(DH) ** -0.5
    NEG = -1.0e30

    ctx = ExitStack()
    with ctx:
        def sb(name, shape, dt=fp32):
            return ctx.enter_context(nc.sbuf_tensor(name, shape, dt))

        def sem(name):
            return ctx.enter_context(nc.semaphore(name))

        def bank(name):
            return ctx.enter_context(nc.psum_tensor(name, [P, 512], fp32))

        def order(h):
            return (h % 2) * 2 + h // 2

        def due(t, starts, count=1, every=1):
            return [(b, i) for b in range(B) for i in range(count) if starts[b] + i * every == t]

        def at(t, times, count):
            return [divmod(u, count) for u, when in enumerate(times) if when == t]

        def due_half(t, starts):
            return [(b, i) for b, i in due(t, starts, 2) if b < B - 1] + [(B - 1, 0)] * (starts[B - 1] == t)

        head_parts = [(b, 0, NC) for b in range(B - 1)] + [(B - 1, 0, NC // 2), (B - 1, NC // 2, NC)]

        def bc(ap, axis, n):
            ap = ap.unsqueeze(axis)
            shape = list(ap.shape)
            shape[axis] = n
            return ap.to_broadcast(shape)

        xs = sb("xs", [P, NT, HD])
        v_aug = sb("v_aug", [P, NT, NH, DA])
        kT = sb("kT", [P, KH, T])
        qT = sb("qT", [P, KH, T])
        x2T = sb("x2T", [P, KH, T])
        normed = sb("normed", [P, 2, NC, HD])
        wgu_sh = sb("wgu_sh", [P, 2, KH, SI])
        wd_sh = sb("wd_sh", [P, IC, HD])
        wgu_dyn = sb("wgu_dyn", [P, 2, E, KH, EI])
        wd_dyn = sb("wd_dyn", [P, E, HD])
        w_route = sb("w_route", [P, KH, E + 1])
        w_gates = sb("w_gates", [P, 3 * KH, 2 * NH])
        b_rows = sb("b_rows", [P, 2])
        w_rows = sb("w_rows", [P, 2 * KH, 2, 8, NH])
        g_pair = sb("g_pair", [P, 2])
        tanh_g = sb("tanh_g", [P, 2])
        half_gf = sb("half_gf", [P, 1])
        out_scale = sb("out_scale", [P, HD])
        ident = sb("ident", [P, P])
        ident_b = sb("ident_b", [P, P], bf16)
        tri_b = sb("tri_b", [P, P], bf16)
        ones_b = sb("ones_b", [P, P], bf16)
        causal_b = sb("causal_b", [P, NH, P], bf16)
        iota1 = sb("iota1", [P, P], bf16)
        tri_e = sb("tri_e", [P, E, E])
        row_of = sb("row_of", [P, NH, 32])
        head_of = sb("head_of", [P, NH])
        rep_of = sb("rep_of", [P, 8])
        is_a = sb("is_a", [P, 1])
        is_m = sb("is_m", [P, 1])
        is_hi = sb("is_hi", [P, 1])
        is_lo = sb("is_lo", [P, 1])
        hi_less_lo = sb("hi_less_lo", [P, 1])
        m_head = sb("m_head", [P, NH])
        a_head = sb("a_head", [P, NH])
        parity = sb("parity", [P, 2])
        par_sel = sb("par_sel", [P, P])
        pair_row = sb("pair_row", [P, B, 2])
        m_half = sb("m_half", [P, 16])
        act_sh = sb("act_sh", [P, 2, IC, SEQ])
        fmin, fabs, parts, u_row, w_row, n_row, av, av_lo = (act_sh[:, i // IC, i % IC, :] for i in range(2 * IC))
        fexp, av_hi = parts, fabs.bitcast(f32r)
        sig = sb("sig", [P, GR, 2, HS])
        a_row, negm = (sig[:, r, :, :].rearrange("p w s -> p (w s)") for r in range(2))
        sig_d = sig[:, :, :, :].rearrange("p r w s -> p r (w s)")
        m_row = sb("m_row", [P, SEQ])
        dec_row = sb("dec_row", [P, NC])
        dec_sel = sb("dec_sel", [P, B, 2, NC])
        dl = sb("dl", [P, SEQ], f32r)
        dr = sb("dr", [P, NC, NH, P], f32r)
        u_t = sb("u_t", [P, NC, B, NH])
        w_t = sb("w_t", [P, NC, B, NH])
        n_t = sb("n_t", [P, NC, B, NH])
        dec_t = sb("dec_t", [P, B, 2, NC])
        dexp = sb("dexp", [P, 2, NH * P])
        cmat = sb("cmat", [P, 2, NH * P])
        gi_row, gf_row = dexp[:, 0, :], dexp[:, 1, :]
        cs, mld = cmat[:, 0, :], cmat[:, 1, :]
        ones_row = mld
        uv = sb("uv", [P, 2, NH, DA])
        state = sb("state", [P, 2, 2, 2 * DA])
        far = sb("far", [P, 2, NH, DA])
        heads = sb("heads", [P, 2, NC, NH, DA])
        st = sb("st", [P, NC, 6])
        st_h = sb("st_h", [P, 16, 6])
        st_s = sb("st_s", [P, 16])
        st_d = sb("st_d", [P, 16])
        st_v = sb("st_v", [P, 16])
        st_d2 = sb("st_d2", [P, 16])
        mean = sb("mean", [P, 16])
        var_eps = sb("var_eps", [P, 16])
        rstd = sb("rstd", [P, 16])
        den = sb("den", [P, 16])
        rden = sb("rden", [P, 16])
        rden2 = sb("rden2", [P, 16])
        hscale = sb("hscale", [P, 16])
        hshift = sb("hshift", [P, 16])
        mean2 = sb("mean2", [P, NC])
        var2 = sb("var2", [P, NC])
        rstd2 = sb("rstd2", [P, NC])
        scale2 = sb("scale2", [P, NC])
        shift2 = sb("shift2", [P, NC])
        logit = sb("logit", [P, 2, NC, E + 1])
        lmax = sb("lmax", [P, NC])
        labs = sb("labs", [P, NC, E])
        lsh = sb("lsh", [P, NC, E])
        ex = sb("ex", [P, NC, E])
        tot75 = sb("tot75", [P, NC])
        pd = sb("pd", [P, NC * E, E])
        pe_ = sb("pe_", [P, NC * E, E])
        pb = sb("pb", [P, NC * E, E])
        pc = pd
        pm = sb("pm", [P, NC * E, E])
        rank = sb("rank", [P, NC, E])
        before = sb("before", [P, NC, E])
        valid = sb("valid", [P, NC, E])
        valid_b = sb("valid_b", [P, NC, E], bf16)
        mden = sb("mden", [P, NC, E])
        rw = sb("rw", [P, NC, E])
        rsum = sb("rsum", [P, NC])
        carry = sb("carry", [P, E])
        carry_b = sb("carry_b", [P, E], bf16)
        msum = sb("msum", [P, E])
        pos = sb("pos", [P, NC, E])
        keep9 = sb("keep9", [P, NC, E + 1])
        l9 = sb("l9", [P, NC, E + 1])
        t9 = sb("t9", [P, NC, E + 1])
        e9 = sb("e9", [P, NC, E + 1])
        sdyn = sb("sdyn", [P, NC])
        w_shared = sb("w_shared", [P, NT])
        tile_j = sb("tile_j", [P, NC * E])
        pk = sb("pk", [P, NC * E])
        onehot = sb("onehot", [P, NC * E, P], bf16)
        val = sb("val", [P, NT * E, NV], bf16)
        res = sb("res", [P, NC * E])
        val_j = sb("val_j", [P, NC * E, EJ, NV], bf16)
        slots = sb("slots", [P, E, EJ, NV])
        slot_w = sb("slot_w", [P, E * EJ])
        slot_id = sb("slot_id", [P, E * EJ])
        spare = sb("spare", [P, E * EJ])
        spare_row = sb("spare_row", [P, E * EJ])
        slot_s = sb("slot_s", [P, E * EJ], i32)
        slot_g = sb("slot_g", [P, E * EJ], i32)
        pair_g = sb("pair_g", [P, E // 2], i32)
        k_flat = kT[:, :, :].rearrange("p k t -> p (k t)")
        q_flat = qT[:, :, :].rearrange("p k t -> p (k t)")
        n_e = EJ * HD
        ek = KH * T // n_e
        rows = [(k_flat if e < ek else q_flat)[:, (e % ek) * n_e:(e % ek + 1) * n_e].rearrange("p (j h) -> p j h", j=EJ)
                for e in range(E)]
        n_flat = normed[:, :, :, :].rearrange("p r c h -> p (r c h)")
        n_pair = KH * 2 * CAP
        xgT = [part.rearrange("p (k s) -> p k s", k=KH)
               for part in (n_flat[:, 0:n_pair], q_flat[:, KH * T - n_pair:KH * T])]
        act_d = n_flat[:, n_pair:n_pair + 2 * CAP].rearrange("p (r s) -> p r s", r=2)
        gathers = [(e, j) for e in range(E) for j in range(EJ if e % 2 == 0 else EJ - 1)]

        def slot_columns(e, j):
            first = (j * P if e % 2 == 0 else (EROWS[2] + j * P) % CAP)
            return slice(first, first + EROWS[j])

        s0_ps, s1_ps, d_ps, h_ps, t_ps, g_ps, u_ps, y_ps = (
            bank(s) for s in ("s0_ps", "s1_ps", "d_ps", "h_ps", "t_ps", "g_ps", "u_ps", "y_ps"))
        qk_ps = [s_[:, 0:2 * P] for s_ in (s0_ps, s1_ps)]
        far_ps = [s_[:, 2 * P:2 * P + 2 * DA] for s_ in (s0_ps, s1_ps)]
        kv_ps = h_ps[:, NH * DA:NH * DA + 2 * DA].rearrange("p (a d) -> p a d", a=2)
        gate_ps = [g_ps, u_ps, y_ps, h_ps]
        qt_ps = [(s0_ps, d_ps), (s1_ps, t_ps)]
        gu_ps = [g_ps, u_ps]
        def x2T_bank(b, k):
            return (s0_ps, s1_ps)[k] if b == B - 1 else t_ps

        def down_bank(b, c):
            return h_ps if b == B - 1 and c % 2 == 1 else y_ps

        def route_bank(b):
            return x2T_bank(b, 0)[:, 0:NC * (E + 1)].rearrange("p (c e) -> p c e", c=NC)

        near_ps = h_ps[:, 0:NH * DA].rearrange("p (h d) -> p h d", h=NH)
        csum_ps = t_ps[:, 64:64 + NC * E].rearrange("p (c e) -> p c e", c=NC)
        slots_ps = t_ps[:, 128:128 + E * EJ * NV]

        x2_dram = nc.dram_tensor("x2_rows", (T, HD), fp32, kind="Internal").ap()
        x_v = A["x"].rearrange("p (b c) h -> b p c h", c=NC)
        v_v = A["ctx"].rearrange("p (b c) (h d) -> b p (c h) d", c=NC, h=NH)
        kT_v = A["ctxT"].rearrange("(k p) (b s) -> b p k s", p=P, s=SEQ)
        x2_v = x2_dram.rearrange("(p b c) h -> b p c h", c=NC, b=B)
        out_v = out[0:T, :].rearrange("(p b c) h -> b p c h", c=NC, b=B)

        x_in = [sem(f"x_in{b}") for b in range(B)]
        k_in = [sem(f"k_in{b}") for b in range(B)]
        v_in = sem("v_in")
        small_in = sem("small_in")
        w_sh_in = sem("w_sh_in")
        w_dyn_in = sem("w_dyn_in")
        pool_step, dve_step, act_step = sem("pool_step"), sem("dve_step"), sem("act_step")
        consts_ready = sem("consts_ready")
        masks_ready = sem("masks_ready")
        ones_ready, spare_zero = sem("ones_ready"), sem("spare_zero")
        tanh_ready = sem("tanh_ready")
        row_masks_ready = sem("row_masks_ready")
        parts_ready, dl_ready = sem("parts_ready"), sem("dl_ready")
        gate_w_ready = sem("gate_w_ready")
        var1_ready, rstd1_ready = sem("var1_ready"), sem("rstd1_ready")
        scale1_ready, q_ready = sem("scale1_ready"), sem("q_ready")
        qT_psum, qT_act, qT_dve = sem("qT_psum"), sem("qT_act"), sem("qT_dve")
        gates_psum, gf_ready, gi_ready = sem("gates_psum"), sem("gf_ready"), sem("gi_ready")
        softplus_ready = sem("softplus_ready")
        mrow_ready, exps_ready = sem("mrow_ready"), sem("exps_ready")
        drows_ready = sem("drows_ready")
        decsel_ready = sem("decsel_ready")
        cols_psum, cols_ready = sem("cols_psum"), sem("cols_ready")
        d_psum, dexp_ready = sem("d_psum"), sem("dexp_ready")
        scores_psum = sem("scores_psum")
        c_ready, far_ready, near_psum = sem("c_ready"), sem("far_ready"), sem("near_psum")
        uv_ready, state_ready, heads_ready = sem("uv_ready"), sem("state_ready"), sem("heads_ready")
        hvar_ready, hrstd_ready, z_ready, x1_ready = (
            sem("hvar_ready"), sem("hrstd_ready"), sem("z_ready"), sem("x1_ready"))
        hscale_ready, scale2_ready = sem("hscale_ready"), sem("scale2_ready")
        var2_ready, rstd2_ready, x2_ready = sem("var2_ready"), sem("rstd2_ready"), sem("x2_ready")
        x2T_psum, x2T_ready = sem("x2T_psum"), sem("x2T_ready")
        route_psum, route_read = sem("route_psum"), sem("route_read")
        lsh_ready, ex_ready = sem("lsh_ready"), sem("ex_ready")
        valid_ready, csum_psum, csum_read = sem("valid_ready"), sem("csum_psum"), sem("csum_read")
        t9_ready, e9_ready = sem("t9_ready"), sem("e9_ready")
        pk_ready, val_ready = sem("pk_ready"), sem("val_ready")
        onehot_ready, onehot_pool, slots_psum, slots_read = sem("onehot_ready"), sem("onehot_pool"), sem("slots_psum"), sem("slots_read")
        gu_psum, sig_ready, gated_ready, act_ready = (
            sem("gu_psum"), sem("sig_ready"), sem("gated_ready"), sem("act_ready"))
        y_psum, o_ready = sem("y_psum"), sem("o_ready")
        x2_stored = [sem(f"x2_stored{b}") for b in range(B)]
        o_stored = [sem(f"o_stored{b}") for b in range(B)]
        slots_ready, ids_ready, shifted_psum, pairs_ready = (
            sem("slots_ready"), sem("ids_ready"), sem("shifted_psum"), sem("pairs_ready"))
        gathered = [sem(f"gathered{e}") for e in range(E)]
        xgT_psum, xgT_ready = sem("xgT_psum"), sem("xgT_ready")
        dg_psum, du_psum, dsig_ready, dact_ready = (
            sem("dg_psum"), sem("du_psum"), sem("dsig_ready"), sem("dact_ready"))
        dy_psum, ys_ready = sem("dy_psum"), sem("ys_ready")
        added = sem("added")

        block = ctx.enter_context(nc.Block())

        @block.sync
        def _(sp):
            for b in range(B):
                sp.dma_start(xs[:, b * NC:(b + 1) * NC, :], x_v[b]).then_inc(x_in[b], 16)
                sp.dma_start(kT[:, :, b * SEQ:(b + 1) * SEQ], kT_v[b]).then_inc(k_in[b], 16)
            for b in range(B):
                sp.dma_start(v_aug[:, b * NC:(b + 1) * NC, :, 0:DH].rearrange("p c h d -> p (c h) d"),
                             v_v[b]).then_inc(v_in, 16)
            sp.wait_ge(ones_ready, 2)
            for j in range(EJ):
                sp.dma_start(out[T + j * P:T + (j + 1) * P, :],
                             state[:, 0, :, :].rearrange("p i d -> p (i d)")[:, 0:HD]).then_inc(spare_zero, 16)
            sp.dma_start(wgu_sh[:, :, :, :], A["wgu_sh"]).then_inc(w_sh_in, 16)
            sp.dma_start(wd_sh[:, :, :], A["wd_sh"]).then_inc(w_sh_in, 16)
            sp.dma_start(wgu_dyn[:, :, :, :, :], A["wgu_dyn"]).then_inc(w_dyn_in, 16)
            sp.dma_start(wd_dyn[:, :, :], A["wd_dyn"]).then_inc(w_dyn_in, 16)
            for t in range(LAST):
                for b, _ in due(t, NORM2):
                    sp.wait_ge(x2_ready, b + 1)
                    sp.dma_start(x2_v[b], normed[:, b % 2, :, :]).then_inc(x2_stored[b], 16)
                for b, _ in due(t, store_at):
                    sp.wait_ge(o_ready, NC * (b + 1))
                    sp.dma_start(out_v[b], xs[:, b * NC:(b + 1) * NC, :]).then_inc(o_stored[b], 16)
            for b in range(B):
                sp.wait_ge(x2_stored[b], 16)
                sp.wait_ge(o_stored[b], 16)
            sp.wait_ge(added, 16 * E * EJ)

        @block.gpsimd
        def _(pool):
            done = [0]

            def step(ins):
                done[0] += 1
                ins.then_inc(pool_step, 1)
                pool.wait_ge(pool_step, done[0])

            pool.memset(m_half[:, :], -0.5)
            pool.memset(ones_b[:, :], 1.0)
            pool.memset(tri_b[:, :], 1.0)
            pool.memset(causal_b[:, :, :], 0.0)
            pool.memset(tri_e[:, :, :], 1.0)
            pool.memset(row_of[:, :, :], 0.0)
            pool.memset(slots[:, :, :, :], 0.0)
            pool.memset(carry[:, :], 0.0)
            pool.memset(carry_b[:, :], 0.0)
            pool.memset(keep9[:, :, :], 1.0)
            step(pool.memset(ident[:, :], 0.0))
            pool.affine_select(out=ident[:, :], in_=ident[:, :], compare_op=ALU.not_equal, fill=1.0, base=0,
                               pattern=[[-1, P]], channel_multiplier=1)
            step(pool.affine_select(out=row_of[:, :, :], in_=row_of[:, :, :], compare_op=ALU.not_equal, fill=1.0,
                                    base=0, pattern=[[-1, NH], [-4, 32]], channel_multiplier=1))
            pool.tensor_copy(ident_b[:, :], ident[:, :])
            pool.affine_select(out=tri_b[:, :], in_=tri_b[:, :], compare_op=ALU.is_ge, fill=0.0, base=0,
                               pattern=[[1, P]], channel_multiplier=-1)
            pool.affine_select(out=causal_b[:, :, :], in_=causal_b[:, :, :], compare_op=ALU.is_ge, fill=NEG, base=0,
                               pattern=[[0, NH], [1, P]], channel_multiplier=-1)
            pool.affine_select(out=tri_e[:, :, :], in_=tri_e[:, :, :], compare_op=ALU.is_gt, fill=0.0, base=0,
                               pattern=[[1, E], [-1, E]], channel_multiplier=0)
            pool.iota(iota1[:, :], pattern=[[1, P]], base=1, channel_multiplier=0,
                      allow_small_or_imprecise_dtypes=True)
            pool.iota(spare_row[:, :], pattern=[[0, E], [P, EJ]], base=T - int(SHIFT), channel_multiplier=1,
                      allow_small_or_imprecise_dtypes=True)
            pool.iota(val[:, :, 0:1], pattern=[[0, NT * E], [0, 1]], base=-int(SHIFT), channel_multiplier=NT,
                      allow_small_or_imprecise_dtypes=True)
            pool.iota(val[:, :, 1:2].rearrange("p (n e) v -> p n (e v)", e=E), pattern=[[1, NT], [0, E]],
                      base=0, channel_multiplier=0,
                      allow_small_or_imprecise_dtypes=True).then_inc(consts_ready, 1)

            def rsqrt(m, src, dst, ready, count, signal):
                pool.wait_ge(ready, count)
                pool.tensor_tensor(dst[:, 0:m], src[:, 0:m], m_half[:, 0:m], ALU.pow).then_inc(signal, 1)

            def scaled_v(n):
                b, c = divmod(n, NC)
                if n >= 2:
                    pool.wait_ge(near_psum, n - 1)
                pool.tensor_tensor(uv[:, n % 2, :, :], v_aug[:, n, :, :], bc(u_t[:, c, b, :], 2, DA),
                                   ALU.mult).then_inc(uv_ready, 1)

            def times_up(b, i):
                m = NG * b + i
                pool.wait_ge(gated_ready, m + 1)
                if b >= 2 and i == 0:
                    pool.wait_ge(y_psum, NC * (b - 1))
                pool.tensor_tensor(act_sh[:, b % 2, i % IC, (i // IC) * HS:(i // IC + 1) * HS], sig[:, m % GR, 0, :],
                                   sig[:, m % GR, 1, :], ALU.mult).then_inc(act_ready, 1)

            def add_x(b, i):
                c = slice(i * NC // 2, (i + 1) * NC // 2)
                pool.wait_ge(z_ready, 2 * b + i + 1)
                if b == 0 and i == 0:
                    pool.wait_ge(tanh_ready, 1)
                z = heads[:, b % 2, c, :, 0:DH]
                xb = xs[:, b * NC:(b + 1) * NC, :].rearrange("p c (h d) -> p c h d", h=NH)[:, c, :, :]
                step(pool.tensor_tensor(z, z, bc(out_scale[:, :].rearrange("p (h d) -> p h d", h=NH), 1, NC // 2),
                                        ALU.mult))
                pool.tensor_tensor(xb, z, xb, ALU.add).then_inc(x1_ready, 1)

            def one_hots(b, c):
                pool.wait_ge(pk_ready, b + 1)
                if b >= 1:
                    pool.wait_ge(slots_psum, b)
                for m in range(c * E, (c + 1) * E):
                    last = pool.tensor_scalar(onehot[:, m, :], iota1[:, :], pk[:, m:m + 1], None, ALU.is_equal)
                last.then_inc(onehot_pool, 1)

            for b in range(B):
                c = slice(b * NC, (b + 1) * NC)
                rsqrt(NC, var_eps[:, c], rstd[:, c], var1_ready, b + 1, rstd1_ready)
            pool.wait_ge(cols_ready, 1)
            pool.wait_ge(v_in, 16 * B)
            pool.wait_ge(ones_ready, 1)
            scaled_v(0)
            for t in range(LAST):
                if t % 2 == 1 and (t + 1) // 2 < NT:
                    scaled_v((t + 1) // 2)
                for u in at(t, act_at, NG):
                    times_up(*u)
                for p, (b, c0, c1) in enumerate(head_parts):
                    if HSTATS[p] == t:
                        g = slice(c0 * NH, c1 * NH)
                        rsqrt((c1 - c0) * NH, var_eps[:, g], rstd[:, g], hvar_ready, p + 1, hrstd_ready)
                for u in due_half(t, ADDX):
                    add_x(*u)
                for b, _ in due(t, STATS2):
                    rsqrt(NC, var2, rstd2, var2_ready, b + 1, rstd2_ready)
                for b, _ in due(t, CAPAC):
                    for c in range(DVE_HOT[b], NC):
                        one_hots(b, c)

            def gather(first, last):
                for e, j in gathers[first:last]:
                    if (e, j) == (0, EJ - 1):
                        pool.wait_ge(pairs_ready, 2)
                    ids = pair_g[:, e // 2:e // 2 + 1] if j == EJ - 1 else slot_g[:, e * EJ + j:e * EJ + j + 1]
                    pool.indirect_dma_start(
                        out=rows[e][:, j, :], out_offset=None, in_=x2_dram[:, :],
                        in_offset=bass.IndirectOffsetOnAxis(ap=ids, axis=0),
                        bounds_check=T - 1, oob_is_err=False).then_inc(gathered[e], 16)

            def scatter_add(e):
                if e == 0:
                    pool.wait_ge(slots_ready, 2)
                pool.wait_ge(ys_ready, e + 1)
                if e >= 1:
                    pool.wait_ge(added, 16 * EJ * e)
                for j in range(EJ):
                    pool.indirect_dma_start(
                        out=out[:, :], out_offset=bass.IndirectOffsetOnAxis(
                            ap=slot_s[0:EROWS[j], e * EJ + j:e * EJ + j + 1], axis=0),
                        in_=rows[e][0:EROWS[j], j, :], in_offset=None,
                        bounds_check=T + EJ * P - 1, oob_is_err=True, compute_op=ALU.add).then_inc(added, 16)

            pool.wait_ge(slots_ready, 1)
            for b in range(B):
                pool.wait_ge(x2_stored[b], 16)
            gather(0, AHEAD)
            pool.wait_ge(spare_zero, 16 * EJ)
            for b in range(B):
                pool.wait_ge(o_stored[b], 16)
            for e in range(E):
                scatter_add(e)
                gather(AHEAD + GAP * e, AHEAD + GAP * (e + 1))

        @block.scalar
        def _(act):
            done = [0]

            def step(ins):
                done[0] += 1
                ins.then_inc(act_step, 1)
                act.wait_ge(act_step, done[0])

            act.dma_start(w_gates[:, :, :], A["w_gates"]).then_inc(small_in, 16)
            act.dma_start(b_rows[:, :], A["b_rows"]).then_inc(small_in, 16)
            act.dma_start(g_pair[:, :], A["g_pair"].partition_broadcast(P)).then_inc(small_in, 16)
            act.dma_start(out_scale[:, :], A["out_scale"].partition_broadcast(P)).then_inc(small_in, 16)
            act.dma_start(w_route[:, :, :], A["w_route"]).then_inc(small_in, 16)
            for i in range(B + 2):
                if i < B:
                    act.wait_ge(scale1_ready, i + 1)
                    if i >= 2:
                        act.wait_ge(qT_psum, KH * (i - 1))
                    for c in range(NC):
                        n = i * NC + c
                        last = act.activation(normed[:, i % 2, c, :], xs[:, n, :], ACT.Identity,
                                              scale=hscale[:, n:n + 1], bias=hshift[:, n:n + 1])
                    last.then_inc(q_ready, 1)
                if 1 <= i <= B:
                    b = i - 1
                    act.wait_ge(qT_psum, KH * b + 1)
                    act.copy(qT[:, 0, b * SEQ:(b + 1) * SEQ], qt_ps[b % 2][0][:, :]).then_inc(qT_act, 1)
                if i >= 2:
                    b = i - 2
                    act.wait_ge(gates_psum, b + 1)
                    act.copy(gf_row[32 * b:32 * b + 32, :], gate_ps[b][32:64, :]).then_inc(gf_ready, 1)
            act.wait_ge(gf_ready, B)
            step(act.activation(fabs[:, :], gf_row[:, :], ACT.Abs, bias=b_rows[:, 1:2]))
            step(act.activation(fexp[:, :], fabs[:, :], ACT.Exp, scale=-1.0))
            act.activation(fabs[:, :], fexp[:, :], ACT.Ln, bias=1.0).then_inc(softplus_ready, 1)
            act.wait_ge(mrow_ready, 1)
            tile = [slice(c * P, (c + 1) * P) for c in range(NC)]
            for c in range(NC):
                last = act.activation(u_row[:, tile[c]], a_row[:, tile[c]], ACT.Exp,
                                      bias=negm[:, (c + 1) * P - 1:(c + 1) * P])
            last.then_inc(exps_ready, 1)
            for c in range(1, NC):
                last = act.activation(w_row[:, tile[c]], negm[:, tile[c]], ACT.Exp, bias=m_row[:, c * P - 1:c * P])
            last.then_inc(exps_ready, 1)
            act.activation(dec_row[:, 1:NC], dec_row[:, 1:NC], ACT.Exp).then_inc(exps_ready, 1)
            act.activation(n_row[:, :], mld[:, :], ACT.Exp, scale=-1.0).then_inc(exps_ready, 1)
            act.wait_ge(parts_ready, 1)
            act.wait_ge(row_masks_ready, 1)
            act.activation(dl[:, :], parts[:, :], ACT.Identity, scale=is_a[:, :], bias=is_m[:, :])
            act.activation(dr[:, :, order(0), :], parts[:, :].rearrange("p (c s) -> p c s", c=NC), ACT.Identity,
                           scale=m_head[:, 0:1], bias=a_head[:, 0:1]).then_inc(dl_ready, 1)
            act.wait_ge(cols_psum, 1)
            for dst, src, c0 in ((u_t, t_ps, 0), (w_t, g_ps, 1), (n_t, u_ps, 0)):
                act.copy(dst[:, c0:NC, :, :],
                         src[:, :].rearrange("p (c b r) -> p c b r", c=NC, b=B)[:, c0:NC, :, 0:NH])
            act.copy(dec_t[:, :, :, :].rearrange("p b a c -> p (b a c)"), y_ps[:, 0:B * 2 * NC]).then_inc(cols_ready, 1)
            act.wait_ge(small_in, 16 * 5)
            act.activation(tanh_g[:, :], g_pair[:, :], ACT.Tanh).then_inc(tanh_ready, 1)

            def decay(n):
                act.wait_ge(d_psum, n + 1)
                if n >= 2:
                    act.wait_ge(c_ready, n - 1)
                act.activation(dexp[:, n % 2, :], d_ps[:, :], ACT.Exp).then_inc(dexp_ready, 1)

            def norm_heads(b, i):
                hb = heads[:, b % 2, :, :, :].rearrange("p c h d -> p (c h) d")
                act.wait_ge(hscale_ready, b + 1)
                for g in range(i * NC * NH // 2, (i + 1) * NC * NH // 2):
                    last = act.activation(hb[:, g, 0:DH], hb[:, g, 0:DH], ACT.Identity, scale=hscale[:, g:g + 1],
                                          bias=hshift[:, g:g + 1])
                last.then_inc(z_ready, 1)

            def norm_rows(b):
                act.wait_ge(scale2_ready, b + 1)
                if b >= 2:
                    act.wait_ge(x2_stored[b - 2], 16)
                    act.wait_ge(x2T_psum, KH * (b - 1))
                for c in range(NC):
                    last = act.activation(normed[:, b % 2, c, :], xs[:, b * NC + c, :], ACT.Identity,
                                          scale=scale2[:, c:c + 1], bias=shift2[:, c:c + 1])
                last.then_inc(x2_ready, 1)

            def copy_x2T(b, k):
                act.wait_ge(x2T_psum, KH * b + k + 1)
                act.copy(x2T[:, k, b * SEQ:(b + 1) * SEQ], x2T_bank(b, k)[:, :]).then_inc(x2T_ready, 1)

            def copy_route(b):
                act.wait_ge(route_psum, b + 1)
                if b >= 2:
                    act.wait_ge(t9_ready, b - 1)
                act.copy(logit[:, b % 2, :, :], route_bank(b)).then_inc(route_read, 1)

            def gate_sigmoid(b, i):
                m = NG * b + i
                act.wait_ge(gu_psum, m + 1)
                if m >= GR:
                    act.wait_ge(act_ready, m - GR + 1)
                act.activation(sig[:, m % GR, 0, :], gu_ps[m % 2][:, 0:HS], ACT.Tanh, scale=0.5)
                act.copy(sig[:, m % GR, 1, :], gu_ps[m % 2][:, HS:2 * HS]).then_inc(sig_ready, 1)

            for t in range(LAST):
                if t % 2 == 0 and t // 2 < NT:
                    decay(t // 2)
                for u in at(t, act_at, NG):
                    gate_sigmoid(*u)
                for u in due_half(t, HNORM):
                    norm_heads(*u)
                for b, _ in due(t, NORM2):
                    if b < B - 1:
                        norm_rows(b)
                for u in due(t, X2T, KH):
                    copy_x2T(*u)
                for b, _ in due(t, ROUTE):
                    copy_route(b)
                for b, _ in due(t, CHOOSE):
                    act.wait_ge(lsh_ready, b + 1)
                    act.activation(ex[:, :, :], lsh[:, :, :], ACT.Exp).then_inc(ex_ready, 1)
                for b, _ in due(t, CAPAC):
                    act.wait_ge(t9_ready, b + 1)
                    act.activation(e9[:, :, :], t9[:, :, :], ACT.Exp).then_inc(e9_ready, 1)

            def copy_xgT(e):
                act.wait_ge(xgT_psum, e + 1)
                if e >= 4:
                    act.wait_ge(du_psum, e - e % 2 - 2)
                src, dst = (slice(0, EJ * P), slice(0, EJ * P)) if e % 2 == 0 else (slice(0, 2 * P), slice(EJ * P, 2 * CAP))
                act.copy(xgT[e // 2 % 2][:, 0, dst], s0_ps[:, src])
                act.copy(xgT[e // 2 % 2][:, 1, dst], d_ps[:, src]).then_inc(xgT_ready, 1)

            def weigh(e):
                act.wait_ge(dy_psum, e + 1)
                for j in range(EJ):
                    src = y_ps[:, j * HD:(j + 1) * HD] if j < 2 else t_ps[0:EROWS[2], 0:HD]
                    last = act.activation(rows[e][0:EROWS[j], j, :], src, ACT.Copy,
                                          scale=slot_w[0:EROWS[j], e * EJ + j:e * EJ + j + 1])
                last.then_inc(ys_ready, 1)

            for e in range(E + 1):
                if e < E:
                    copy_xgT(e)
                    act.wait_ge(dg_psum, e + 1)
                    if e >= 2:
                        act.wait_ge(dact_ready, e - 1)
                    act.activation(sig_d[:, e % 2, 0:CAP], g_ps[:, 0:CAP], ACT.Tanh, scale=0.5).then_inc(dsig_ready, 1)
                if e >= 1:
                    weigh(e - 1)

        @block.tensor
        def _(pe):
            pe.wait_ge(consts_ready, 1)

            def gates_k(b):
                pe.wait_ge(k_in[b], 16)
                for m in range(KH):
                    pe.matmul(gate_ps[b][0:64, :], w_rows[:, KH + m, :, :, :].rearrange("p q j h -> p (q j h)"),
                              kT[:, m, b * SEQ:(b + 1) * SEQ], start=(m == 0), stop=False)

            def gates_q(b):
                pe.wait_ge(qT_act, b + 1)
                pe.wait_ge(qT_dve, b + 1)
                for m in range(KH):
                    last = pe.matmul(gate_ps[b][0:64, :], w_rows[:, m, :, :, :].rearrange("p q j h -> p (q j h)"),
                                     qT[:, m, b * SEQ:(b + 1) * SEQ], start=False, stop=(m == KH - 1))
                last.then_inc(gates_psum, 1)

            for b in range(B):
                pe.wait_ge(q_ready, b + 1)
                if b >= 2:
                    pe.wait_ge(qT_act, b - 1)
                    pe.wait_ge(qT_dve, b - 1)
                for k, dst in enumerate(qt_ps[b % 2]):
                    for c in range(NC):
                        last = pe.transpose(dst[:, c * P:(c + 1) * P], normed[:, b % 2, c, k * P:(k + 1) * P],
                                            ident[:, :])
                    last.then_inc(qT_psum, 1)
                if b == 0:
                    pe.wait_ge(gate_w_ready, 1)
                gates_k(b)
                if b >= 1:
                    gates_q(b - 1)
            gates_q(B - 1)
            for i, (row, dst, c0) in enumerate(((u_row, t_ps, 0), (w_row, g_ps, 1), (n_row, u_ps, 0))):
                pe.wait_ge(exps_ready, (1, 2, 4)[i])
                for c in range(c0, NC):
                    pe.transpose(dst[:, c * P:(c + 1) * P], row[:, c * P:(c + 1) * P], ident[:, :])
            pe.wait_ge(decsel_ready, 1)
            pe.matmul(y_ps[:, 0:B * 2 * NC], par_sel[:, :], dec_sel[:, :, :, :].rearrange("p b a c -> p (b a c)"),
                      start=True, stop=True).then_inc(cols_psum, 1)
            pe.wait_ge(drows_ready, 1)
            pe.wait_ge(dl_ready, 1)
            pe.wait_ge(v_in, 16 * B)
            pe.wait_ge(ones_ready, 1)

            def scores(n):
                b, c = divmod(n, NC)
                tok = slice(n * P, (n + 1) * P)
                r = slice(32 * b, 32 * b + 32)
                if n >= 1:
                    pe.wait_ge(dexp_ready, n)
                pe.matmul(d_ps[:, :], dl[r, c * P:(c + 1) * P], dr[r, c, :, :].rearrange("p h s -> p (h s)"),
                          start=True, stop=False)
                pe.matmul(d_ps[:, :], ident_b[:, :], causal_b[:, :, :].rearrange("p h s -> p (h s)"),
                          start=False, stop=True).then_inc(d_psum, 1)
                if n >= 1:
                    pe.wait_ge(far_ready, n)
                for h in range(NH):
                    g = slice(DH * (h % 2), DH * (h % 2) + DH)
                    i = h // 2
                    last = pe.matmul(qk_ps[h % 2][:, i * P:(i + 1) * P], kT[g, i, tok], qT[g, i, tok],
                                     start=True, stop=True)
                if c > 0:
                    pe.wait_ge(state_ready, n)
                    for i in range(2):
                        last = pe.matmul(far_ps[i], qT[:, i, tok], state[:, (n - 1) % 2, i, :], start=True, stop=True)
                last.then_inc(scores_psum, 1)

            def near(n):
                if n >= 0:
                    pe.wait_ge(c_ready, n + 1)
                    pe.wait_ge(state_ready, n + 1)
                if n >= 1:
                    pe.wait_ge(heads_ready, n)
                for h in range(NH if n >= 0 else 0):
                    last = pe.matmul(near_ps[:, h, :], cmat[:, n % 2, order(h) * P:(order(h) + 1) * P],
                                     v_aug[:, n, h, :], start=True, stop=True)
                if n + 1 < NT:
                    pe.wait_ge(uv_ready, n + 2)
                    for h in range(NH):
                        g = slice(DH * (h % 2), DH * (h % 2) + DH)
                        last = pe.matmul(kv_ps[g, h // 2, :], v_aug[:, n + 1, h, 0:DH], uv[:, (n + 1) % 2, h, :],
                                         start=True, stop=True)
                last.then_inc(near_psum, 1)

            def transpose_x2(b, k):
                pe.wait_ge(x2_ready, b + 1)
                if b == B - 1:
                    pe.wait_ge(far_ready, NT)
                elif k >= 1:
                    pe.wait_ge(x2T_ready, KH * b + k)
                elif b >= 1:
                    pe.wait_ge(slots_read, b)
                for c in range(NC):
                    last = pe.transpose(x2T_bank(b, k)[:, c * P:(c + 1) * P], normed[:, b % 2, c, k * P:(k + 1) * P],
                                        ident[:, :])
                last.then_inc(x2T_psum, 1)

            def route(b):
                pe.wait_ge(x2T_ready, KH * (b + 1))
                for c in range(NC):
                    s = slice((b * NC + c) * P, (b * NC + c + 1) * P)
                    for k in range(KH):
                        last = pe.matmul(route_bank(b)[:, c, :], x2T[:, k, s], w_route[:, k, :],
                                         start=(k == 0), stop=(k == KH - 1))
                last.then_inc(route_psum, 1)

            def count(b):
                pe.wait_ge(valid_ready, b + 1)
                pe.wait_ge(route_read, b + 1)
                if b >= 1:
                    pe.wait_ge(slots_read, b)
                pe.matmul(csum_ps, ones_b[:, :], bc(carry_b[:, :], 1, NC), start=True, stop=False)
                for k in range(1, NC):
                    pe.matmul(csum_ps[:, k:NC, :], ones_b[:, :], valid_b[:, 0:NC - k, :], start=False, stop=False)
                pe.matmul(csum_ps, tri_b[:, :], valid_b[:, :, :], start=False, stop=True).then_inc(csum_psum, 1)

            def list_slots(b):
                pe.wait_ge(onehot_ready, sum(DVE_HOT[:b + 1]))
                pe.wait_ge(onehot_pool, NC * (b + 1) - sum(DVE_HOT[:b + 1]))
                pe.wait_ge(val_ready, EJ * (b + 1))
                pe.wait_ge(csum_read, b + 1)
                for e in range(E):
                    for c in range(NC):
                        m = c * E + e
                        last = pe.matmul(slots_ps[:, e * EJ * NV:(e + 1) * EJ * NV], onehot[:, m, :],
                                         val_j[:, m, :, :].rearrange("p j v -> p (j v)"),
                                         start=(c == 0), stop=(c == NC - 1))
                last.then_inc(slots_psum, 1)

            def gate_up(b, i):
                m = NG * b + i
                s = slice(b * SEQ + (i // IC) * HS, b * SEQ + (i // IC + 1) * HS)
                w_i = slice((i % IC) * P, (i % IC + 1) * P)
                pe.wait_ge(x2T_ready, KH * (b + 1))
                if m == 0:
                    pe.wait_ge(w_sh_in, 32)
                if m >= 2:
                    pe.wait_ge(gated_ready, m - 1)
                for w in range(2):
                    for k in range(KH):
                        last = pe.matmul(gu_ps[m % 2][:, w * HS:(w + 1) * HS], wgu_sh[:, w, k, w_i],
                                         x2T[:, k, s], start=(k == 0), stop=(k == KH - 1))
                last.then_inc(gu_psum, 1)

            def down(b, c):
                pe.wait_ge(act_ready, NG * b + IC * (c // (NC // 2) + 1))
                n = b * NC + c
                if b == B - 1 and c == 1:
                    pe.wait_ge(heads_ready, NT)
                elif b == B - 1 and c > 1:
                    pe.wait_ge(o_ready, n - 1)
                elif n >= 1:
                    pe.wait_ge(o_ready, n)
                for i in range(IC):
                    last = pe.matmul(down_bank(b, c)[:, 0:HD], act_sh[:, b % 2, i, c * P:(c + 1) * P], wd_sh[:, i, :],
                                     start=(i == 0), stop=(i == IC - 1))
                last.then_inc(y_psum, 1)

            for t in range(LAST):
                if t == LISTS[B - 1] + 1:
                    pe.wait_ge(ids_ready, 1)
                    pe.matmul(t_ps[EROWS[2]:P, 0:E // 2], ident[:, 0:EROWS[2]], slot_id[:, 2 * EJ - 1:E * EJ:2 * EJ],
                              start=True, stop=True).then_inc(shifted_psum, 1)
                n = t // 2
                if t % 2 == 0 and n < NT:
                    scores(n)
                if t % 2 == 1 and n <= NT:
                    near(n - 1)
                for u in at(t, gate_up_at, NG):
                    gate_up(*u)
                for u in at(t, down_at, NC):
                    down(*u)
                for b, _ in due(t, COUNT):
                    count(b)
                for b, _ in due(t, LISTS):
                    list_slots(b)
                for u in due(t, X2T, KH):
                    transpose_x2(*u)
                for b, _ in due(t, ROUTE):
                    route(b)

            def spread(e):
                tiles = [j for g, j in gathers if g == e]
                pe.wait_ge(gathered[e], 16 * len(tiles))
                if e >= 1:
                    pe.wait_ge(xgT_ready, e)
                for k, dst in ((0, s0_ps), (1, d_ps)):
                    for t in tiles:
                        last = pe.transpose(dst[:, t * P:(t + 1) * P], rows[e][:, t, k * P:(k + 1) * P], ident[:, :])
                last.then_inc(xgT_psum, 1)

            def expert_gate_up(e):
                pe.wait_ge(xgT_ready, e + 1)
                if e >= 1:
                    pe.wait_ge(dact_ready, e)
                for w, dst, signal in ((0, g_ps, dg_psum), (1, u_ps, du_psum)):
                    for k in range(KH):
                        last = pe.matmul(dst[:, 0:CAP], wgu_dyn[:, w, e, k, :],
                                         xgT[e // 2 % 2][:, k, e % 2 * CAP:(e % 2 + 1) * CAP],
                                         start=(k == 0), stop=(k == KH - 1))
                    last.then_inc(signal, 1)

            def expert_down(e):
                pe.wait_ge(dact_ready, e + 1)
                if e == 0:
                    pe.wait_ge(o_ready, NT)
                    pe.wait_ge(pairs_ready, 2)
                if e >= 1:
                    pe.wait_ge(ys_ready, e)
                for t in range(EJ):
                    m = EROWS[t]
                    dst = y_ps[:, t * HD:(t + 1) * HD] if t < 2 else t_ps[0:m, 0:HD]
                    last = pe.matmul(dst, act_d[:, e % 2, slot_columns(e, t)], wd_dyn[:, e, :], start=True, stop=True)
                last.then_inc(dy_psum, 1)

            pe.wait_ge(w_dyn_in, 32)
            pe.wait_ge(gated_ready, NG * B)
            pe.wait_ge(slots_read, B)
            spread(0)
            for e in range(E):
                expert_gate_up(e)
                if e + 1 < E:
                    spread(e + 1)
                expert_down(e)

        @block.vector
        def _(dve):
            done = [0]

            def step(ins):
                done[0] += 1
                ins.then_inc(dve_step, 1)
                dve.wait_ge(dve_step, done[0])

            def count(ins):
                done[0] += 1
                ins.then_inc(dve_step, 1)
                return done[0]

            stats_done = [0]

            def variance(m, width, eps, mean=mean):
                dve.tensor_tensor(st_s[:, 0:m], st[:, 0:m, 1], st[:, 0:m, 4], ALU.add)
                dve.tensor_tensor(st_v[:, 0:m], st[:, 0:m, 2], st[:, 0:m, 5], ALU.add)
                step(dve.tensor_tensor(st_d[:, 0:m], st[:, 0:m, 1], st[:, 0:m, 4], ALU.subtract))
                dve.tensor_scalar(mean[:, 0:m], st_s[:, 0:m], 0.5, None, ALU.mult)
                dve.tensor_scalar(st_v[:, 0:m], st_v[:, 0:m], 1.0 / width, eps, ALU.mult, ALU.add)
                step(dve.scalar_tensor_tensor(out=st_d2[:, 0:m], in0=st_d[:, 0:m], scalar=0.25, in1=st_d[:, 0:m],
                                              op0=ALU.mult, op1=ALU.mult))

            dve.memset(v_aug[:, :, :, DH:DA].rearrange("p n h d -> p (n h d)"), 1.0).then_inc(ones_ready, 1)
            dve.memset(state[:, :, :, :].rearrange("p r i d -> p (r i d)"), 0.0).then_inc(ones_ready, 1)
            dve.memset(ones_row[:, :], 1.0)
            dve.memset(dec_sel[:, :, :, :].rearrange("p b a c -> p (b a c)"), 0.0)

            def gate_weights():
                dve.wait_ge(small_in, 16 * 5)
                for m in range(KH):
                    for q in range(2):
                        wq, wk, wv = (bc(w_gates[:, m + KH * i, q * NH:(q + 1) * NH], 1, 8) for i in range(3))
                        dve.tensor_copy(w_rows[:, m, q, :, :], wq)
                        last = dve.tensor_tensor(w_rows[:, KH + m, q, :, :], wk, wv, ALU.add)
                last.then_inc(gate_w_ready, 1)

            def row_masks():
                dve.wait_ge(consts_ready, 1)
                dve.tensor_reduce(head_of[:, :], row_of[:, :, :], AX.X, ALU.add)
                dve.tensor_reduce(pair_row[:, :, :].rearrange("p b a -> p (b a)"),
                                  row_of[:, :, :].rearrange("p (a r) (b j) -> p b j a r", a=2, j=8)[:, :, 0, :, :],
                                  AX.X, ALU.add)
                step(dve.tensor_reduce(rep_of[:, :], row_of[:, :, :].rearrange("p h (b j) -> p j b h", j=8), AX.XY, ALU.add))
                dve.tensor_tensor(is_a[:, :], rep_of[:, 0:1], rep_of[:, 1:2], ALU.add)
                dve.tensor_tensor(is_m[:, :], rep_of[:, 2:3], rep_of[:, 3:4], ALU.add)
                dve.tensor_tensor(is_hi[:, :], rep_of[:, 0:1], rep_of[:, 2:3], ALU.add)
                dve.tensor_tensor(is_lo[:, :], rep_of[:, 1:2], rep_of[:, 3:4], ALU.add)
                step(dve.tensor_tensor(parity[:, :], head_of[:, 0:2], head_of[:, 2:4], ALU.add))
                for a in range(2):
                    dve.tensor_copy(par_sel[:, a * DH:(a + 1) * DH], parity[:, a:a + 1].to_broadcast([P, DH]))
                dve.tensor_tensor(hi_less_lo[:, :], is_hi[:, :], is_lo[:, :], ALU.subtract)
                dve.tensor_tensor(m_head[:, :], head_of[:, :], is_m[:, :].to_broadcast([P, NH]), ALU.mult)
                dve.tensor_tensor(a_head[:, :], head_of[:, :], is_a[:, :].to_broadcast([P, NH]), ALU.mult).then_inc(
                    row_masks_ready, 1)

            for i in range(B + 2):
                if i < B:
                    dve.wait_ge(x_in[i], 16)
                    for c in range(NC):
                        last = dve.bn_stats(st[:, c, :], xs[:, i * NC + c, :])
                    step(last)
                    cols = slice(i * NC, (i + 1) * NC)
                    variance(NC, HD, 1e-5, mean[:, cols])
                    dve.tensor_tensor(var_eps[:, cols], st_v[:, 0:NC], st_d2[:, 0:NC], ALU.add).then_inc(var1_ready, 1)
                if i == 2:
                    row_masks()
                if i >= 3:
                    b = i - 3
                    dve.wait_ge(qT_psum, KH * b + 2)
                    dve.tensor_copy(qT[:, 1, b * SEQ:(b + 1) * SEQ], qt_ps[b % 2][1][:, :]).then_inc(qT_dve, 1)
                if i < B:
                    dve.wait_ge(rstd1_ready, i + 1)
                    dve.tensor_copy(hscale[:, cols], rstd[:, cols])
                    dve.scalar_tensor_tensor(out=hshift[:, cols], in0=mean[:, cols], scalar=-1.0, in1=rstd[:, cols],
                                             op0=ALU.mult, op1=ALU.mult).then_inc(scale1_ready, 1)
                if i == 1:
                    gate_weights()
            dve.wait_ge(qT_psum, KH * B)
            dve.tensor_copy(qT[:, 1, (B - 1) * SEQ:B * SEQ], qt_ps[(B - 1) % 2][1][:, :]).then_inc(qT_dve, 1)
            for b in range(B):
                dve.wait_ge(gates_psum, b + 1)
                dve.tensor_copy(gi_row[32 * b:32 * b + 32, :], gate_ps[b][0:32, :]).then_inc(gi_ready, 1)
            dve.wait_ge(gi_ready, B)
            dve.wait_ge(gf_ready, B)
            step(dve.tensor_scalar(fmin[:, :], gf_row[:, :], b_rows[:, 1:2], 0.0, ALU.add, ALU.min))
            dve.wait_ge(softplus_ready, 1)
            step(dve.tensor_tensor(fmin[:, :], fmin[:, :], fabs[:, :], ALU.subtract))
            step(dve.tensor_tensor_scan(cs[:, :], ones_row[:, :], fmin[:, :], 0.0, ALU.mult, ALU.add))
            step(dve.scalar_tensor_tensor(out=a_row[:, :], in0=gi_row[:, :], scalar=b_rows[:, 0:1], in1=cs[:, :],
                                          op0=ALU.add, op1=ALU.subtract))
            step(dve.tensor_tensor_scan(m_row[:, :], ones_row[:, :], a_row[:, :], -3.0e38, ALU.mult, ALU.max))
            dve.tensor_tensor(dec_row[:, 1:NC], m_row[:, P - 1:(NC - 1) * P:P], m_row[:, 2 * P - 1:NC * P:P],
                              ALU.subtract)
            dve.tensor_tensor(mld[:, :], cs[:, :], m_row[:, :], ALU.add)
            dve.tensor_scalar(negm[:, :], m_row[:, :], -1.0, None, ALU.mult).then_inc(mrow_ready, 1)
            dve.wait_ge(mrow_ready, 1)
            step(dve.tensor_scalar(av[:, :], a_row[:, :], is_a[:, :], None, ALU.mult))
            step(dve.scalar_tensor_tensor(out=av[:, :], in0=negm[:, :], scalar=is_m[:, :], in1=av[:, :],
                                          op0=ALU.mult, op1=ALU.add))
            dve.tensor_copy(av_hi[:, :], av[:, :])
            step(dve.tensor_scalar(av_lo[:, :], av[:, :], is_lo[:, :], None, ALU.mult))
            dve.scalar_tensor_tensor(out=parts[:, :], in0=av_hi[:, :].bitcast(fp32), scalar=hi_less_lo[:, :],
                                     in1=av_lo[:, :], op0=ALU.mult, op1=ALU.add).then_inc(parts_ready, 1)
            dve.wait_ge(exps_ready, 3)
            dve.tensor_tensor(dec_sel[:, :, :, 1:NC].rearrange("p b a c -> p (b a) c"),
                              bc(pair_row[:, :, :].rearrange("p b a -> p (b a)"), 2, NC - 1),
                              bc(dec_row[:, 1:NC], 1, 2 * B), ALU.mult).then_inc(decsel_ready, 1)
            dve.wait_ge(parts_ready, 1)
            for h in range(1, NH):
                last = dve.tensor_scalar(dr[:, :, order(h), :], parts[:, :].rearrange("p (c s) -> p c s", c=NC),
                                         m_head[:, h:h + 1], a_head[:, h:h + 1], ALU.mult, ALU.add)
            last.then_inc(drows_ready, 1)
            dve.wait_ge(tanh_ready, 1)
            dve.tensor_scalar(half_gf[:, :], tanh_g[:, 1:2], 0.5, None, ALU.mult)
            step(dve.tensor_scalar(out_scale[:, :], out_scale[:, :], tanh_g[:, 0:1], None, ALU.mult))

            def decay_scores(n):
                b, c = divmod(n, NC)
                dve.wait_ge(scores_psum, n + 1)
                dve.wait_ge(dexp_ready, n + 1)
                if n >= 2:
                    dve.wait_ge(near_psum, n)
                for a in range(2):
                    m = slice(a * 2 * P, (a + 1) * 2 * P)
                    last = dve.scalar_tensor_tensor(out=cmat[:, n % 2, m], in0=qk_ps[a], scalar=QSCALE,
                                                    in1=dexp[:, n % 2, m], op0=ALU.mult, op1=ALU.mult)
                last.then_inc(c_ready, 1)
                if c > 0:
                    for i in range(2):
                        last = dve.tensor_tensor(far[:, n % 2, 2 * i:2 * i + 2, :],
                                                 far_ps[i].rearrange("p (h d) -> p h d", h=2),
                                                 bc(w_t[:, c, b, 2 * i:2 * i + 2], 2, DA), ALU.mult)
                    last.then_inc(far_ready, 1)
                else:
                    dve.memset(far[:, n % 2, :, :], 0.0).then_inc(far_ready, 1)

            def new_state(n):
                b, c = divmod(n, NC)
                dve.wait_ge(near_psum, n + 1)
                if n == 0:
                    dve.wait_ge(spare_zero, 16 * EJ)
                if n >= 2:
                    dve.wait_ge(scores_psum, n)
                if c == 0 or c == NC - 1:
                    for a in range(2):
                        g, d = slice(DH * a, DH * a + DH), slice(DA * a, DA * a + DA)
                        last = dve.tensor_copy(state[g, n % 2, :, d], kv_ps[g, :, :])
                    last.then_inc(state_ready, 1)
                else:
                    dve.wait_ge(state_ready, n)
                    for i in range(2):
                        for a in range(2):
                            g, d = slice(DH * a, DH * a + DH), slice(DA * a, DA * a + DA)
                            last = dve.scalar_tensor_tensor(
                                out=state[g, n % 2, i, d], in0=state[g, (n - 1) % 2, i, d],
                                scalar=dec_t[g, b, i, c:c + 1], in1=kv_ps[g, i, :], op0=ALU.mult, op1=ALU.add)
                    last.then_inc(state_ready, 1)

            def join(n):
                b, c = divmod(n, NC)
                dve.wait_ge(near_psum, n + 2)
                dve.wait_ge(far_ready, n + 1)
                if b >= 2 and c == 0:
                    dve.wait_ge(x1_ready, 2 * (b - 1))
                dve.scalar_tensor_tensor(
                    out=heads[:, b % 2, c, :, :].rearrange("p h d -> p (h d)"),
                    in0=far[:, n % 2, :, :].rearrange("p h d -> p (h d)"), scalar=QSCALE,
                    in1=h_ps[:, 0:NH * DA], op0=ALU.mult, op1=ALU.add).then_inc(heads_ready, 1)
                dve.wait_ge(heads_ready, n + 1)
                for h in range(NH):
                    last = dve.bn_stats(st_h[:, c * NH + h, :], heads[:, b % 2, c, h, 0:DH])
                stats_done[0] = count(last)

            def head_stats(p, b, c0, c1):
                g = slice(c0 * NH, c1 * NH)
                hb = heads[:, b % 2, :, :, :].rearrange("p c h d -> p (c h) d")[:, g, :]
                ch = "p (c h) -> p c h"
                a_sum = count(dve.scalar_tensor_tensor(out=den[:, g], in0=hb[:, :, DH], scalar=-1.0, in1=hb[:, :, DH],
                                                       op0=ALU.mult, op1=ALU.max))
                dve.wait_ge(dve_step, stats_done[0])
                sums = count(dve.tensor_tensor(st_s[:, g], st_h[:, g, 1], st_h[:, g, 4], ALU.add))
                dve.wait_ge(dve_step, a_sum)
                a_max = count(dve.tensor_tensor(den[:, g].rearrange(ch, h=NH), den[:, g].rearrange(ch, h=NH),
                                                n_t[:, c0:c1, b, :], ALU.max))
                difs = count(dve.tensor_tensor(st_d[:, g], st_h[:, g, 1], st_h[:, g, 4], ALU.subtract))
                m2 = count(dve.tensor_tensor(st_v[:, g], st_h[:, g, 2], st_h[:, g, 5], ALU.add))
                dve.wait_ge(dve_step, a_max)
                a_eps = count(dve.tensor_scalar(den[:, g], den[:, g], 1e-6, None, ALU.add))
                dve.wait_ge(dve_step, difs)
                d2 = count(dve.scalar_tensor_tensor(out=st_d2[:, g], in0=st_d[:, g], scalar=0.25, in1=st_d[:, g],
                                                    op0=ALU.mult, op1=ALU.mult))
                dve.tensor_scalar(mean[:, g], st_s[:, g], 0.5, None, ALU.mult)
                dve.wait_ge(dve_step, a_eps)
                a_rec = count(dve.reciprocal(rden[:, g], den[:, g]))
                dve.wait_ge(dve_step, d2)
                var = count(dve.scalar_tensor_tensor(out=st_v[:, g], in0=st_v[:, g], scalar=1.0 / DH, in1=st_d2[:, g],
                                                     op0=ALU.mult, op1=ALU.add))
                dve.wait_ge(dve_step, a_rec)
                step(dve.tensor_tensor(rden2[:, g], rden[:, g], rden[:, g], ALU.mult))
                step(dve.tensor_tensor(st_v[:, g], st_v[:, g], rden2[:, g], ALU.mult))
                dve.tensor_scalar(var_eps[:, g], st_v[:, g], 1e-6, None, ALU.add).then_inc(hvar_ready, 1)

            def head_norm(p, b, c0, c1):
                g = slice(c0 * NH, c1 * NH)
                dve.wait_ge(hrstd_ready, p + 1)
                if b >= 1:
                    dve.wait_ge(z_ready, 2 * b)
                step(dve.tensor_tensor(hscale[:, g], rstd[:, g], rden[:, g], ALU.mult))
                shift = dve.scalar_tensor_tensor(out=hshift[:, g], in0=mean[:, g], scalar=-1.0, in1=hscale[:, g],
                                                 op0=ALU.mult, op1=ALU.mult)
                if p < B:
                    shift.then_inc(hscale_ready, 1)
                    return
                step(shift)
                hb = heads[:, b % 2, :, :, :].rearrange("p c h d -> p (c h) d")
                for i in range(c0 * NH, c1 * NH):
                    last = dve.tensor_scalar(hb[:, i, 0:DH], hb[:, i, 0:DH], hscale[:, i:i + 1], hshift[:, i:i + 1],
                                             ALU.mult, ALU.add)
                step(last)
                z = heads[:, b % 2, c0:c1, :, 0:DH]
                xb = xs[:, b * NC + c0:b * NC + c1, :].rearrange("p c (h d) -> p c h d", h=NH)
                step(dve.tensor_tensor(z, z, bc(out_scale[:, :].rearrange("p (h d) -> p h d", h=NH), 1, c1 - c0),
                                       ALU.mult))
                dve.tensor_tensor(xb, z, xb, ALU.add).then_inc(x1_ready, 1)

            def norm2_stats(b):
                dve.wait_ge(x1_ready, 2 * (b + 1))
                for c in range(NC):
                    last = dve.bn_stats(st[:, c, :], xs[:, b * NC + c, :])
                step(last)
                variance(NC, HD, 1e-5, mean2)
                dve.tensor_tensor(var2[:, :], st_v[:, 0:NC], st_d2[:, 0:NC], ALU.add).then_inc(var2_ready, 1)

            def norm2(b):
                dve.wait_ge(rstd2_ready, b + 1)
                if b == B - 1:
                    dve.wait_ge(x2_stored[b - 2], 16)
                    dve.wait_ge(x2T_psum, KH * (b - 1))
                    for c in range(NC):
                        last = dve.tensor_scalar(normed[:, b % 2, c, :], xs[:, b * NC + c, :], mean2[:, c:c + 1],
                                                 rstd2[:, c:c + 1], ALU.subtract, ALU.mult)
                    last.then_inc(x2_ready, 1)
                    return
                if b >= 1:
                    dve.wait_ge(x2_ready, b)
                dve.tensor_copy(scale2[:, :], rstd2[:, :])
                dve.scalar_tensor_tensor(out=shift2[:, :], in0=mean2[:, :], scalar=-1.0, in1=rstd2[:, :],
                                         op0=ALU.mult, op1=ALU.mult).then_inc(scale2_ready, 1)

            def choose(b):
                lg = logit[:, b % 2, :, 0:E]
                pq = "p (c i) j -> p c i j"
                dve.wait_ge(route_read, b + 1)
                maxed = count(dve.tensor_reduce(lmax[:, :], lg, AX.X, ALU.max))
                absed = count(dve.scalar_tensor_tensor(out=labs[:, :, :], in0=lg, scalar=-1.0, in1=lg, op0=ALU.mult,
                                                       op1=ALU.max))
                li, lj = bc(lg, 3, E), bc(lg, 2, E)
                pd4, pm4 = (t[:, :, :].rearrange(pq, c=NC) for t in (pd, pm))
                diffs = count(dve.tensor_tensor(pd4, lj, li, ALU.subtract))
                dve.wait_ge(dve_step, maxed)
                dve.tensor_tensor(lsh[:, :, :], lg, bc(lmax[:, :], 2, E), ALU.subtract).then_inc(lsh_ready, 1)
                dve.wait_ge(dve_step, absed)
                amax = count(dve.tensor_tensor(pm4, bc(labs[:, :, :], 2, E), bc(labs[:, :, :], 3, E), ALU.max))
                flat = "p m j -> p (m j)"
                tri = bc(tri_e[:, :, :].rearrange("p i j -> p (i j)"), 1, NC)
                f4 = "p (c i) j -> p c (i j)"
                dve.wait_ge(dve_step, diffs)
                ties = count(dve.scalar_tensor_tensor(out=pe_[:, :, :].rearrange(f4, c=NC),
                                                      in0=pd[:, :, :].rearrange(f4, c=NC), scalar=0.0, in1=tri,
                                                      op0=ALU.is_equal, op1=ALU.mult))
                dve.wait_ge(dve_step, amax)
                close = count(dve.scalar_tensor_tensor(out=pm[:, :, :].rearrange(flat), in0=pm[:, :, :].rearrange(flat),
                                                       scalar=0.2, in1=pd[:, :, :].rearrange(flat),
                                                       op0=ALU.mult, op1=ALU.add))
                dve.wait_ge(dve_step, ties)
                ahead = count(dve.scalar_tensor_tensor(out=pb[:, :, :].rearrange(flat), in0=pd[:, :, :].rearrange(flat),
                                                       scalar=0.0, in1=pe_[:, :, :].rearrange(flat),
                                                       op0=ALU.is_gt, op1=ALU.add))
                dve.wait_ge(dve_step, ahead)
                step(dve.scalar_tensor_tensor(out=pm[:, :, :].rearrange(flat), in0=pm[:, :, :].rearrange(flat), scalar=0.0,
                                              in1=pb[:, :, :].rearrange(flat), op0=ALU.is_ge, op1=ALU.is_gt))
                dve.tensor_reduce(rank[:, :, :].rearrange("p c e -> p (c e)"), pb[:, :, :], AX.X, ALU.add)

            def pick(b):
                ce = "p c e -> p (c e)"
                pc4, pb4, pm4 = (t[:, :, :].rearrange("p (c i) j -> p c i j", c=NC) for t in (pc, pb, pm))
                dve.wait_ge(ex_ready, b + 1)
                ej = bc(ex[:, :, :], 2, E)
                total = count(dve.tensor_reduce(tot75[:, :], ex[:, :, :], AX.X, ALU.add))
                mass = count(dve.tensor_tensor(pc4, pb4, ej, ALU.mult))
                dve.wait_ge(dve_step, total)
                total = count(dve.tensor_scalar(tot75[:, :], tot75[:, :], 0.75, None, ALU.mult))
                peers = count(dve.tensor_tensor(pm4, pm4, ej, ALU.mult))
                dve.wait_ge(dve_step, mass)
                mass = count(dve.tensor_reduce(before[:, :, :].rearrange(ce), pc[:, :, :], AX.X, ALU.add))
                dve.wait_ge(dve_step, peers)
                dens = count(dve.tensor_reduce(mden[:, :, :].rearrange(ce), pm[:, :, :], AX.X, ALU.add))
                dve.wait_ge(dve_step, mass)
                less = count(dve.tensor_tensor(before[:, :, :], before[:, :, :], bc(tot75[:, :], 2, E), ALU.is_lt))
                dve.wait_ge(dve_step, dens)
                dens = count(dve.tensor_scalar(mden[:, :, :], mden[:, :, :], 1e-30, None, ALU.max))
                dve.wait_ge(dve_step, less)
                chosen = count(dve.scalar_tensor_tensor(out=valid[:, :, :].rearrange(ce),
                                                        in0=rank[:, :, :].rearrange(ce), scalar=4.0,
                                                        in1=before[:, :, :].rearrange(ce),
                                                        op0=ALU.is_lt, op1=ALU.mult))
                dve.wait_ge(dve_step, dens)
                if b >= 1:
                    step(dve.tensor_tensor(carry[:, :], carry[:, :], msum[:, :], ALU.add))
                    dve.wait_ge(csum_psum, b)
                    dve.tensor_copy(carry_b[:, :], carry[:, :])
                dve.wait_ge(dve_step, chosen)
                dve.tensor_copy(valid_b[:, :, :], valid[:, :, :]).then_inc(valid_ready, 1)

            def share(b):
                step(dve.reciprocal(mden[:, :, :], mden[:, :, :]))
                step(dve.tensor_tensor(rw[:, :, :], ex[:, :, :], mden[:, :, :], ALU.mult))
                masked = count(dve.tensor_tensor(rw[:, :, :], rw[:, :, :], valid[:, :, :], ALU.mult))
                dve.tensor_reduce(msum[:, :], valid[:, :, :].rearrange("p c e -> p e c"), AX.X, ALU.add)
                dve.wait_ge(dve_step, masked)
                step(dve.tensor_reduce(rsum[:, :], rw[:, :, :], AX.X, ALU.add))
                step(dve.reciprocal(rsum[:, :], rsum[:, :]))
                step(dve.tensor_tensor(rw[:, :, :], rw[:, :, :], bc(rsum[:, :], 2, E), ALU.mult))

            def capacity(b):
                dve.wait_ge(csum_psum, b + 1)
                dve.tensor_copy(pos[:, :, :], csum_ps).then_inc(csum_read, 1)
                dve.wait_ge(csum_read, b + 1)
                if b >= 1:
                    dve.wait_ge(onehot_pool, NC * b - sum(DVE_HOT[:b]))
                pf = pos[:, :, :].rearrange("p c e -> p (c e)")
                within = count(dve.tensor_scalar(l9[:, :, 0:E], pos[:, :, :], float(CAP), None, ALU.is_le))
                second = count(dve.tensor_scalar(tile_j[:, :], pf, float(P), None, ALU.is_gt))
                dve.wait_ge(dve_step, within)
                kept = count(dve.tensor_tensor(keep9[:, :, 0:E], l9[:, :, 0:E], valid[:, :, :], ALU.mult))
                dve.wait_ge(dve_step, second)
                third = count(dve.scalar_tensor_tensor(out=tile_j[:, :], in0=pf, scalar=float(2 * P), in1=tile_j[:, :],
                                                       op0=ALU.is_gt, op1=ALU.add))
                dve.wait_ge(dve_step, kept)
                floor = count(dve.tensor_scalar(l9[:, :, :], keep9[:, :, :], -NEG, NEG, ALU.mult, ALU.add))
                dve.wait_ge(dve_step, third)
                place = count(dve.scalar_tensor_tensor(out=pk[:, :], in0=tile_j[:, :], scalar=-float(P), in1=pf,
                                                       op0=ALU.mult, op1=ALU.add))
                dve.wait_ge(dve_step, floor)
                masked = count(dve.tensor_tensor(l9[:, :, :], l9[:, :, :], logit[:, b % 2, :, :], ALU.add))
                dve.wait_ge(dve_step, place)
                dve.tensor_tensor(pk[:, :].rearrange("p (c e) -> p c e", c=NC), pk[:, :].rearrange("p (c e) -> p c e", c=NC),
                                  keep9[:, :, 0:E], ALU.mult).then_inc(pk_ready, 1)
                dve.wait_ge(dve_step, masked)
                step(dve.tensor_reduce(lmax[:, :], l9[:, :, :], AX.X, ALU.max))
                dve.tensor_tensor(t9[:, :, :], l9[:, :, :], bc(lmax[:, :], 2, E + 1), ALU.subtract).then_inc(t9_ready, 1)

            def weights(b):
                kf = keep9[:, :, 0:E]
                dve.wait_ge(e9_ready, b + 1)
                step(dve.tensor_reduce(rsum[:, :], e9[:, :, :], AX.X, ALU.add))
                inverse = count(dve.reciprocal(rsum[:, :], rsum[:, :]))
                routed = count(dve.tensor_reduce(sdyn[:, :], e9[:, :, 0:E], AX.X, ALU.add))
                dve.wait_ge(dve_step, inverse)
                scale = count(dve.tensor_scalar(rsum[:, :], rsum[:, :], half_gf[:, :], None, ALU.mult))
                kept = count(dve.tensor_tensor(rw[:, :, :], rw[:, :, :], kf, ALU.mult))
                dve.wait_ge(dve_step, scale)
                step(dve.tensor_tensor(sdyn[:, :], sdyn[:, :], rsum[:, :], ALU.mult))
                step(dve.tensor_tensor(rw[:, :, :], rw[:, :, :], bc(sdyn[:, :], 2, E), ALU.mult))
                rf = rw[:, :, :].rearrange("p c e -> p (c e)")
                vb = val[:, b * NC * E:(b + 1) * NC * E, :]
                if b >= 1:
                    dve.wait_ge(slots_psum, b)
                step(dve.tensor_copy(vb[:, :, 2], rf))
                step(dve.tensor_tensor(res[:, :], rf, vb[:, :, 2], ALU.subtract))
                part = count(dve.tensor_copy(vb[:, :, 3], res[:, :]))
                dve.tensor_tensor(w_shared[:, b * NC:(b + 1) * NC], e9[:, :, E], rsum[:, :], ALU.mult)
                dve.wait_ge(dve_step, part)
                step(dve.tensor_tensor(res[:, :], res[:, :], vb[:, :, 3], ALU.subtract))
                step(dve.tensor_copy(vb[:, :, 4], res[:, :]))
                for j in range(EJ):
                    dve.scalar_tensor_tensor(out=val_j[:, :, j, :], in0=bc(tile_j[:, :], 2, NV), scalar=float(j),
                                             in1=vb, op0=ALU.is_equal,
                                             op1=ALU.mult).then_inc(val_ready, 1)

            def one_hots(b, c):
                m = slice(c * E, (c + 1) * E)
                dve.tensor_tensor(onehot[:, m, :], bc(iota1[:, :], 1, E), bc(pk[:, m], 2, P),
                                  ALU.is_equal).then_inc(onehot_ready, 1)

            def add_slots(b):
                dve.wait_ge(slots_psum, b + 1)
                sf = slots[:, :, :, :].rearrange("p e j v -> p (e j v)")
                dve.tensor_tensor(sf, sf, slots_ps, ALU.add).then_inc(slots_read, 1)
                dve.wait_ge(slots_read, b + 1)

            def gated(b, i):
                m = NG * b + i
                dve.wait_ge(sig_ready, m + 1)
                dve.scalar_tensor_tensor(out=sig[:, m % GR, 0, :], in0=sig[:, m % GR, 0, :], scalar=1.0,
                                         in1=gu_ps[m % 2][:, 0:HS], op0=ALU.add, op1=ALU.mult).then_inc(gated_ready, 1)

            def shared_out(b, c):
                n = b * NC + c
                dve.wait_ge(y_psum, n + 1)
                dve.scalar_tensor_tensor(out=xs[:, n, :], in0=down_bank(b, c)[:, 0:HD], scalar=w_shared[:, n:n + 1],
                                         in1=xs[:, n, :], op0=ALU.mult, op1=ALU.add).then_inc(o_ready, 1)

            for t in range(LAST):
                if t == LISTS[B - 1] + 1:
                    dve.wait_ge(shifted_psum, 1)
                    dve.tensor_scalar(pair_g[EROWS[2]:P, :], t_ps[EROWS[2]:P, 0:E // 2], float(T - 1), None,
                                      ALU.min).then_inc(pairs_ready, 1)
                n = t // 2
                if t % 2 == 0 and n < NT:
                    decay_scores(n)
                if t % 2 == 1 and n < NT:
                    new_state(n)
                if t % 2 == 1 and 1 <= n <= NT:
                    join(n - 1)
                for u in at(t, act_at, NG):
                    gated(*u)
                for u in at(t - 1, down_at, NC):
                    shared_out(*u)
                for p, part in enumerate(head_parts):
                    if HSTATS[p] == t:
                        head_stats(p, *part)
                for p, part in enumerate(head_parts):
                    if HNORM[p] == t:
                        head_norm(p, *part)
                for b, _ in due(t, STATS2):
                    norm2_stats(b)
                for b, _ in due(t, NORM2):
                    norm2(b)
                for b, _ in due(t, CHOOSE):
                    choose(b)
                for b, _ in due(t, PICK):
                    pick(b)
                for b, _ in due(t, SHARE):
                    share(b)
                for b, _ in due(t, CAPAC):
                    capacity(b)
                for b, _ in due(t, WEIGHTS):
                    weights(b)
                for b, _ in due(t, ONEHOT):
                    for c in range(DVE_HOT[b]):
                        one_hots(b, c)
                for b, _ in due(t, LISTS):
                    add_slots(b)
                if t == LISTS[B - 1]:
                    sl = slots[:, :, :, :].rearrange("p e j v -> p (e j) v")
                    dve.tensor_tensor(slot_w[:, :], sl[:, :, 3], sl[:, :, 4], ALU.add)
                    step(dve.tensor_tensor(slot_id[:, :], sl[:, :, 0], sl[:, :, 1], ALU.add))
                    dve.tensor_scalar(slot_id[:, :], slot_id[:, :], SHIFT, None, ALU.add).then_inc(ids_ready, 1)
                    dve.wait_ge(ids_ready, 1)
                    dve.tensor_scalar(slot_g[:, :], slot_id[:, :], float(T - 1), None, ALU.min).then_inc(slots_ready, 1)
                    step(dve.scalar_tensor_tensor(out=spare[:, :], in0=slot_id[:, :], scalar=SHIFT,
                                                  in1=spare_row[:, :], op0=ALU.is_ge, op1=ALU.mult))
                    dve.tensor_tensor(slot_w[:, :], slot_w[:, :], sl[:, :, 2], ALU.add)
                    dve.tensor_tensor(slot_s[:, :], slot_id[:, :], spare[:, :], ALU.add).then_inc(slots_ready, 1)
                    dve.tensor_scalar(pair_g[0:EROWS[2], :], slot_id[0:EROWS[2], EJ - 1:E * EJ:2 * EJ], float(T - 1),
                                      None, ALU.min).then_inc(pairs_ready, 1)

            for e in range(E):
                dve.wait_ge(dsig_ready, e + 1)
                step(dve.scalar_tensor_tensor(out=sig_d[:, e % 2, 0:CAP], in0=sig_d[:, e % 2, 0:CAP], scalar=1.0,
                                              in1=g_ps[:, 0:CAP], op0=ALU.add, op1=ALU.mult))
                dve.wait_ge(du_psum, e + 1)
                if e >= 2:
                    dve.wait_ge(dy_psum, e - 1)
                dve.tensor_tensor(act_d[:, e % 2, :], sig_d[:, e % 2, 0:CAP], u_ps[:, 0:CAP],
                                  ALU.mult).then_inc(dact_ready, 1)


def kernel(**inputs):
    import numpy as np
    import concourse.bacc as bacc
    from concourse.bass_utils import run_bass_kernel_spmd as run

    a = {k: np.asarray(v) for k, v in inputs.items()}
    P, KH = 128, 2

    def lay(t):
        return np.ascontiguousarray(t)

    x = a["x"].reshape(16, P, 256).transpose(1, 0, 2)
    ctx = a["ctx_1024"].reshape(16, P, 256).transpose(1, 0, 2)
    sh = np.stack([a["L0_ffn_sh_gate_w"][0], a["L0_ffn_sh_up_w"][0]])
    dyn = np.stack([a["L0_ffn_dyn_gate_w"], a["L0_ffn_dyn_up_w"]])
    gates = np.concatenate([a["L0_xattn_igate_kernel"], a["L0_xattn_fgate_kernel"]], axis=1)
    laid = {
        "x": lay(x),
        "ctx": lay(ctx),
        "ctxT": lay(a["ctx_1024"].reshape(2048, 256).T),
        "wgu_sh": lay(sh.reshape(2, 512, KH, P).transpose(3, 0, 2, 1)),
        "wd_sh": lay(a["L0_ffn_sh_down_w"][0].reshape(256, 4, P).transpose(2, 1, 0)),
        "wgu_dyn": lay(dyn.reshape(2, 8, P, KH, P).transpose(4, 0, 1, 3, 2)),
        "wd_dyn": lay(a["L0_ffn_dyn_down_w"].transpose(2, 0, 1)),
        "w_route": lay(a["L0_ffn_gate_w"].reshape(9, KH, P).transpose(2, 1, 0)),
        "w_gates": lay(gates.reshape(3 * KH, P, 8).transpose(1, 0, 2)),
        "b_rows": lay(np.tile(np.stack([a["L0_xattn_igate_bias"], a["L0_xattn_fgate_bias"]], axis=1), (32, 1))),
        "g_pair": lay(np.concatenate([a["g_xattn"], a["g_ffn"]])),
        "out_scale": lay(a["L0_xattn_outnorm_scale"]),
    }
    nc = bacc.Bacc("TRN2", target_bir_lowering=False, num_devices=1)
    fp32 = mybir.dt.float32
    aps = {k: nc.dram_tensor(f"in_{k}", v.shape, fp32, kind="ExternalInput").ap() for k, v in laid.items()}
    out = nc.dram_tensor("out_rows", (2048 + 3 * P, 256), fp32, kind="ExternalOutput").ap()
    gated_mlstm_moe_block(nc, aps, out)
    r = run(nc, [{f"in_{k}": v for k, v in laid.items()}], core_ids=[0])
    return r.results[0]["out_rows"][:2048].reshape(P, 16, 256).transpose(1, 0, 2).reshape(4, 512, 256)
```
